# Optimizing a Trainium2 kernel written in Bass

```python
import numpy as np
import jax
import jax.numpy as jnp

def _softmax(x, axis=-1):
    return jax.nn.softmax(x, axis=axis)

def _gelu(x):
    return jax.nn.gelu(x, approximate=True)

def _silu(x):
    return jax.nn.silu(x)

def _sigmoid(x):
    return jax.nn.sigmoid(x)

def _layernorm(x, axis=-1, eps=1e-05):
    m = jnp.mean(x, axis=axis, keepdims=True)
    v = jnp.var(x, axis=axis, keepdims=True)
    return (x - m) / jnp.sqrt(v + eps)

def _scatter_add(tgt, idx, src, axis=0):
    return tgt.at[idx].add(src)

def _segment_sum(src, seg, n):
    return jax.ops.segment_sum(src, seg, n)
kernel_name = 'mk_xattn_ffn_d2_seqx_r4_7306e7'

def setup_inputs(seed: int=0):
    np.random.seed(seed)
    _w = jnp.asarray

    def _rec_inputs():
        import jax
        import jax.numpy as jnp
        _rk = jax.random.key(seed)
        x = -0.0002928 + 1 * jax.random.normal(jax.random.fold_in(_rk, 1), (64, 128, 256), jnp.float32)
        _lenS = 128 - jax.random.randint(jax.random.fold_in(_rk, 7), (64,), 0, max(1, 128 // 4) + 1, jnp.int32)
        _lenS2 = 128 - jax.random.randint(jax.random.fold_in(_rk, 8), (64,), 0, max(1, 128 // 4) + 1, jnp.int32)
        _ctx_1024P = jax.random.normal(jax.random.fold_in(_rk, 11), (64, 16, 256), jnp.float32)
        _ctx_1024c = jax.random.dirichlet(jax.random.fold_in(_rk, 511), 0.3 * jnp.ones((16,), jnp.float32), (64, 128))
        _ctx_1024t = jnp.einsum('bsk,bkd->bsd', _ctx_1024c, _ctx_1024P)
        _ctx_1024t = _ctx_1024t * jax.lax.rsqrt(jnp.mean(jnp.square(_ctx_1024t)) + 1e-12) * 0.953939
        ctx_1024 = 4.13588e-05 + 0.999923 * (_ctx_1024t + 0.3 * jax.random.normal(jax.random.fold_in(_rk, 611), (64, 128, 256), jnp.float32))
        return (x, ctx_1024)
    x, ctx_1024 = _rec_inputs()

    def _L0_xattn_setup():
        import jax, jax.numpy as jnp
        import numpy as np
        EMBED_DIM = 256
        NUM_HEADS = 16
        HEAD_DIM = EMBED_DIM // NUM_HEADS
        key = jax.random.key(seed)
        ks = jax.random.split(key, 11)
        B, Q, K = (4, 256, 512)
        s = 1.0 / np.sqrt(EMBED_DIM)
        return {'query': jax.random.normal(ks[0], (B, Q, EMBED_DIM), jnp.float32), 'key': jax.random.normal(ks[1], (B, K, EMBED_DIM), jnp.float32), 'value': jax.random.normal(ks[2], (B, K, EMBED_DIM), jnp.float32), 'Wq': jax.random.normal(ks[3], (EMBED_DIM, EMBED_DIM), jnp.float32) * s, 'bq': jnp.zeros((EMBED_DIM,), jnp.float32), 'Wk': jax.random.normal(ks[4], (EMBED_DIM, EMBED_DIM), jnp.float32) * s, 'bk': jnp.zeros((EMBED_DIM,), jnp.float32), 'Wv': jax.random.normal(ks[5], (EMBED_DIM, EMBED_DIM), jnp.float32) * s, 'bv': jnp.zeros((EMBED_DIM,), jnp.float32), 'Wo': jax.random.normal(ks[6], (EMBED_DIM, EMBED_DIM), jnp.float32) * s, 'bo': jnp.zeros((EMBED_DIM,), jnp.float32)}
    _L0_xattn_all = _L0_xattn_setup()
    _L0_xattn_in = {k: v for k, v in _L0_xattn_all.items() if k in ('Wq', 'bq', 'Wk', 'bk', 'Wv', 'bv', 'Wo', 'bo')}
    del _L0_xattn_all

    def _L0_ffn_setup():
        import jax, jax.numpy as jnp
        import numpy as np
        TOP_K = 2

        def _gelu(x):
            return jax.nn.gelu(x, approximate=False)
        key = jax.random.key(seed)
        ks = jax.random.split(key, 6)
        B, S, D, F, E = (2, 512, 256, 512, 8)
        sc_g = 1.0 / np.sqrt(D)

        def xav(k, shape, fan_in, fan_out):
            lim = np.sqrt(6.0 / (fan_in + fan_out))
            return jax.random.uniform(k, shape, jnp.float32, -lim, lim)
        return {'x': jax.random.normal(ks[0], (B, S, D), jnp.float32), 'Wg': xav(ks[1], (D, E), D, E), 'Wu': xav(ks[2], (E, D, F), D, F), 'Wd': xav(ks[3], (E, F, D), F, D), 'W1': xav(ks[4], (D, F), D, F), 'W2': xav(ks[5], (F, D), F, D)}
    _L0_ffn_all = _L0_ffn_setup()
    _L0_ffn_in = {k: v for k, v in _L0_ffn_all.items() if k in ('Wg', 'Wu', 'Wd', 'W1', 'W2')}
    del _L0_ffn_all

    def _L1_xattn_setup():
        import jax, jax.numpy as jnp
        import numpy as np
        D_MODEL = 256
        NHEAD = 16
        WINDOW = 128
        key = jax.random.key(seed)
        ks = jax.random.split(key, 7)
        B, L, D = (4, 1024, D_MODEL)
        s = 0.02
        return {'q': jax.random.normal(ks[0], (B, L, D), jnp.float32), 'k': jax.random.normal(ks[1], (B, L, D), jnp.float32), 'v': jax.random.normal(ks[2], (B, L, D), jnp.float32), 'in_proj_w': jax.random.normal(ks[3], (3 * D, D), jnp.float32) * s, 'in_proj_b': jnp.zeros((3 * D,), jnp.float32), 'out_w': jax.random.normal(ks[4], (D, D), jnp.float32) * s, 'out_b': jnp.zeros((D,), jnp.float32)}
    _L1_xattn_all = _L1_xattn_setup()
    _L1_xattn_in = {k: v for k, v in _L1_xattn_all.items() if k in ('in_proj_w', 'in_proj_b', 'out_w', 'out_b')}
    del _L1_xattn_all

    def _L1_ffn_setup():
        import jax, jax.numpy as jnp
        import numpy as np
        B, S, D, H, M, E, K = (4, 256, 256, 16, 2, 8, 2)
        KD = D // H
        F = 2 * D
        EPS = 1e-06

        def _ln(x, g, b):
            m = jnp.mean(x, axis=-1, keepdims=True)
            v = jnp.mean(jnp.square(x - m), axis=-1, keepdims=True)
            return (x - m) * jax.lax.rsqrt(v + EPS) * g + b
        key = jax.random.key(seed)
        ks = jax.random.split(key, 12)
        r = lambda i, shape: jax.random.normal(ks[i], shape, jnp.float32) * 0.02
        return {'x': jax.random.normal(ks[0], (B, S, D), jnp.float32), 'ln1_g': jnp.ones((D,), jnp.float32), 'ln1_b': jnp.zeros((D,), jnp.float32), 'ln2_g': jnp.ones((D,), jnp.float32), 'ln2_b': jnp.zeros((D,), jnp.float32), 'mha_wq': r(1, (M, D, H, KD)), 'mha_bq': jnp.zeros((M, H, KD), jnp.float32), 'mha_wk': r(2, (M, D, H, KD)), 'mha_bk': jnp.zeros((M, H, KD), jnp.float32), 'mha_wv': r(3, (M, D, H, KD)), 'mha_bv': jnp.zeros((M, H, KD), jnp.float32), 'mha_wo': r(4, (M, H, KD, D)), 'mha_bo': jnp.zeros((M, D), jnp.float32), 'mha_rw': r(5, (D, M)), 'mha_rb': jnp.zeros((M,), jnp.float32), 'ffn_rw': r(6, (D, E)), 'ffn_rb': jnp.zeros((E,), jnp.float32), 'fw1': r(7, (E, D, F)), 'fw2': r(8, (E, F, D))}
    _L1_ffn_all = _L1_ffn_setup()
    _L1_ffn_in = {k: v for k, v in _L1_ffn_all.items() if k in ('ln1_g', 'ln1_b', 'ln2_g', 'ln2_b', 'mha_wq', 'mha_bq', 'mha_wk', 'mha_bk', 'mha_wv', 'mha_bv', 'mha_wo', 'mha_bo', 'mha_rw', 'mha_rb', 'ffn_rw', 'ffn_rb', 'fw1', 'fw2')}
    del _L1_ffn_all
    return {'x': x, 'ctx_1024': ctx_1024, 'L0_xattn_Wq': _L0_xattn_in['Wq'], 'L0_xattn_bq': _L0_xattn_in['bq'], 'L0_xattn_Wk': _L0_xattn_in['Wk'], 'L0_xattn_bk': _L0_xattn_in['bk'], 'L0_xattn_Wv': _L0_xattn_in['Wv'], 'L0_xattn_bv': _L0_xattn_in['bv'], 'L0_xattn_Wo': _L0_xattn_in['Wo'], 'L0_xattn_bo': _L0_xattn_in['bo'], 'L0_ffn_Wg': _L0_ffn_in['Wg'], 'L0_ffn_Wu': _L0_ffn_in['Wu'], 'L0_ffn_Wd': _L0_ffn_in['Wd'], 'L0_ffn_W1': _L0_ffn_in['W1'], 'L0_ffn_W2': _L0_ffn_in['W2'], 'L1_xattn_in_proj_w': _L1_xattn_in['in_proj_w'], 'L1_xattn_in_proj_b': _L1_xattn_in['in_proj_b'], 'L1_xattn_out_w': _L1_xattn_in['out_w'], 'L1_xattn_out_b': _L1_xattn_in['out_b'], 'L1_ffn_ln1_g': _L1_ffn_in['ln1_g'], 'L1_ffn_ln1_b': _L1_ffn_in['ln1_b'], 'L1_ffn_ln2_g': _L1_ffn_in['ln2_g'], 'L1_ffn_ln2_b': _L1_ffn_in['ln2_b'], 'L1_ffn_mha_wq': _L1_ffn_in['mha_wq'], 'L1_ffn_mha_bq': _L1_ffn_in['mha_bq'], 'L1_ffn_mha_wk': _L1_ffn_in['mha_wk'], 'L1_ffn_mha_bk': _L1_ffn_in['mha_bk'], 'L1_ffn_mha_wv': _L1_ffn_in['mha_wv'], 'L1_ffn_mha_bv': _L1_ffn_in['mha_bv'], 'L1_ffn_mha_wo': _L1_ffn_in['mha_wo'], 'L1_ffn_mha_bo': _L1_ffn_in['mha_bo'], 'L1_ffn_mha_rw': _L1_ffn_in['mha_rw'], 'L1_ffn_mha_rb': _L1_ffn_in['mha_rb'], 'L1_ffn_ffn_rw': _L1_ffn_in['ffn_rw'], 'L1_ffn_ffn_rb': _L1_ffn_in['ffn_rb'], 'L1_ffn_fw1': _L1_ffn_in['fw1'], 'L1_ffn_fw2': _L1_ffn_in['fw2']}

def reference(x, ctx_1024, L0_xattn_Wq, L0_xattn_bq, L0_xattn_Wk, L0_xattn_bk, L0_xattn_Wv, L0_xattn_bv, L0_xattn_Wo, L0_xattn_bo, L0_ffn_Wg, L0_ffn_Wu, L0_ffn_Wd, L0_ffn_W1, L0_ffn_W2, L1_xattn_in_proj_w, L1_xattn_in_proj_b, L1_xattn_out_w, L1_xattn_out_b, L1_ffn_ln1_g, L1_ffn_ln1_b, L1_ffn_ln2_g, L1_ffn_ln2_b, L1_ffn_mha_wq, L1_ffn_mha_bq, L1_ffn_mha_wk, L1_ffn_mha_bk, L1_ffn_mha_wv, L1_ffn_mha_bv, L1_ffn_mha_wo, L1_ffn_mha_bo, L1_ffn_mha_rw, L1_ffn_mha_rb, L1_ffn_ffn_rw, L1_ffn_ffn_rb, L1_ffn_fw1, L1_ffn_fw2):
    import jax
    import jax.numpy as jnp

    def _L0_xattn_ref(query, key, value, Wq, bq, Wk, bk, Wv, bv, Wo, bo):
        import jax, jax.numpy as jnp
        import numpy as np
        EMBED_DIM = 256
        NUM_HEADS = 16
        HEAD_DIM = EMBED_DIM // NUM_HEADS
        B = query.shape[0]
        q = query @ Wq.T + bq
        k = key @ Wk.T + bk
        v = value @ Wv.T + bv
        q = q.reshape(B, -1, NUM_HEADS, HEAD_DIM)
        k = k.reshape(B, -1, NUM_HEADS, HEAD_DIM)
        v = v.reshape(B, -1, NUM_HEADS, HEAD_DIM)
        scores = jnp.einsum('bqhd,bkhd->bhqk', q, k) / np.sqrt(HEAD_DIM).astype(np.float32)
        probs = jax.nn.softmax(scores, axis=-1)
        out = jnp.einsum('bhqk,bkhd->bqhd', probs, v)
        out = out.reshape(B, -1, EMBED_DIM)
        return out @ Wo.T + bo

    def _L0_ffn_ref(x, Wg, Wu, Wd, W1, W2):
        import jax, jax.numpy as jnp
        import numpy as np
        TOP_K = 2

        def _gelu(x):
            return jax.nn.gelu(x, approximate=False)
        B, S, D = x.shape
        E = Wu.shape[0]
        T = B * S
        xt = x.reshape(T, D)
        probs = jax.nn.softmax(xt @ Wg, axis=-1)
        topv, topi = jax.lax.top_k(probs, TOP_K)
        topv = topv / jnp.sum(topv, axis=-1, keepdims=True)
        cw = jnp.zeros((T, E), x.dtype).at[jnp.arange(T)[:, None], topi].set(topv)
        h = _gelu(jnp.einsum('td,edf->tef', xt, Wu))
        y = jnp.einsum('tef,efd->ted', h, Wd)
        moe = jnp.einsum('ted,te->td', y, cw)
        shared = _gelu(xt @ W1) @ W2
        return (shared + moe).reshape(B, S, D)

    def _L1_xattn_ref(q, k, v, in_proj_w, in_proj_b, out_w, out_b):
        import jax, jax.numpy as jnp
        import numpy as np
        D_MODEL = 256
        NHEAD = 16
        WINDOW = 128
        B, L, D = q.shape
        H, W = (NHEAD, WINDOW)
        hd = D // H
        nW = L // W
        Wq, Wk, Wv = (in_proj_w[:D], in_proj_w[D:2 * D], in_proj_w[2 * D:])
        bq, bk, bv = (in_proj_b[:D], in_proj_b[D:2 * D], in_proj_b[2 * D:])
        qp = (q @ Wq.T + bq).reshape(B, nW, W, H, hd)
        kp = (k @ Wk.T + bk).reshape(B, nW, W, H, hd)
        vp = (v @ Wv.T + bv).reshape(B, nW, W, H, hd)
        scale = 1.0 / np.sqrt(hd).astype(np.float32)
        scores = jnp.einsum('bnqhd,bnkhd->bnhqk', qp, kp) * scale
        attn = jax.nn.softmax(scores, axis=-1)
        out = jnp.einsum('bnhqk,bnkhd->bnqhd', attn, vp).reshape(B, L, D)
        return out @ out_w.T + out_b

    def _L1_ffn_ref(x, ln1_g, ln1_b, ln2_g, ln2_b, mha_wq, mha_bq, mha_wk, mha_bk, mha_wv, mha_bv, mha_wo, mha_bo, mha_rw, mha_rb, ffn_rw, ffn_rb, fw1, fw2):
        import jax, jax.numpy as jnp
        import numpy as np
        B, S, D, H, M, E, K = (4, 256, 256, 16, 2, 8, 2)
        KD = D // H
        F = 2 * D
        EPS = 1e-06

        def _ln(x, g, b):
            m = jnp.mean(x, axis=-1, keepdims=True)
            v = jnp.mean(jnp.square(x - m), axis=-1, keepdims=True)
            return (x - m) * jax.lax.rsqrt(v + EPS) * g + b
        n1 = _ln(x, ln1_g, ln1_b)
        mha_probs = jax.nn.softmax(jnp.mean(n1, axis=1) @ mha_rw + mha_rb, axis=-1)
        q = jnp.einsum('btd,mdhk->mbhtk', n1, mha_wq) + mha_bq[:, None, :, None, :]
        kk = jnp.einsum('btd,mdhk->mbhtk', n1, mha_wk) + mha_bk[:, None, :, None, :]
        v = jnp.einsum('btd,mdhk->mbhtk', n1, mha_wv) + mha_bv[:, None, :, None, :]
        scores = jnp.einsum('mbhtk,mbhsk->mbhts', q, kk) / jnp.sqrt(jnp.float32(KD))
        attn = jax.nn.softmax(scores, axis=-1)
        ctx = jnp.einsum('mbhts,mbhsk->mbthk', attn, v)
        mha_out = jnp.einsum('mbthk,mhkd->mbtd', ctx, mha_wo) + mha_bo[:, None, None, :]
        x = x + jnp.einsum('mbtd,bm->btd', mha_out, mha_probs)
        n2 = _ln(x, ln2_g, ln2_b)
        ffn_probs = jax.nn.softmax(jnp.mean(n2, axis=1) @ ffn_rw + ffn_rb, axis=-1)
        topk_p, topk_i = jax.lax.top_k(ffn_probs, K)
        topk_p = topk_p / jnp.sum(topk_p, axis=-1, keepdims=True)
        sw1 = fw1[topk_i]
        sw2 = fw2[topk_i]
        h = jax.nn.gelu(jnp.einsum('btd,bkdf->bktf', n2, sw1), approximate=False)
        eo = jnp.einsum('bktf,bkfd->bktd', h, sw2)
        return x + jnp.einsum('bktd,bk->btd', eo, topk_p)
    x = x + _L0_xattn_ref(_layernorm(x, axis=-1), ctx_1024, ctx_1024, L0_xattn_Wq, L0_xattn_bq, L0_xattn_Wk, L0_xattn_bk, L0_xattn_Wv, L0_xattn_bv, L0_xattn_Wo, L0_xattn_bo)
    x = x + _L0_ffn_ref(_layernorm(x, axis=-1), L0_ffn_Wg, L0_ffn_Wu, L0_ffn_Wd, L0_ffn_W1, L0_ffn_W2)
    x = x + _L1_xattn_ref(_layernorm(x, axis=-1), ctx_1024, ctx_1024, L1_xattn_in_proj_w, L1_xattn_in_proj_b, L1_xattn_out_w, L1_xattn_out_b)
    x = x + _L1_ffn_ref(_layernorm(x, axis=-1), L1_ffn_ln1_g, L1_ffn_ln1_b, L1_ffn_ln2_g, L1_ffn_ln2_b, L1_ffn_mha_wq, L1_ffn_mha_bq, L1_ffn_mha_wk, L1_ffn_mha_bk, L1_ffn_mha_wv, L1_ffn_mha_bv, L1_ffn_mha_wo, L1_ffn_mha_bo, L1_ffn_mha_rw, L1_ffn_mha_rb, L1_ffn_ffn_rw, L1_ffn_ffn_rb, L1_ffn_fw1, L1_ffn_fw2)
    return x

_drawn_inputs = setup_inputs


def setup_inputs(seed=0):
    import zlib

    import numpy as np

    out = dict(_drawn_inputs(seed))
    spreads = {'L0_xattn_bq': (0.0, 0.1),
     'L0_xattn_bk': (0.0, 2.0),
     'L0_xattn_bv': (0.0, 0.1),
     'L0_xattn_bo': (0.0, 0.1),
     'L1_xattn_in_proj_b': (0.0, 0.37),
     'L1_xattn_out_b': (0.0, 0.1),
     'L1_ffn_ln1_g': (1.0, 0.6),
     'L1_ffn_ln1_b': (0.0, 0.8),
     'L1_ffn_ln2_g': (1.0, 0.6),
     'L1_ffn_ln2_b': (0.0, 2.0),
     'L1_ffn_mha_bq': (0.0, 0.8),
     'L1_ffn_mha_bk': (0.0, 2.0),
     'L1_ffn_mha_bv': (0.0, 0.707),
     'L1_ffn_mha_bo': (0.0, 0.27),
     'L1_ffn_mha_rb': (0.0, 0.8),
     'L1_ffn_ffn_rb': (0.0, 1.331)}
    factors = {'L1_ffn_mha_wq': 8.0,
     'L1_ffn_mha_wk': 8.0,
     'L1_ffn_mha_wv': 3.383,
     'L1_ffn_mha_wo': 3.095,
     'L1_ffn_mha_rw': 8.0,
     'L1_ffn_ffn_rw': 2.739}
    for name, (base, spread) in spreads.items():
        noise = np.random.default_rng([zlib.crc32(name.encode()), seed]).standard_normal(out[name].shape)
        drawn = base * np.exp(spread * noise) if base else spread * noise
        out[name] = jnp.asarray(drawn.astype(out[name].dtype))
    for name, factor in factors.items():
        out[name] = (out[name] * factor).astype(out[name].dtype)
    return out
```

```python
from contextlib import ExitStack

import concourse.bass as bass
from concourse import mybir

F32 = mybir.dt.float32
F32R = mybir.dt.float32r
BF16 = mybir.dt.bfloat16
I32 = mybir.dt.int32
ALU = mybir.AluOpType
ACT = mybir.ActivationFunctionType
AX = mybir.AxisListType

P = 128
D = 256
H = 16
HD = D // H
KC = D // P
G = 4
T = G * P
HB = 4
PARTS = 3
Q_SLOTS = (0, 1, 2, 0, 1, 0)
K_SLOTS = (0, 0, 0, 1, 1, 2)
ROWS = 16 * len(Q_SLOTS)
NEWTON = 3
GUESS = 0x5F3759DF
FIRST_STEP = -10
LOOP_FIRST = 6
BODY = 8


def at(step, per_body, turn, const):
    return const if turn is None else const + per_body * turn


def wait(eng, sem, value):
    if isinstance(value, int) and value <= 0:
        return
    eng.wait_ge(sem, value)


def wait_apart(eng, sem, value, passed):
    wait(eng, sem, value)
    eng.sem_inc(passed, 1)


def clear_semaphores(nc, sems):
    nc.all_engine_barrier()
    nc.clear_and_free_semaphores(sems)
    nc.all_engine_barrier()


def steps(eng, n_steps, loop_first, program):
    turns = (n_steps + FIRST_STEP - loop_first) // BODY
    last_loop = loop_first + turns * BODY
    for i in range(FIRST_STEP, loop_first):
        program(i, None)
    with eng.Fori(0, turns) as turn:
        for i in range(loop_first, loop_first + BODY):
            program(i, turn)
    for i in range(last_loop, n_steps + 4):
        program(i, None)


def attention_phase(nc, name, src, context, dst, units, router, ident, identb, B):
    U = len(units)
    NG = B // G
    NM = NG * U
    N = NM * G
    XR = 2 // U
    FILLS0 = [0, 1, 2, 3, 4, 5, 6, 7, 8, 9] if U == 1 else [0, 1, 4, 5, 6, 7, "R", 8, 9]
    FILLS1 = FILLS0 if U == 1 else [4, 5, 6, 7, 8, 9]
    FPB = len(FILLS0) + len(FILLS1)
    GPB = 2 // U
    loop_first = LOOP_FIRST + (BODY if U == 2 else 0)

    def fidx(m, k):
        return FPB * (m // 2) + (len(FILLS0) if m % 2 else 0) + (FILLS1 if m % 2 else FILLS0).index(k)

    def has(m, k):
        return k in (FILLS1 if m % 2 else FILLS0)

    es = ExitStack()
    with es:
        def sb(n, shape, dt):
            return es.enter_context(nc.sbuf_tensor(f"{name}_{n}", shape, dt))

        def ps(n, shape, dt):
            return es.enter_context(nc.psum_tensor(f"{name}_{n}", shape, dt))

        sems = []

        def sem(n):
            sems.append(nc.alloc_semaphore(name=f"{name}_{n}"))
            return sems[-1]

        w32 = sb("w32", [P, 4, KC, D], F32)
        whi = sb("whi", [P, U, 4, KC, D], F32R)
        wlo = sb("wlo", [P, U, 4, KC, D], F32R)
        bq = sb("bq", [P, U, KC], F32)
        bk = sb("bk", [P, U, KC], F32)
        bv = sb("bv", [P, U, 2, D], F32)
        bo = sb("bo", [P, U, D], F32)

        x_in = sb("x_in", [P, XR, G, D], F32)
        stats = sb("stats", [P, G, 6], F32)
        moments = sb("moments", [P, G, 2], F32)
        rstd = sb("rstd", [P, G], F32)
        var_eps = sb("var_eps", [P, G], F32)
        half_bits = sb("half_bits", [P, G], I32)
        square = sb("square", [P, G], F32)
        n_tok = sb("n_tok", [P, G, D], F32)
        nT_hi = sb("nT_hi", [P, KC, T], F32R)
        nT_lo = sb("nT_lo", [P, KC, T], F32R)
        if U == 1:
            ctx_in = sb("ctx_in", [P, 2, G, D], F32)
            cT_hi = sb("cT_hi", [P, KC, T], F32R)
            cT_lo = sb("cT_lo", [P, KC, T], F32R)
        else:
            cT_hi, cT_lo = nT_hi, nT_lo
            nT = sb("nT", [P, KC, T], F32)
            gamma = sb("gamma", [P, KC], F32)
            beta = sb("beta", [P, KC], F32)
            mean = sb("mean", [P, KC, G], F32)
            rw = sb("rw", [P, KC, U], F32)
            rb = sb("rb", [P, G, U], F32)
            logit = sb("logit", [P, G, U], F32)
            lmax = sb("lmax", [P, G], F32)
            lexp = sb("lexp", [P, G, U], F32)
            lsum = sb("lsum", [P, G], F32)
            p_new = sb("p_new", [P, G, U], F32)
            p_use = sb("p_use", [P, G, U], F32)
        parts = [sb("q_parts", [P, 2, KC, PARTS, T], BF16), sb("k_parts", [P, 2, KC, PARTS, T], BF16)]
        rest = sb("rest", [P, 2, T], F32)
        qs = sb("qs", [ROWS + PARTS, 2, H, T], BF16)
        ks = sb("ks", [ROWS + PARTS, 2, H, T], BF16)
        v_aug = sb("v_aug", [P, 2, G, H, 2 * HD], F32)
        nmax = sb("nmax", [P, 2, H], F32)
        mres = sb("mres", [P, 2, H], F32)
        mparts = sb("mparts", [P, 2, PARTS, H], BF16)
        mT = sb("mT", [PARTS * H, 2, P], BF16)
        probs = sb("probs", [P, 2, H, P], F32)
        o_un = sb("o_un", [P, H // HB, P], F32)
        o_rec = sb("o_rec", [P, H], F32)
        o_tok = sb("o_tok", [P, H, HD], F32)
        oT_hi = sb("oT_hi", [P, KC, P], F32R)
        oT_lo = sb("oT_lo", [P, KC, P], F32R)
        x_res = sb("x_res", [P, G, D], F32)
        y_bias = sb("y_bias", [P, D], F32)
        y_out = sb("y_out", [P, 2, D], F32)

        S = [ps(f"S{j}", [P, HB, P], F32) for j in range(2)]
        ST = [ps(f"ST{j}", [P, HB * P], F32) for j in range(2)]
        PO = ps("PO", [P, H // HB, P], F32)
        X = ps("X", [P, T], F32)
        R = [ps(f"R{j}", [P, T], F32) for j in range(2)]

        w_loaded = [sem(f"w_loaded{u}") for u in range(U)]
        b_loaded = sem("b_loaded")
        w_hi_done, w_lo_done, ones_done = sem("w_hi_done"), sem("w_lo_done"), sem("ones_done")
        x_loaded = [sem(f"x_loaded{k}") for k in range(XR)]
        ctx_loaded = [sem(f"ctx_loaded{k}") for k in range(2)]
        xr_loaded = [sem(f"xr_loaded{b}") for b in range(G)]
        ln_stats, ln_moments, ln_guess, newton_done, n_ready = sem("ln_stats"), sem("ln_moments"), sem("ln_guess"), sem("newton_done"), sem("n_ready")
        fill_ready, fill_freed = sem("fill_ready"), sem("fill_freed")
        xT_hi_done, xT_lo_done = sem("xT_hi_done"), sem("xT_lo_done")
        part1_done, part2_done, part3_done = sem("part1_done"), sem("part2_done"), sem("part3_done")
        stacked = [sem(f"stacked{k}") for k in range(2)]
        s_ready, max_done, mpart_done, mT_ready, mT_done = (
            sem("s_ready"), sem("max_done"), sem("mpart_done"), sem("mT_ready"), sem("mT_done"))
        negmax_stacked = [sem(f"negmax_stacked{k}") for k in range(2)]
        st_ready, exp_done, pv_done, o_un_done = sem("st_ready"), sem("exp_done"), sem("pv_done"), sem("o_un_done")
        o_turned, o_rec_done, o_tok_done, oT_ready, oT_hi_done, oT_lo_done = (
            sem("o_turned"), sem("o_rec_done"), sem("o_tok_done"), sem("oT_ready"), sem("oT_hi_done"), sem("oT_lo_done"))
        y_ready, y_bias_done, y_done = sem("y_ready"), sem("y_bias_done"), sem("y_done")
        y_stored = [sem(f"y_stored{k}") for k in range(2)]
        sp_passed, pe_passed, dve_passed, pool_passed = sem("sp_passed"), sem("pe_passed"), sem("dve_passed"), sem("pool_passed")
        mean_done, rt_done, rt_exp_done, p_copied = sem("mean_done"), sem("rt_done"), sem("rt_exp_done"), sem("p_copied")

        W_IN = 16 * 4
        B_IN = 16 * (4 * U + (4 if U == 2 else 0))
        STACK_DMAS = 2 * KC * len(Q_SLOTS)

        def ub(per, i, turn, c=0):
            return at(i, per * BODY, turn, per * i + c)

        def gr(per, m, turn, c=0):
            return at(m, per * GPB, turn, per * (m // U + 1) + c)

        def fl(m, k, turn, c=0):
            return at(m, FPB, turn, fidx(m, k) + 1 + c)

        def ug_valid(m, turn):
            return turn is not None or 0 <= m < NM

        def ub_valid(i, turn):
            return turn is not None or 0 <= i < N

        def pos(turn, n):
            return 0 if turn is None else n * turn

        with nc.Block() as block:

            @block.sync
            def _(sp):
                for u, w in enumerate(units):
                    if u > 0:
                        sp.wait_ge(w_lo_done, u)
                    for k, key in enumerate(("wq", "wk", "wv", "wo")):
                        sp.dma_start(w32[:, k, :, :], w[key].rearrange("(c p) n -> p c n", p=P)).then_inc(w_loaded[u], 16)
                    sp.dma_start(bq[:, u, :], w["bq"]).then_inc(b_loaded, 16)
                    sp.dma_start(bk[:, u, :], w["bk"]).then_inc(b_loaded, 16)
                    sp.dma_start(bv[:, u, :, :], w["bv"].rearrange("(a b n) -> a b n", a=1, b=1).to_broadcast([P, 2, D])).then_inc(b_loaded, 16)
                    sp.dma_start(bo[:, u, :], w["bo"].rearrange("(a n) -> a n", a=1).to_broadcast([P, D])).then_inc(b_loaded, 16)
                if U == 2:
                    sp.dma_start(gamma[:, :], router["gamma"]).then_inc(b_loaded, 16)
                    sp.dma_start(beta[:, :], router["beta"]).then_inc(b_loaded, 16)
                    sp.dma_start(rw[:, :, :], router["rw"].rearrange("(c p) n -> p c n", p=P)).then_inc(b_loaded, 16)
                    sp.dma_start(rb[:, :, :], router["rb"].rearrange("(a b n) -> a b n", a=1, b=1).to_broadcast([P, G, U])).then_inc(b_loaded, 16)

                def program(i, turn):
                    if ub_valid(i + 1, turn):
                        k, b = (i + 1) // G % 2, (i + 1) % G
                        wait(sp, mT_done, ub(1, i + 2, turn))
                        sp.dma_start(qs[ROWS:ROWS + PARTS, k, :, b * P:(b + 1) * P], mT[:, (i + 1) % 2, :]).then_inc(negmax_stacked[(i + 1) % 2], 16)
                    m = (i + 10) // G
                    if (i + 10) % G == 0 and ug_valid(m, turn) and m % U == 0:
                        g = m // U
                        wait_apart(sp, n_ready, gr(G, m, turn, -G * XR), sp_passed)
                        sp.dma_start(x_in[:, g % XR, :, :], src[bass.ds(g * G + pos(turn, GPB * G), G)].rearrange("b t d -> t b d")).then_inc(x_loaded[g % XR], 16)
                        if U == 1:
                            if m >= 2:
                                wait_apart(sp, fill_ready, fl(m - 2, 3, turn), sp_passed)
                            sp.dma_start(ctx_in[:, m % 2, :, :], context[bass.ds(m * G + pos(turn, 2 * G), G)].rearrange("b t d -> t b d")).then_inc(ctx_loaded[m % 2], 16)
                    for r, (tile, slots) in enumerate(((qs, Q_SLOTS), (ks, K_SLOTS))):
                        m = (i + 4 - r) // G
                        if (i + 4 - r) % G == 0 and ug_valid(m, turn):
                            if m >= 2:
                                wait_apart(sp, st_ready, ub(4, 4 * m - 4, turn), sp_passed)
                            for c in range(KC):
                                wait(sp, part3_done, at(m, 8, turn, 4 * m + 2 * r + c + 1))
                                for s, part in enumerate(slots):
                                    sp.dma_start(tile[16 * s:16 * s + 16, m % 2, 8 * c:8 * c + 8, :], parts[r][:, m % 2, c, part, :]).then_inc(stacked[m % 2], 16)
                    if ub_valid(i, turn) and (i // G) % U == 0:
                        b, m = i % G, i // G
                        wait_apart(sp, y_done, ub(1, i - G + 1, turn), sp_passed)
                        sp.dma_start(x_res[:, b, :], src[bass.ds((m // U) * G + b + pos(turn, GPB * G), 1)].rearrange("b t d -> t (b d)")).then_inc(xr_loaded[b], 16)
                    if ub_valid(i - 3, turn) and ((i - 3) // G) % U == U - 1:
                        b, m = (i - 3) % G, (i - 3) // G
                        wait_apart(sp, y_done, ub(1, i - 2, turn), sp_passed)
                        sp.dma_start(dst[bass.ds((m // U) * G + b + pos(turn, GPB * G), 1)].rearrange("b t d -> t (b d)"), y_out[:, b % 2, :]).then_inc(y_stored[b % 2], 16)

                steps(sp, N, loop_first, program)
                for k in range(2):
                    sp.wait_ge(y_stored[k], 16 * B // 2)

            @block.tensor
            def _(pe):
                pe.wait_ge(w_lo_done, U)
                pe.wait_ge(ones_done, 2)

                def product(out, pairs, first=True):
                    n = 3 * len(pairs)
                    last = None
                    for q, ((ahi, alo), (bhi, blo)) in enumerate(pairs):
                        for z, (a, b_) in enumerate(((ahi, bhi), (ahi, blo), (alo, bhi))):
                            last = pe.matmul(out, a, b_, start=(q == 0 and z == 0), stop=(q == len(pairs) - 1 and z == 2))
                    return last

                def fill(m, k, turn):
                    if not ug_valid(m, turn) or not has(m, k):
                        return
                    u = m % U
                    f = fidx(m, k)
                    r = R[f % FPB % 2]
                    back = 1 if (U == 2 and f % FPB == 0) else 2
                    wait(pe, fill_freed, fl(m, k, turn, -back))
                    if k in (0, 1):
                        wait(pe, n_ready, gr(G, m, turn))
                        for b in range(G):
                            last = pe.transpose(r[:, b * P:(b + 1) * P], n_tok[:, b, k * P:(k + 1) * P], ident[:, :])
                    elif k in (2, 3):
                        wait(pe, ctx_loaded[m % 2], at(m, 16, turn, 16 * (m // 2 + 1)))
                        for b in range(G):
                            last = pe.transpose(r[:, b * P:(b + 1) * P], ctx_in[:, m % 2, b, (k - 2) * P:(k - 1) * P], ident[:, :])
                    elif k in (4, 5, 6, 7):
                        t, c = (k - 4) // 2, k % 2
                        if U == 1:
                            wait(pe, fill_freed, fl(m, 3, turn))
                        else:
                            wait(pe, xT_lo_done, gr(2, m, turn))
                        hi, lo = (nT_hi, nT_lo) if t == 0 else (cT_hi, cT_lo)
                        last = product(r[:, :], [((whi[:, u, t, kc, c * P:(c + 1) * P], wlo[:, u, t, kc, c * P:(c + 1) * P]),
                                                  (hi[:, kc, :], lo[:, kc, :])) for kc in range(KC)])
                    elif k == "R":
                        wait(pe, mean_done, gr(2, m, turn))
                        for b in range(G):
                            for kc in range(KC):
                                last = pe.matmul(r[:, b * U:(b + 1) * U], mean[:, kc, b:b + 1].to_broadcast([P, P]), rw[:, kc, :],
                                                 start=(kc == 0), stop=(kc == KC - 1))
                    else:
                        for j in range(2):
                            b = 2 * (k - 8) + j
                            last = product(r[:, j * D:(j + 1) * D], [((cT_hi[:, kc, b * P:(b + 1) * P], cT_lo[:, kc, b * P:(b + 1) * P]),
                                                                     (whi[:, u, 2, kc, :], wlo[:, u, 2, kc, :])) for kc in range(KC)])
                    last.then_inc(fill_ready, 1)

                def scores(i, j, turn):
                    k, b = i // G % 2, i % G
                    m = i // G
                    if b == 0 and j == 0:
                        wait(pe, stacked[k], at(m, 16 * STACK_DMAS, turn, 16 * STACK_DMAS * (m // 2 + 1)))
                    wait(pe, max_done, ub(4, i, turn, j - 1))
                    for h in range(HB * j, HB * j + HB):
                        last = pe.matmul(S[j % 2][:, h % HB, :], qs[0:ROWS, k, h, b * P:(b + 1) * P], ks[0:ROWS, k, h, b * P:(b + 1) * P],
                                         start=True, stop=True)
                    last.then_inc(s_ready, 1)

                def scores_turned(i, j, turn):
                    k, b = i // G % 2, i % G
                    if j == 0:
                        wait(pe, negmax_stacked[i % 2], at(i, 16 * BODY // 2, turn, 16 * (i // 2 + 1)))
                    wait(pe, exp_done, ub(4, i, turn, j - 1))
                    for h in range(HB * j, HB * j + HB):
                        last = pe.matmul(ST[j % 2][:, (h % HB) * P:(h % HB + 1) * P], ks[:, k, h, b * P:(b + 1) * P], qs[:, k, h, b * P:(b + 1) * P],
                                         start=True, stop=True)
                    last.then_inc(st_ready, 1)

                def weigh(i, j, turn):
                    k, b, m = i // G % 2, i % G, i // G
                    if j == 0:
                        wait(pe, o_un_done, ub(1, i, turn))
                        wait(pe, fill_freed, fl(m, 8 + b // 2, turn))
                    wait(pe, exp_done, ub(4, i, turn, j + 1))
                    for q in range(HB):
                        h = HB * j + q
                        last = pe.matmul(PO[32 * q:32 * q + 32, j, :], v_aug[:, k, b, h, :], probs[:, i % 2, h, :], start=True, stop=True)
                    last.then_inc(pv_done, 1)

                def program(i, turn):
                    if ub_valid(i + 1, turn):
                        wait(pe, mpart_done, ub(4, i + 2, turn))
                        wait_apart(pe, y_bias_done, ub(1, i - 2, turn), pe_passed)
                        pe.transpose(X[0:PARTS * H, 0:P // 2].bitcast(BF16), mparts[:, (i + 1) % 2, :, :].rearrange("p a h -> p (a h)"),
                                     identb[:, :]).then_inc(mT_ready, 1)
                    d = i - 2
                    for j in range(4):
                        if ub_valid(i + 2, turn):
                            scores(i + 2, j, turn)
                        if ub_valid(i, turn):
                            scores_turned(i, j, turn)
                        if ub_valid(i - 1, turn):
                            weigh(i - 1, j, turn)
                        if ub_valid(d, turn):
                            if j == 0:
                                wait(pe, o_un_done, ub(1, d + 1, turn))
                                if ub_valid(i + 1, turn):
                                    wait(pe, mT_done, ub(1, i + 2, turn))
                                wait(pe, y_bias_done, ub(1, d, turn))
                                for q in range(H // HB):
                                    last = pe.transpose(X[:, q * P:(q + 1) * P], o_un[:, q, :], ident[:, :])
                                last.then_inc(o_turned, 1)
                            elif j == 1:
                                wait(pe, o_tok_done, ub(1, d + 1, turn))
                                for c in range(KC):
                                    last = pe.transpose(X[:, c * P:(c + 1) * P], o_tok[:, 8 * c:8 * c + 8, :].rearrange("p h d -> p (h d)"), ident[:, :])
                                last.then_inc(oT_ready, 1)
                            elif j == 2:
                                wait(pe, oT_lo_done, ub(1, d + 1, turn))
                                u = (d // G) % U
                                product(X[:, 0:D], [((oT_hi[:, kc, :], oT_lo[:, kc, :]), (whi[:, u, 3, kc, :], wlo[:, u, 3, kc, :]))
                                                    for kc in range(KC)]).then_inc(y_ready, 1)
                        m, r = (i + 7) // G, (i + 7) % G
                        if r == 0:
                            if j == 0:
                                fill(m - 1, 8, turn)
                                fill(m - 1, 9, turn)
                            for k in ([0], [1], [2], [3])[j]:
                                fill(m, k, turn)
                        elif r in (1, 2) and j in (0, 2):
                            fill(m, 2 + 2 * r + j // 2, turn)
                        elif r == 3 and j == 0:
                            fill(m, "R", turn)

                steps(pe, N, loop_first, program)

            @block.scalar
            def _(act):
                for u in range(U):
                    act.wait_ge(w_loaded[u], W_IN)
                    act.activation(whi[:, u, :, :, :].rearrange("p k c n -> p (k c n)"), w32[:, :, :, :].rearrange("p k c n -> p (k c n)"),
                                   ACT.Copy).then_inc(w_hi_done, 1)
                act.wait_ge(b_loaded, B_IN)

                def fill_out(m, k, turn):
                    if not ug_valid(m, turn) or not has(m, k):
                        return
                    u = m % U
                    r = R[fidx(m, k) % FPB % 2]
                    if k in (0, 1, 2, 3):
                        if U == 1:
                            hi = nT_hi if k < 2 else cT_hi
                            wait(act, fill_ready, fl(m, k, turn))
                            act.activation(hi[:, k % 2, :], r[:, :], ACT.Copy).then_inc(xT_hi_done, 1)
                        else:
                            wait(act, fill_freed, fl(m, k, turn))
                            act.activation(nT_hi[:, k, :], nT[:, k, :], ACT.Copy).then_inc(xT_hi_done, 1)
                    elif k in (4, 5, 6, 7):
                        t, c = (k - 4) // 2, k % 2
                        bias = (bq, bk)[t]
                        if m >= 2:
                            wait(act, stacked[m % 2], at(m, 16 * STACK_DMAS, turn, 16 * STACK_DMAS * (m // 2)))
                        wait(act, fill_ready, fl(m, k, turn))
                        act.activation(parts[t][:, m % 2, c, 0, :], r[:, :], ACT.Identity, bias=bias[:, u, c:c + 1]).then_inc(part1_done, 1)

                def part2(m, k, turn):
                    if not ug_valid(m, turn):
                        return
                    t, c = (k - 4) // 2, k % 2
                    wait(act, fill_freed, fl(m, k, turn))
                    act.activation(parts[t][:, m % 2, c, 1, :], rest[:, k % 2, :], ACT.Copy).then_inc(part2_done, 1)

                def program(i, turn):
                    if ub_valid(i + 1, turn):
                        wait(act, mT_ready, ub(1, i + 2, turn))
                        wait(act, negmax_stacked[(i + 1) % 2], at(i, 16 * BODY // 2, turn, 16 * ((i + 1) // 2)))
                        act.activation(mT[:, (i + 1) % 2, :], X[0:PARTS * H, 0:P // 2].bitcast(BF16), ACT.Copy).then_inc(mT_done, 1)
                    m, r = (i + 7) // G, (i + 7) % G
                    for j in range(4):
                        if ub_valid(i, turn):
                            wait(act, st_ready, ub(4, i, turn, j + 1))
                            wait(act, pv_done, ub(4, i - 2, turn, j + 1))
                            act.activation(probs[:, i % 2, HB * j:HB * j + HB, :].rearrange("p h q -> p (h q)"), ST[j % 2][:, :], ACT.Exp,
                                           scale=float(HD) ** -0.5).then_inc(exp_done, 1)
                        if j == 1 and ub_valid(i - 2, turn):
                            wait(act, oT_ready, ub(1, i - 1, turn))
                            act.activation(oT_hi[:, :, :].rearrange("p c t -> p (c t)"), X[:, 0:D], ACT.Copy).then_inc(oT_hi_done, 1)
                        if r == 0:
                            fill_out(m, j, turn)
                        elif r in (1, 2):
                            k = 2 + 2 * r + j // 2
                            if j in (0, 2):
                                fill_out(m, k, turn)
                            else:
                                part2(m, k, turn)
                        elif r == 3 and j == 2 and has(m, "R") and ug_valid(m, turn):
                            wait(act, rt_done, gr(4, m, turn, -1))
                            act.activation(lexp[:, :, :], logit[:, :, :], ACT.Exp).then_inc(rt_exp_done, 1)
                    if ub_valid(i - 1, turn):
                        wait(act, pv_done, ub(4, i, turn))
                        wait(act, o_turned, ub(1, i - 1, turn))
                        act.activation(o_un[:, :, :].rearrange("p c t -> p (c t)"), PO[:, :, :].rearrange("p c t -> p (c t)"), ACT.Copy).then_inc(o_un_done, 1)

                steps(act, N, loop_first, program)

            @block.vector
            def _(dve):
                for u in range(U):
                    dve.wait_ge(w_hi_done, u + 1)
                    dve.tensor_tensor(wlo[:, u, :, :, :].rearrange("p k c n -> p (k c n)"), w32[:, :, :, :].rearrange("p k c n -> p (k c n)"),
                                      whi[:, u, :, :, :].rearrange("p k c n -> p (k c n)"), ALU.subtract).then_inc(w_lo_done, 1)
                dve.wait_ge(b_loaded, B_IN)

                def layernorm(m, turn):
                    g = m // U
                    wait(dve, x_loaded[g % XR], at(m, 16, turn, 16 * (g // XR + 1)))
                    wait(dve, n_ready, gr(G, m, turn, -G))
                    for b in range(G):
                        dve.bn_stats(stats[:, b, :], x_in[:, g % XR, b, :]).then_inc(ln_stats, 1)
                    for b in range(G):
                        wait_apart(dve, ln_stats, gr(G, m, turn, b + 1 - G), dve_passed)
                        dve.bn_aggr(moments[:, b, :], stats[:, b, :]).then_inc(ln_moments, 1)
                    wait(dve, ln_moments, gr(G, m, turn))
                    dve.tensor_scalar(var_eps[:, :], moments[:, :, 1:2].rearrange("p b o -> p (b o)"), 1e-5 if U == 1 else 1e-6, None,
                                      ALU.add).then_inc(ln_guess, 1)
                    wait(dve, ln_guess, gr(3, m, turn, -2))
                    dve.tensor_scalar(half_bits[:, :], var_eps[:, :].bitcast(I32), 1, None, ALU.logical_shift_right).then_inc(ln_guess, 1)
                    wait(dve, ln_guess, gr(3, m, turn, -1))
                    dve.tensor_scalar(rstd[:, :].bitcast(I32), half_bits[:, :], -1, GUESS, ALU.mult, ALU.add).then_inc(ln_guess, 1)
                    wait(dve, newton_done, gr(4 * NEWTON, m, turn))
                    if m >= U:
                        wait(dve, fill_ready, fl(m - U, 1, turn))
                    for b in range(G):
                        dve.tensor_scalar(n_tok[:, b, :], x_in[:, g % XR, b, :], moments[:, b, 0:1], rstd[:, b:b + 1],
                                          ALU.subtract, ALU.mult).then_inc(n_ready, 1)

                def fill_out(m, k, turn):
                    if not ug_valid(m, turn) or not has(m, k):
                        return
                    u = m % U
                    r = R[fidx(m, k) % FPB % 2]
                    if k in (0, 1, 2, 3):
                        if U == 1:
                            hi, lo = (nT_hi, nT_lo) if k < 2 else (cT_hi, cT_lo)
                            wait(dve, xT_hi_done, gr(4, m, turn, k - 3))
                            dve.tensor_tensor(lo[:, k % 2, :], r[:, :], hi[:, k % 2, :], ALU.subtract).then_inc(fill_freed, 1)
                        else:
                            wait(dve, fill_ready, fl(m, k, turn))
                            wait(dve, xT_lo_done, gr(2, m, turn, -2))
                            dve.tensor_scalar(nT[:, k, :], r[:, :], gamma[:, k:k + 1], beta[:, k:k + 1], ALU.mult, ALU.add).then_inc(fill_freed, 1)
                    elif k in (4, 5, 6, 7):
                        t, c = (k - 4) // 2, k % 2
                        bias = (bq, bk)[t]
                        wait(dve, part1_done, at(m, 8, turn, 4 * m + k - 3))
                        wait(dve, part3_done, at(m, 8, turn, 4 * m + k - 5))
                        dve.scalar_tensor_tensor(rest[:, k % 2, :], r[:, :], bias[:, u, c:c + 1], parts[t][:, m % 2, c, 0, :],
                                                 ALU.add, ALU.subtract).then_inc(fill_freed, 1)
                    elif k == "R":
                        wait(dve, fill_ready, fl(m, k, turn))
                        dve.scalar_tensor_tensor(logit[:, :, :].rearrange("p b u -> p (b u)"), r[:, 0:G * U], 1.0 / P,
                                                 rb[:, :, :].rearrange("p b u -> p (b u)"), ALU.mult, ALU.add).then_inc(fill_freed, 1)
                        wait(dve, fill_freed, fl(m, k, turn))
                        dve.tensor_reduce(lmax[:, :], logit[:, :, :], AX.X, ALU.max).then_inc(rt_done, 1)
                        wait(dve, rt_done, gr(4, m, turn, -3))
                        dve.tensor_tensor(lexp[:, :, :], logit[:, :, :], lmax[:, :].rearrange("p (b o) -> p b o", o=1).to_broadcast([P, G, U]),
                                          ALU.subtract).then_inc(rt_done, 1)
                        wait(dve, rt_done, gr(4, m, turn, -2))
                        dve.tensor_copy(logit[:, :, :], lexp[:, :, :]).then_inc(rt_done, 1)
                    else:
                        wait(dve, fill_ready, fl(m, k, turn))
                        if m >= 2:
                            wait(dve, pv_done, ub(4, 4 * m - 4, turn))
                        b = 2 * (k - 8)
                        dve.tensor_tensor(v_aug[:, m % 2, b:b + 2, :, 0:HD], r[:, :].rearrange("p (b h d) -> p b h d", b=2, h=H),
                                          bv[:, u, :, :].rearrange("p b (h d) -> p b h d", h=H), ALU.add).then_inc(fill_freed, 1)

                def unit_weights(m, turn):
                    wait(dve, rt_exp_done, gr(1, m, turn))
                    dve.tensor_reduce(lsum[:, :], lexp[:, :, :], AX.X, ALU.add).then_inc(rt_done, 1)
                    wait(dve, rt_done, gr(4, m, turn))
                    wait(dve, p_copied, gr(3, m, turn, -3))
                    dve.reciprocal(lmax[:, :], lsum[:, :]).then_inc(p_copied, 1)
                    wait(dve, p_copied, gr(3, m, turn, -2))
                    dve.tensor_tensor(p_new[:, :, :], lexp[:, :, :], lmax[:, :].rearrange("p (b o) -> p b o", o=1).to_broadcast([P, G, U]),
                                      ALU.mult).then_inc(p_copied, 1)

                def maximum(i, j, turn):
                    wait(dve, s_ready, ub(4, i, turn, j + 1))
                    if j == 0:
                        wait(dve, mpart_done, ub(4, i - 1, turn))
                    dve.tensor_reduce(nmax[:, i % 2, HB * j:HB * j + HB], S[j % 2][:, :, :], AX.X, ALU.max, negate=True).then_inc(max_done, 1)

                def program(i, turn):
                    m, r = (i + 7) // G, (i + 7) % G
                    d = i - 2
                    u, b = (d // G) % U, d % G
                    for j in range(4):
                        if ub_valid(i + 2, turn):
                            maximum(i + 2, j, turn)
                        if r == 0 and j == 0:
                            fill_out(m - 1, 8, turn)
                            fill_out(m - 1, 9, turn)
                        if r == 0:
                            fill_out(m, j, turn)
                        elif r in (1, 2) and j in (0, 2):
                            fill_out(m, 2 + 2 * r + j // 2, turn)
                        elif r == 1 and j == 1 and U == 2 and ug_valid(m, turn) and m % 2 == 0:
                            if m >= U:
                                wait(dve, fill_ready, fl(m - U, "R", turn))
                            for c in range(KC):
                                dve.tensor_reduce(mean[:, c, :], nT[:, c, :].rearrange("p (b t) -> p b t", b=G), AX.X, ALU.add).then_inc(mean_done, 1)
                        elif r == 3 and U == 2 and ug_valid(m, turn) and m % 2 == 0:
                            if j == 0:
                                fill_out(m, "R", turn)
                            elif j == 3:
                                unit_weights(m, turn)
                        if ub_valid(d, turn):
                            if j == 0:
                                wait(dve, o_turned, ub(1, d + 1, turn))
                                xv = X[:, :].rearrange("p (h e) -> p h e", h=H)
                                dve.reciprocal(o_rec[:, :].rearrange("p (h o) -> p h o", o=1), xv[:, :, HD:HD + 1]).then_inc(o_rec_done, 1)
                                wait(dve, o_rec_done, ub(1, d + 1, turn))
                                dve.tensor_tensor(o_tok[:, :, :], xv[:, :, 0:HD], o_rec[:, :].rearrange("p (h o) -> p h o", o=1).to_broadcast([P, H, HD]),
                                                  ALU.mult).then_inc(o_tok_done, 1)
                            elif j == 1:
                                wait(dve, oT_hi_done, ub(1, d + 1, turn))
                                dve.tensor_tensor(oT_lo[:, :, :].rearrange("p c t -> p (c t)"), X[:, 0:D], oT_hi[:, :, :].rearrange("p c t -> p (c t)"),
                                                  ALU.subtract).then_inc(oT_lo_done, 1)
                            elif j == 2:
                                wait(dve, y_ready, ub(1, d + 1, turn))
                                wait(dve, y_done, ub(1, d, turn))
                                dve.tensor_tensor(y_bias[:, :], X[:, 0:D], bo[:, u, :], ALU.add).then_inc(y_bias_done, 1)
                            elif U == 2:
                                if u == 0 and b == 0:
                                    wait(dve, p_copied, gr(3, d // G, turn, -1))
                                    wait(dve, y_done, ub(1, d, turn))
                                    dve.tensor_copy(p_use[:, :, :], p_new[:, :, :]).then_inc(p_copied, 1)
                                if b == 0 and u == 0:
                                    wait(dve, p_copied, gr(3, d // G, turn))
                                wait(dve, y_bias_done, ub(1, d + 1, turn))
                                if u == 0:
                                    wait(dve, xr_loaded[b], gr(16, d // G, turn))
                                else:
                                    wait(dve, y_stored[b % 2], at(d, 32, turn, 16 * (2 * (d // 8) + b // 2)))
                                    wait(dve, y_done, ub(1, d - 3, turn))
                                out = x_res[:, b, :] if u == 0 else y_out[:, b % 2, :]
                                dve.scalar_tensor_tensor(out, y_bias[:, :], p_use[:, b, u:u + 1], x_res[:, b, :], ALU.mult, ALU.add).then_inc(y_done, 1)
                    if r == 3 and U == 1 and ug_valid(m + 1, turn):
                        layernorm(m + 1, turn)
                    if r == 3 and U == 2 and m % 2 == 1 and ug_valid(m + 1, turn):
                        layernorm(m + 1, turn)

                steps(dve, N, loop_first, program)

            @block.gpsimd
            def _(pool):
                pool.memset(v_aug[:, :, :, :, HD:2 * HD], 1.0).then_inc(ones_done, 1)
                pool.wait_ge(ones_done, 1)
                pool.memset(ks[ROWS:ROWS + PARTS, :, :, :], 1.0).then_inc(ones_done, 1)
                pool.wait_ge(ones_done, 2)

                def rstd_newton(m, turn):
                    done = 0

                    def stepped(instruction):
                        nonlocal done
                        done += 1
                        instruction.then_inc(newton_done, 1)
                        wait_apart(pool, newton_done, gr(4 * NEWTON, m, turn, done - 4 * NEWTON), pool_passed)

                    wait(pool, ln_guess, gr(3, m, turn))
                    for _ in range(NEWTON):
                        stepped(pool.tensor_tensor(square[:, :], rstd[:, :], rstd[:, :], ALU.mult))
                        stepped(pool.tensor_tensor(square[:, :], square[:, :], var_eps[:, :], ALU.mult))
                        stepped(pool.tensor_scalar(square[:, :], square[:, :], -0.5, 1.5, ALU.mult, ALU.add))
                        stepped(pool.tensor_tensor(rstd[:, :], rstd[:, :], square[:, :], ALU.mult))

                def program(i, turn):
                    m, r = (i + 7) // G, (i + 7) % G
                    if r == 3 and ug_valid(m + 1, turn) and (m + 1) % U == 0:
                        rstd_newton(m + 1, turn)
                    if r in (1, 2) and ug_valid(m, turn):
                        for c in range(KC):
                            wait(pool, part2_done, at(m, 8, turn, 4 * m + 2 * (r - 1) + c + 1))
                            pool.tensor_tensor(parts[r - 1][:, m % 2, c, 2, :], rest[:, c, :], parts[r - 1][:, m % 2, c, 1, :],
                                               ALU.subtract).then_inc(part3_done, 1)
                    if U == 2 and r == 0 and ug_valid(m, turn) and m % 2 == 0:
                        for c in range(KC):
                            wait(pool, xT_hi_done, gr(2, m, turn, c - 1))
                            pool.tensor_tensor(nT_lo[:, c, :], nT[:, c, :], nT_hi[:, c, :], ALU.subtract).then_inc(xT_lo_done, 1)
                    if U == 1 and ub_valid(i - 2, turn):
                        d = i - 2
                        wait(pool, y_bias_done, ub(1, d + 1, turn))
                        wait(pool, xr_loaded[d % G], gr(16, d // G, turn))
                        wait(pool, y_stored[d % 2], at(d, 16 * BODY // 2, turn, 16 * (d // 2)))
                        pool.tensor_tensor(y_out[:, d % 2, :], y_bias[:, :], x_res[:, d % G, :], ALU.add).then_inc(y_done, 1)
                    if ub_valid(i + 2, turn):
                        e, z = i + 2, i % 2
                        wait(pool, max_done, ub(4, e + 1, turn))
                        wait_apart(pool, mT_ready, ub(1, e - 1, turn), pool_passed)
                        pool.tensor_copy(mparts[:, z, 0, :], nmax[:, z, :]).then_inc(mpart_done, 1)
                        wait(pool, mpart_done, ub(4, e, turn, 1))
                        pool.tensor_tensor(mres[:, z, :], nmax[:, z, :], mparts[:, z, 0, :], ALU.subtract).then_inc(mpart_done, 1)
                        wait_apart(pool, mpart_done, ub(4, e, turn, 2), pool_passed)
                        pool.tensor_copy(mparts[:, z, 1, :], mres[:, z, :]).then_inc(mpart_done, 1)
                        wait(pool, mpart_done, ub(4, e, turn, 3))
                        pool.tensor_tensor(mparts[:, z, 2, :], mres[:, z, :], mparts[:, z, 1, :], ALU.subtract).then_inc(mpart_done, 1)

                steps(pool, N, loop_first, program)
        clear_semaphores(nc, sems)


E = 8
F = 512
FC = F // P
TOP = 2
U32 = mybir.dt.uint32
BELOW_ALL = -3.0e38


def newton_steps(eng, done, counted, rstd, square, minus_half_var):
    n = 0
    for _ in range(NEWTON):
        for out, a, b, op in ((square, rstd, rstd, ALU.mult), (square, square, minus_half_var, ALU.mult)):
            eng.tensor_tensor(out[:, :], a[:, :], b[:, :], op).then_inc(done, 1)
            n += 1
            counted(n)
        eng.scalar_tensor_tensor(rstd[:, :], square[:, :], 1.5, rstd[:, :], ALU.add, ALU.mult).then_inc(done, 1)
        n += 1
        counted(n)


def route_phase(nc, name, src, n_dst, by_token, w_router, b_router, gamma, beta, logits, ident, ones, B):
    NG = B // G
    with ExitStack() as es:
        def sb(n, shape, dt):
            return es.enter_context(nc.sbuf_tensor(f"{name}_{n}", shape, dt))

        def ps(n, shape, dt):
            return es.enter_context(nc.psum_tensor(f"{name}_{n}", shape, dt))

        sems = []

        def sem(n):
            sems.append(nc.alloc_semaphore(name=f"{name}_{n}"))
            return sems[-1]

        x_in = sb("x_in", [P, 2, G, D], F32)
        n_tok = sb("n_tok", [P, 2, G, D], F32)
        stats = sb("stats", [P, G, 6], F32)
        moments = sb("moments", [P, G, 2], F32)
        var_eps = sb("var_eps", [P, G], F32)
        half_bits = sb("half_bits", [P, G], I32)
        square = sb("square", [P, G], F32)
        rstd = sb("rstd", [P, G], F32)
        rw = sb("rw", [P, KC, E], F32)
        rb = sb("rb", [P, G, E], F32)
        cols = sb("cols", [P, KC, T if by_token else G], F32)
        PT = [ps(f"PT{c}", [P, T], F32) for c in range(KC)]
        PL = [ps(f"PL{k}", [P, T], F32) for k in range(2)]
        if not by_token:
            gam = sb("gam", [P, D], F32)
            bet = sb("bet", [P, D], F32)

        w_loaded = sem("w_loaded")
        x_loaded = [sem(f"x_loaded{k}") for k in range(2)]
        n_stored = [sem(f"n_stored{k}") for k in range(2)]
        ln_stats, ln_moments, ln_guess, newton_done = sem("ln_stats"), sem("ln_moments"), sem("ln_guess"), sem("newton_done")
        n_plain, n_scaled, n_ready = sem("n_plain"), sem("n_scaled"), sem("n_ready")
        pt_ready, cols_done, pl_ready, logits_done = sem("pt_ready"), sem("cols_done"), sem("pl_ready"), sem("logits_done")
        sp_passed, dve_passed = sem("sp_passed"), sem("dve_passed")
        W_IN = 16 if by_token else 64
        routed = logits is not None

        def cnt(per, turn, k, c=0):
            return per * (2 * turn + k + 1) + c

        with nc.Block() as block:

            @block.sync
            def _(sp):
                if routed:
                    sp.dma_start(rw[:, :, :], w_router.rearrange("(c p) e -> p c e", p=P)).then_inc(w_loaded, 16)
                if not by_token:
                    sp.dma_start(rb[:, :, :], b_router.rearrange("(a b e) -> a b e", a=1, b=1).to_broadcast([P, G, E])).then_inc(w_loaded, 16)
                    sp.dma_start(gam[:, :], gamma.rearrange("(a n) -> a n", a=1).to_broadcast([P, D])).then_inc(w_loaded, 16)
                    sp.dma_start(bet[:, :], beta.rearrange("(a n) -> a n", a=1).to_broadcast([P, D])).then_inc(w_loaded, 16)
                for k in range(2):
                    sp.dma_start(x_in[:, k, :, :], src[k * G:k * G + G].rearrange("b t d -> t b d")).then_inc(x_loaded[k], 16)
                with sp.Fori(0, NG // 2 - 1) as turn:
                    for k in range(2):
                        wait_apart(sp, n_ready, cnt(1, turn, k), sp_passed)
                        sp.dma_start(n_dst[bass.ds((2 * turn + k) * G, G)].rearrange("b t d -> t b d"), n_tok[:, k, :, :]).then_inc(n_stored[k], 16)
                        sp.dma_start(x_in[:, k, :, :], src[bass.ds((2 * turn + k + 2) * G, G)].rearrange("b t d -> t b d")).then_inc(x_loaded[k], 16)
                for k in range(2):
                    sp.wait_ge(n_ready, NG - 1 + k)
                    sp.dma_start(n_dst[(NG - 2 + k) * G:(NG - 1 + k) * G].rearrange("b t d -> t b d"), n_tok[:, k, :, :]).then_inc(n_stored[k], 16)
                for k in range(2):
                    sp.wait_ge(n_stored[k], 16 * NG // 2)

            @block.vector
            def _(dve):
                if routed:
                    dve.wait_ge(w_loaded, W_IN)

                def group(turn, k, first):
                    dve.wait_ge(x_loaded[k], 16 * (turn + 1))
                    for b in range(G):
                        dve.bn_stats(stats[:, b, :], x_in[:, k, b, :]).then_inc(ln_stats, 1)
                    for b in range(G):
                        wait_apart(dve, ln_stats, cnt(G, turn, k, b + 1 - G), dve_passed)
                        dve.bn_aggr(moments[:, b, :], stats[:, b, :]).then_inc(ln_moments, 1)
                    dve.wait_ge(ln_moments, cnt(G, turn, k))
                    var = moments[:, :, 1:2].rearrange("p b o -> p (b o)")
                    eps = 1e-5 if by_token else 1e-6
                    dve.tensor_scalar(var_eps[:, :], var, eps, None, ALU.add).then_inc(ln_guess, 1)
                    dve.wait_ge(ln_guess, cnt(4, turn, k, -3))
                    dve.tensor_scalar(half_bits[:, :], var_eps[:, :].bitcast(I32), 1, None, ALU.logical_shift_right).then_inc(ln_guess, 1)
                    dve.wait_ge(ln_guess, cnt(4, turn, k, -2))
                    dve.tensor_scalar(rstd[:, :].bitcast(I32), half_bits[:, :], -1, GUESS, ALU.mult, ALU.add).then_inc(ln_guess, 1)
                    dve.tensor_scalar(var_eps[:, :], var, eps, -0.5, ALU.add, ALU.mult).then_inc(ln_guess, 1)
                    dve.wait_ge(ln_guess, cnt(4, turn, k))
                    per = 3 * NEWTON
                    newton_steps(dve, newton_done, lambda n: dve.wait_ge(newton_done, cnt(per, turn, k, n - per)), rstd, square, var_eps)
                    if not first:
                        dve.wait_ge(n_stored[k], 16 * turn)
                        if routed:
                            dve.wait_ge(cols_done, cnt(KC if by_token else 1, turn, k, -2 * (KC if by_token else 1)))
                    for b in range(G):
                        ins = dve.tensor_scalar(n_tok[:, k, b, :], x_in[:, k, b, :], moments[:, b, 0:1], rstd[:, b:b + 1], ALU.subtract, ALU.mult)
                        ins.then_inc(n_plain, 1)
                    dve.wait_ge(n_plain, cnt(G, turn, k))
                    if by_token:
                        dve.sem_inc(n_ready, 1)
                    else:
                        v = n_tok[:, k, :, :]
                        dve.tensor_tensor(v, v, gam[:, :].rearrange("p (o n) -> p o n", o=1).to_broadcast([P, G, D]), ALU.mult).then_inc(n_scaled, 1)
                        dve.wait_ge(n_scaled, cnt(1, turn, k))
                        dve.tensor_tensor(v, v, bet[:, :].rearrange("p (o n) -> p o n", o=1).to_broadcast([P, G, D]), ALU.add).then_inc(n_ready, 1)
                    if not routed:
                        return
                    dve.wait_ge(pl_ready, cnt(1, turn, k))
                    out = logits[:, bass.ds((2 * turn + k) * G, G), :]
                    pl = PL[k][:, 0:G * E].rearrange("p (b e) -> p b e", b=G)
                    if by_token:
                        dve.tensor_copy(out, pl).then_inc(logits_done, 1)
                    else:
                        dve.tensor_tensor(out, pl, rb[:, :, :], ALU.add).then_inc(logits_done, 1)

                for k in range(2):
                    group(0, k, True)
                with dve.Fori(1, NG // 2) as turn:
                    for k in range(2):
                        group(turn, k, False)

            if routed:
                @block.tensor
                def _(pe):
                    pe.wait_ge(w_loaded, W_IN)

                    def group(turn, k, first):
                        pe.wait_ge(n_ready, cnt(1, turn, k))
                        if by_token:
                            for c in range(KC):
                                if not (first and k == 0):
                                    pe.wait_ge(cols_done, cnt(KC, turn, k, c + 1 - 2 * KC))
                                for b in range(G):
                                    last = pe.transpose(PT[c][:, b * P:(b + 1) * P], n_tok[:, k, b, c * P:(c + 1) * P], ident[:, :])
                                last.then_inc(pt_ready, 1)
                            pe.wait_ge(cols_done, cnt(KC, turn, k))
                        else:
                            if not (first and k == 0):
                                pe.wait_ge(cols_done, cnt(1, turn, k, -1))
                            for c in range(KC):
                                for b in range(G):
                                    last = pe.matmul(PT[0][:, c * G + b:c * G + b + 1], n_tok[:, k, b, c * P:(c + 1) * P], ones[:, 0:1], start=True, stop=True)
                            last.then_inc(pt_ready, 1)
                            pe.wait_ge(cols_done, cnt(1, turn, k))
                        if not first:
                            pe.wait_ge(logits_done, cnt(1, turn, k, -2))
                        for b in range(G):
                            for c in range(KC):
                                a = cols[:, c, b * P:(b + 1) * P] if by_token else cols[:, c, b:b + 1].to_broadcast([P, P])
                                last = pe.matmul(PL[k][:, b * E:(b + 1) * E], a, rw[:, c, :], start=(c == 0), stop=(c == KC - 1))
                        last.then_inc(pl_ready, 1)

                    for k in range(2):
                        group(0, k, True)
                    with pe.Fori(1, NG // 2) as turn:
                        for k in range(2):
                            group(turn, k, False)

                @block.scalar
                def _(act):
                    def group(turn, k, first):
                        if not (first and k == 0):
                            act.wait_ge(pl_ready, cnt(1, turn, k, -1))
                        if by_token:
                            for c in range(KC):
                                act.wait_ge(pt_ready, cnt(KC, turn, k, c + 1 - KC))
                                act.activation(cols[:, c, :], PT[c][:, :], ACT.Copy).then_inc(cols_done, 1)
                        else:
                            act.wait_ge(pt_ready, cnt(1, turn, k))
                            act.activation(cols[:, :, :].rearrange("p c b -> p (c b)"), PT[0][:, 0:KC * G], ACT.Copy, scale=1.0 / P).then_inc(cols_done, 1)

                    for k in range(2):
                        group(0, k, True)
                    with act.Fori(1, NG // 2) as turn:
                        for k in range(2):
                            group(turn, k, False)
        clear_semaphores(nc, sems)


def top_two_phase(nc, name, logits, weights, experts, tokens_sorted, B):
    with ExitStack() as es:
        def sb(n, shape, dt):
            return es.enter_context(nc.sbuf_tensor(f"{name}_{n}", shape, dt))

        sems = []

        def sem(n):
            sems.append(nc.alloc_semaphore(name=f"{name}_{n}"))
            return sems[-1]

        rev = sb("rev", [P, B, E], F32)
        eq = sb("eq", [P, B, E], F32)
        best = sb("best", [P, TOP, B], F32)
        pick = sb("pick", [P, TOP, B], F32)
        onehot = [sb(f"onehot{k}", [P, B, E], F32) for k in range(TOP)]
        rest = sb("rest", [P, B, E], F32)
        ratio = sb("ratio", [P, B], F32)
        step, gone, exp_done, rev_done = sem("step"), sem("gone"), sem("exp_done"), sem("rev_done")
        if tokens_sorted:
            n_dram, place, slot_token, tile_expert = (tokens_sorted[k] for k in ("slots", "place", "slot_token", "tile_expert"))
            NT = tokens_sorted["tiles"]
            ones_tri = sb("ones_tri", [P, P], F32)
            both = sb("both", [P, B, E], F32)
            before = sb("before", [P, E, B], F32)
            carry = sb("carry", [P, E, B + 1], F32)
            zero = sb("zero", [P, B + 1], F32)
            padded = sb("padded", [P, E], F32)
            padded_i = sb("padded_i", [P, E], I32)
            base = sb("base", [P, E + 1], F32)
            posf = sb("posf", [P, B, E], F32)
            token = sb("token", [P, B], I32)
            slot = sb("slot", [P, TOP, B], U32)
            slot_now = sb("slot_now", [P, TOP, 4], U32)
            token_now = sb("token_now", [P, 4], I32)
            taken, scatter_passed = sem("taken"), sem("scatter_passed")
            row = sb("row", [P, B], I32)
            rowf = sb("rowf", [P, B], F32)
            zeros_i = sb("zeros_i", [P, NT], I32)
            tile_row = sb("tile_row", [1, NT], F32)
            tile_sum = sb("tile_sum", [1, NT], F32)
            tile_ge = sb("tile_ge", [1, NT], F32)
            PR = es.enter_context(nc.psum_tensor(f"{name}_PR", [P, B * E], F32))
            PC = es.enter_context(nc.psum_tensor(f"{name}_PC", [P, B * E], F32))
            tri_done, ranks_ready, cleared, scattered, listed = (
                sem("tri_done"), sem("ranks_ready"), sem("cleared"), sem("scattered"), sem("listed"))

        def wide(v):
            return v.rearrange("p (b o) -> p b o", o=1).to_broadcast([P, B, E])

        with nc.Block() as block:

            @block.vector
            def _(dve):
                n = 0

                def then(instruction):
                    nonlocal n
                    n += 1
                    instruction.then_inc(step, 1)
                    dve.wait_ge(step, n)

                dve.wait_ge(rev_done, 1)
                scores = logits
                for k in range(TOP):
                    then(dve.tensor_reduce(best[:, k, :], scores[:, :, :], AX.X, ALU.max))
                    then(dve.tensor_tensor(eq[:, :, :], scores[:, :, :], wide(best[:, k, :]), ALU.is_equal))
                    then(dve.tensor_tensor(eq[:, :, :], eq[:, :, :], rev[:, :, :], ALU.mult))
                    then(dve.tensor_reduce(pick[:, k, :], eq[:, :, :], AX.X, ALU.max))
                    then(dve.tensor_tensor(onehot[k][:, :, :], eq[:, :, :], wide(pick[:, k, :]), ALU.is_equal))
                    if k == 0:
                        then(dve.scalar_tensor_tensor(rest[:, :, :].rearrange("p b e -> p (b e)"), onehot[0][:, :, :].rearrange("p b e -> p (b e)"), BELOW_ALL,
                                                      logits[:, :, :].rearrange("p b e -> p (b e)"), ALU.mult, ALU.add))
                        scores = rest
                dve.tensor_tensor(ratio[:, :], best[:, 1, :], best[:, 0, :], ALU.subtract).then_inc(gone, 1)
                dve.wait_ge(exp_done, 1)
                then(dve.tensor_scalar(best[:, 0, :], ratio[:, :], 1.0, None, ALU.add))
                then(dve.reciprocal(best[:, 1, :], best[:, 0, :]))
                then(dve.tensor_copy(weights[:, :, 0:1].rearrange("p b o -> p (b o)"), best[:, 1, :]))
                then(dve.tensor_tensor(weights[:, :, 1:2].rearrange("p b o -> p (b o)"), best[:, 1, :], ratio[:, :], ALU.mult))
                if not tokens_sorted:
                    for k in range(TOP):
                        then(dve.tensor_scalar(experts[0:1, :].rearrange("p (b k) -> p b k", k=TOP)[:, :, k], pick[0:1, k, :], -1.0, float(E), ALU.mult, ALU.add))
                    return
                then(dve.tensor_tensor(both[:, :, :], onehot[0][:, :, :], onehot[1][:, :, :], ALU.add))
                dve.sem_inc(gone, 1)
                then(dve.memset(zero[:, :], 0.0))
                then(dve.memset(carry[:, :, 0:1], 0.0))
                then(dve.memset(base[:, 0:1], float(tokens_sorted["first_slot"])))
                dve.wait_ge(ranks_ready, 2)
                for e in range(E):
                    then(dve.tensor_tensor_scan(carry[:, e, 1:B + 1], PC[:, :].rearrange("p (b e) -> p e b", e=E)[:, e, :], zero[:, 1:B + 1], 0.0, ALU.add, ALU.add))
                then(dve.tensor_scalar(padded_i[:, :], carry[:, :, B:B + 1].rearrange("p e o -> p (e o)"), float(P - 1), None, ALU.add))
                then(dve.tensor_scalar(padded_i[:, :], padded_i[:, :], 7, 7, ALU.logical_shift_right, ALU.logical_shift_left))
                then(dve.tensor_copy(padded[:, :], padded_i[:, :]))
                for e in range(E):
                    then(dve.tensor_tensor(base[:, e + 1:e + 2], base[:, e:e + 1], padded[:, e:e + 1], ALU.add))
                then(dve.tensor_tensor(posf[:, :, :], PR[:, :].rearrange("p (b e) -> p b e", e=E), carry[:, :, 0:B].rearrange("p e b -> p b e"), ALU.add))
                then(dve.tensor_tensor(posf[:, :, :], posf[:, :, :], base[:, 0:E].rearrange("p (o e) -> p o e", o=1).to_broadcast([P, B, E]), ALU.add))
                for k in range(TOP):
                    then(dve.tensor_tensor(onehot[k][:, :, :], onehot[k][:, :, :], posf[:, :, :], ALU.mult))
                    then(dve.tensor_reduce(pick[:, k, :], onehot[k][:, :, :], AX.X, ALU.add))
                    then(dve.tensor_copy(place[:, k, :], pick[:, k, :]))
                    then(dve.tensor_scalar(row[:, :], place[:, k, :].bitcast(I32), P - 1, None, ALU.bitwise_and))
                    then(dve.tensor_copy(rowf[:, :], row[:, :]))
                    then(dve.tensor_tensor(pick[:, k, :], pick[:, k, :], rowf[:, :], ALU.subtract))
                    then(dve.tensor_scalar(pick[:, k, :], pick[:, k, :], 1.0 / P, None, ALU.mult))
                    then(dve.scalar_tensor_tensor(pick[:, k, :], rowf[:, :], float(NT), pick[:, k, :], ALU.mult, ALU.add))
                    then(dve.tensor_copy(slot[:, k, :], pick[:, k, :]))
                dve.sem_inc(gone, 1)
                dve.wait_ge(rev_done, 2)
                then(dve.memset(tile_sum[:, :], 0.0))
                for e in range(1, E + 1):
                    then(dve.tensor_scalar(tile_ge[:, :], tile_row[:, :], base[0:1, e:e + 1], None, ALU.is_ge))
                    then(dve.tensor_tensor(tile_sum[:, :], tile_sum[:, :], tile_ge[:, :], ALU.add))
                then(dve.tensor_scalar(tile_sum[:, :], tile_sum[:, :], float(E - 1), None, ALU.min))
                first = tokens_sorted["first_slot"] // P
                then(dve.tensor_copy(tile_expert[0:1, :], tile_sum[:, :]))
                then(dve.memset(tile_sum[:, 0:first], float(E)))
                then(dve.tensor_copy(tile_expert[0:1, 0:first], tile_sum[:, 0:first]))

            @block.scalar
            def _(act):
                act.wait_ge(gone, 1)
                act.activation(ratio[:, :], ratio[:, :], ACT.Exp).then_inc(exp_done, 1)

            @block.gpsimd
            def _(pool):
                pool.iota(rev[:, :, :], [[0, B], [-1, E]], base=E, channel_multiplier=0, allow_small_or_imprecise_dtypes=True).then_inc(rev_done, 1)
                if not tokens_sorted:
                    return
                pool.wait_ge(rev_done, 1)
                pool.iota(tile_row[:, :], [[P, NT]], base=0, channel_multiplier=0, allow_small_or_imprecise_dtypes=True).then_inc(rev_done, 1)
                pool.wait_ge(rev_done, 2)
                pool.memset(ones_tri[:, :], 1.0).then_inc(tri_done, 1)
                pool.wait_ge(tri_done, 1)
                pool.affine_select(out=ones_tri[:, :], in_=ones_tri[:, :], compare_op=ALU.is_gt, fill=0.0, base=0, pattern=[[1, P]], channel_multiplier=-1).then_inc(tri_done, 1)
                pool.iota(token[:, :], [[P, B]], base=0, channel_multiplier=1).then_inc(tri_done, 1)
                pool.memset(zeros_i[:, :], 0).then_inc(tri_done, 1)
                pool.wait_ge(tri_done, 4)
                first = tokens_sorted["first_slot"] // P
                pool.dma_start(n_dram[:, 0:first], token[:, 0:first]).then_inc(cleared, 16)
                pool.dma_start(n_dram[:, first:NT], zeros_i[:, first:NT]).then_inc(cleared, 16)
                pool.wait_ge(cleared, 32)
                pool.wait_ge(gone, 3)
                flat = n_dram.rearrange("p (b o) -> (p b) o", o=1)
                def scatter(turn, first):
                    if not first:
                        wait_apart(pool, scattered, 16 * 4 * TOP * turn, scatter_passed)
                    for k in range(TOP):
                        pool.tensor_copy(slot_now[:, k, :], slot[:, k, bass.ds(4 * turn, 4)]).then_inc(taken, 1)
                    pool.tensor_copy(token_now[:, :], token[:, bass.ds(4 * turn, 4)]).then_inc(taken, 1)
                    wait_apart(pool, taken, 3 * turn + 3, scatter_passed)
                    for k in range(TOP):
                        for b in range(4):
                            pool.indirect_dma_start(flat, bass.IndirectOffsetOnAxis(ap=slot_now[:, k, b:b + 1], axis=0), token_now[:, b:b + 1], None).then_inc(scattered, 16)

                scatter(0, True)
                with pool.Fori(1, B // 4) as turn:
                    scatter(turn, False)
                pool.wait_ge(scattered, 16 * B * TOP)
                pool.dma_start(slot_token[:, :], n_dram[:, :]).then_inc(listed, 16)
                pool.wait_ge(listed, 16)

            if tokens_sorted:
                @block.tensor
                def _(pe):
                    pe.wait_ge(tri_done, 2)
                    pe.wait_ge(gone, 2)
                    v = both[:, :, :].rearrange("p b e -> p (b e)")
                    pe.matmul(PR[:, :], ones_tri[:, :], v, start=True, stop=True).then_inc(ranks_ready, 1)
                    pe.matmul(PC[:, :], tokens_sorted["ones"][:, :], v, start=True, stop=True).then_inc(ranks_ready, 1)
        clear_semaphores(nc, sems)


def experts_phase(nc, name, rows, gather, tile_expert, weights, y_dst, n_tiles, ident):
    NE = len(weights)
    with ExitStack() as es:
        def sb(n, shape, dt):
            return es.enter_context(nc.sbuf_tensor(f"{name}_{n}", shape, dt))

        def ps(n, shape, dt):
            return es.enter_context(nc.psum_tensor(f"{name}_{n}", shape, dt))

        sems = []

        def sem(n):
            sems.append(nc.alloc_semaphore(name=f"{name}_{n}"))
            return sems[-1]

        w32 = sb("w32", [P, 2, KC * F], F32)
        wu_hi = sb("wu_hi", [P, NE, KC, F], F32R)
        wu_lo = sb("wu_lo", [P, NE, KC, F], F32R)
        wd_hi = sb("wd_hi", [P, NE, FC, D], F32R)
        wd_lo = sb("wd_lo", [P, NE, FC, D], F32R)
        x_in = sb("x_in", [P, 4, D], F32)
        xT_hi = sb("xT_hi", [P, 2, KC, P], F32R)
        xT_lo = sb("xT_lo", [P, 2, KC, P], F32R)
        hid = sb("hid", [P, 2, F], F32)
        hT_hi = sb("hT_hi", [P, 2, FC, P], F32R)
        hT_lo = sb("hT_lo", [P, 2, FC, P], F32R)
        y_out = sb("y_out", [P, 4, D], F32)
        gather_now = sb("gather_now", [P, 4], U32)
        taken = sem("taken")
        PX = [ps(f"PX{k}", [P, T], F32) for k in range(2)]
        PH = [ps(f"PH{k}", [P, F], F32) for k in range(2)]
        PT = [ps(f"PT{k}", [P, F], F32) for k in range(2)]
        PY = [ps(f"PY{k}", [P, T], F32) for k in range(2)]
        w_loaded = [sem(f"w_loaded{k}") for k in range(2)]
        w_hi_done, w_lo_done = sem("w_hi_done"), sem("w_lo_done")
        x_loaded = [sem(f"x_loaded{k}") for k in range(4)]
        xT_ready, xT_hi_done, xT_lo_done = sem("xT_ready"), sem("xT_hi_done"), sem("xT_lo_done")
        h_ready, gelu_done, hT_ready, hT_hi_done, hT_lo_done = (
            sem("h_ready"), sem("gelu_done"), sem("hT_ready"), sem("hT_hi_done"), sem("hT_lo_done"))
        y_ready, y_copied = sem("y_ready"), sem("y_copied")
        y_stored = [sem(f"y_stored{k}") for k in range(4)]
        passed, pe_passed = sem("passed"), sem("pe_passed")
        STEP0, LOOP0, PER = -3, 6, 4
        turns = (n_tiles - 4 - LOOP0) // PER
        LOOP1 = LOOP0 + PER * turns

        def run(eng, program):
            for i in range(STEP0, LOOP0):
                program(i, None)
            with eng.Fori(0, turns) as turn:
                for i in range(LOOP0, LOOP0 + PER):
                    program(i, turn)
            for i in range(LOOP1, n_tiles + 4):
                program(i, None)

        def done(i, turn, per=1, c=0):
            return at(i, per * PER, turn, per * (i + 1) + c)

        def ring4(i, turn):
            return at(i, 16, turn, 16 * (i // 4 + 1))

        def valid(i, turn):
            return turn is not None or 0 <= i < n_tiles

        def off(turn):
            return 0 if turn is None else PER * turn

        with nc.Block() as block:

            @block.sync
            def _(sp):
                for q, w in enumerate([w for pair in weights for w in pair]):
                    if q >= 2:
                        sp.wait_ge(w_lo_done, q - 1)
                    c = KC if q % 2 == 0 else FC
                    sp.dma_start(w32[:, q % 2, :].rearrange("p (c n) -> p c n", c=c), w.rearrange("(c p) n -> p c n", p=P)).then_inc(w_loaded[q % 2], 16)

                def program(i, turn):
                    if gather is None and valid(i + 3, turn):
                        wait_apart(sp, xT_ready, done(i - 1, turn), passed)
                        b = (i + 3) // TOP
                        sp.dma_start(x_in[:, (i + 3) % 4, :], rows[bass.ds(b + (0 if turn is None else PER // TOP * turn), 1)].rearrange("b t d -> t (b d)")
                                     ).then_inc(x_loaded[(i + 3) % 4], 16)
                    if valid(i - 3, turn):
                        wait_apart(sp, y_copied, done(i - 3, turn), passed)
                        sp.dma_start(y_dst[bass.ds(i - 3 + off(turn), 1)].rearrange("b t d -> t (b d)"), y_out[:, (i - 3) % 4, :]).then_inc(y_stored[(i - 3) % 4], 16)

                run(sp, program)
                for k in range(4):
                    sp.wait_ge(y_stored[k], 16 * (n_tiles // 4))

            if gather is not None:
                @block.gpsimd
                def _(pool):
                    def program(i, turn):
                        if valid(i + 3, turn):
                            wait_apart(pool, xT_ready, done(i - 1, turn), passed)
                            k = (i + 3) % 4
                            pool.tensor_copy(gather_now[:, k:k + 1], gather[:, bass.ds(i + 3 + off(turn), 1)]).then_inc(taken, 1)
                            wait_apart(pool, taken, done(i + 3, turn), passed)
                            pool.indirect_dma_start(x_in[:, k, :], None, rows.rearrange("b t d -> (b t) d"),
                                                    bass.IndirectOffsetOnAxis(ap=gather_now[:, k:k + 1], axis=0)).then_inc(x_loaded[k], 16)

                    run(pool, program)

            @block.tensor
            def _(pe):
                pe.wait_ge(w_lo_done, 2 * NE)

                def expert(i, turn):
                    return pe.value_load(tile_expert[0:1, bass.ds(i + off(turn), 1)], min_val=0, max_val=NE - 1)

                def program(i, turn):
                    if valid(i, turn):
                        wait(pe, xT_lo_done, done(i, turn))
                        wait_apart(pe, gelu_done, done(i - 2, turn), pe_passed)
                        e = expert(i, turn)
                        for c in range(KC):
                            for z, (a, w) in enumerate(((xT_hi, wu_hi), (xT_hi, wu_lo), (xT_lo, wu_hi))):
                                last = pe.matmul(PH[i % 2][:, :], a[:, i % 2, c, :], w[:, bass.ds(e, 1), c, :].rearrange("p o n -> p (o n)"),
                                                 start=(c == 0 and z == 0), stop=(c == KC - 1 and z == 2))
                        last.then_inc(h_ready, 1)
                    if valid(i - 1, turn):
                        wait(pe, gelu_done, done(i - 1, turn))
                        wait(pe, hT_lo_done, done(i - 3, turn))
                        for c in range(FC):
                            last = pe.transpose(PT[(i - 1) % 2][:, c * P:(c + 1) * P], hid[:, (i - 1) % 2, c * P:(c + 1) * P], ident[:, :])
                        last.then_inc(hT_ready, 1)
                    if valid(i - 2, turn):
                        k = i % 2
                        wait(pe, hT_lo_done, done(i - 2, turn))
                        wait_apart(pe, y_copied, done(i - 4, turn), pe_passed)
                        e = expert(i - 2, turn)
                        for c in range(FC):
                            for z, (a, w) in enumerate(((hT_hi, wd_hi), (hT_hi, wd_lo), (hT_lo, wd_hi))):
                                last = pe.matmul(PY[k][:, 0:D], a[:, k, c, :], w[:, bass.ds(e, 1), c, :].rearrange("p o n -> p (o n)"),
                                                 start=(c == 0 and z == 0), stop=(c == FC - 1 and z == 2))
                        last.then_inc(y_ready, 1)
                    if valid(i + 1, turn):
                        k = (i + 1) % 2
                        wait(pe, x_loaded[(i + 1) % 4], ring4(i + 1, turn))
                        wait(pe, xT_lo_done, done(i - 1, turn))
                        for c in range(KC):
                            last = pe.transpose(PX[k][:, c * P:(c + 1) * P], x_in[:, (i + 1) % 4, c * P:(c + 1) * P], ident[:, :])
                        last.then_inc(xT_ready, 1)

                run(pe, program)

            @block.scalar
            def _(act):
                for q in range(2 * NE):
                    act.wait_ge(w_loaded[q % 2], 16 * (q // 2 + 1))
                    w = (wu_hi if q % 2 == 0 else wd_hi)[:, q // 2, :, :].rearrange("p c n -> p (c n)")
                    act.activation(w, w32[:, q % 2, :], ACT.Copy).then_inc(w_hi_done, 1)

                def program(i, turn):
                    if valid(i, turn):
                        wait(act, hT_ready, done(i - 2, turn))
                        wait(act, h_ready, done(i, turn))
                        act.activation(hid[:, i % 2, :], PH[i % 2][:, :], ACT.Gelu).then_inc(gelu_done, 1)
                    if valid(i - 1, turn):
                        k = (i - 1) % 2
                        wait(act, hT_ready, done(i - 1, turn))
                        wait(act, y_ready, done(i - 3, turn))
                        act.activation(hT_hi[:, k, :, :].rearrange("p c t -> p (c t)"), PT[k][:, :], ACT.Copy).then_inc(hT_hi_done, 1)
                    if valid(i + 1, turn):
                        k = (i + 1) % 2
                        wait(act, xT_ready, done(i + 1, turn))
                        wait(act, h_ready, done(i - 1, turn))
                        act.activation(xT_hi[:, k, :, :].rearrange("p c t -> p (c t)"), PX[k][:, 0:D], ACT.Copy).then_inc(xT_hi_done, 1)

                run(act, program)

            @block.vector
            def _(dve):
                for q in range(2 * NE):
                    dve.wait_ge(w_hi_done, q + 1)
                    hi, lo = ((wu_hi, wu_lo) if q % 2 == 0 else (wd_hi, wd_lo))
                    dve.tensor_tensor(lo[:, q // 2, :, :].rearrange("p c n -> p (c n)"), w32[:, q % 2, :],
                                      hi[:, q // 2, :, :].rearrange("p c n -> p (c n)"), ALU.subtract).then_inc(w_lo_done, 1)

                def program(i, turn):
                    if valid(i - 1, turn):
                        k = (i - 1) % 2
                        wait(dve, hT_hi_done, done(i - 1, turn))
                        dve.tensor_tensor(hT_lo[:, k, :, :].rearrange("p c t -> p (c t)"), PT[k][:, :], hT_hi[:, k, :, :].rearrange("p c t -> p (c t)"),
                                          ALU.subtract).then_inc(hT_lo_done, 1)
                    if valid(i - 2, turn):
                        wait(dve, y_ready, done(i - 2, turn))
                        wait(dve, y_stored[(i - 2) % 4], at(i, 16, turn, 16 * ((i - 2) // 4)))
                        dve.tensor_copy(y_out[:, (i - 2) % 4, :], PY[i % 2][:, 0:D]).then_inc(y_copied, 1)
                    if valid(i + 1, turn):
                        k = (i + 1) % 2
                        wait(dve, xT_hi_done, done(i + 1, turn))
                        dve.tensor_tensor(xT_lo[:, k, :, :].rearrange("p c t -> p (c t)"), PX[k][:, 0:D], xT_hi[:, k, :, :].rearrange("p c t -> p (c t)"),
                                          ALU.subtract).then_inc(xT_lo_done, 1)

                run(dve, program)
        clear_semaphores(nc, sems)


def combine_phase(nc, name, src, added_rows, y, dst, weights, place, B):
    with ExitStack() as es:
        def sb(n, shape, dt):
            return es.enter_context(nc.sbuf_tensor(f"{name}_{n}", shape, dt))

        sems = []

        def sem(n):
            sems.append(nc.alloc_semaphore(name=f"{name}_{n}"))
            return sems[-1]

        R4 = 4
        x = sb("x", [P, R4, D], F32)
        ysh = sb("ysh", [P, R4, D], F32)
        yk = sb("yk", [P, R4, TOP, D], F32)
        out = sb("out", [P, R4, D], F32)
        loaded = [sem(f"loaded{k}") for k in range(R4)]
        gathered = [sem(f"gathered{k}") for k in range(R4)]
        summed, added = sem("summed"), sem("added")
        stored = [sem(f"stored{k}") for k in range(R4)]
        passed = sem("passed")
        place_now = sb("place_now", [P, R4, TOP], U32)
        taken = sem("taken")
        NTURN = B // R4

        with nc.Block() as block:

            @block.sync
            def _(sp):
                def load(b, k):
                    sp.dma_start(x[:, k, :], src[bass.ds(b, 1)].rearrange("b t d -> t (b d)")).then_inc(loaded[k], 16)
                    sp.dma_start(ysh[:, k, :], added_rows[bass.ds(b, 1)].rearrange("b t d -> t (b d)")).then_inc(loaded[k], 16)
                    if place is None:
                        sp.dma_start(yk[:, k, :, :], y[bass.ds(b * TOP, TOP)].rearrange("b t d -> t b d")).then_inc(loaded[k], 16)

                def store(b, k, turn):
                    wait_apart(sp, added, R4 * turn + k + 1, passed)
                    sp.dma_start(dst[bass.ds(b, 1)].rearrange("b t d -> t (b d)"), out[:, k, :]).then_inc(stored[k], 16)

                for k in range(R4):
                    load(k, k)
                with sp.Fori(0, NTURN - 1) as turn:
                    for k in range(R4):
                        store(R4 * turn + k, k, turn)
                        load(R4 * turn + k + R4, k)
                for k in range(R4):
                    store(B - R4 + k, k, NTURN - 1)
                for k in range(R4):
                    sp.wait_ge(stored[k], 16 * NTURN)

            if place is not None:
                @block.gpsimd
                def _(pool):
                    flat = y.rearrange("b t d -> (b t) d")

                    def gather(b, k):
                        for q in range(TOP):
                            pool.tensor_copy(place_now[:, k, q:q + 1], place[:, q, bass.ds(b, 1)]).then_inc(taken, 1)
                        wait_apart(pool, taken, TOP * (b + 1), passed)
                        for q in range(TOP):
                            pool.indirect_dma_start(yk[:, k, q, :], None, flat, bass.IndirectOffsetOnAxis(ap=place_now[:, k, q:q + 1], axis=0)).then_inc(gathered[k], 16)

                    for k in range(R4):
                        gather(k, k)
                    with pool.Fori(0, NTURN - 1) as turn:
                        for k in range(R4):
                            wait_apart(pool, added, R4 * turn + k + 1, passed)
                            gather(R4 * turn + k + R4, k)

            @block.vector
            def _(dve):
                def add(turn, k, first):
                    dve.wait_ge(loaded[k], (32 if place is not None else 48) * (turn + 1))
                    if place is not None:
                        dve.wait_ge(gathered[k], 32 * (turn + 1))
                    if not first:
                        dve.wait_ge(stored[k], 16 * turn)
                    b = R4 * turn + k
                    dve.tensor_tensor(out[:, k, :], x[:, k, :], ysh[:, k, :], ALU.add).then_inc(summed, 1)
                    dve.wait_ge(summed, TOP * b + 1)
                    for q in range(TOP):
                        dve.scalar_tensor_tensor(out[:, k, :], yk[:, k, q, :], weights[:, bass.ds(b, 1), q:q + 1].rearrange("p o n -> p (o n)"), out[:, k, :], ALU.mult, ALU.add
                                                 ).then_inc(summed if q < TOP - 1 else added, 1)
                        if q < TOP - 1:
                            dve.wait_ge(summed, TOP * (b + 1))

                for k in range(R4):
                    add(0, k, True)
                with dve.Fori(1, NTURN) as turn:
                    for k in range(R4):
                        add(turn, k, False)
        clear_semaphores(nc, sems)


def program(nc, t, B):
    def scratch(n, shape, dt=F32):
        return nc.dram_tensor(n, shape, dt, kind="Internal").ap()

    x1, x2, x3, x4 = (scratch(f"x{k}_scratch", (B, P, D)) for k in range(1, 5))
    x3_normed = scratch("x3_normed_scratch", (B, P, D))
    normed = scratch("normed_scratch", (B, P, D))
    list_tiles = B * TOP + E
    n_tiles = B + list_tiles
    y_rows = scratch("expert_rows_scratch", (n_tiles, P, D))
    slots = scratch("slots_scratch", (P, n_tiles), U32)

    with ExitStack() as es:
        ident = es.enter_context(nc.sbuf_tensor("ident", [P, P], F32))
        identb = es.enter_context(nc.sbuf_tensor("identb", [P, P], BF16))
        ones = es.enter_context(nc.sbuf_tensor("ones", [P, P], F32))
        const_done = es.enter_context(nc.semaphore("const_done"))
        with nc.Block() as block:
            @block.gpsimd
            def _(pool):
                pool.memset(ident[:, :], 0.0).then_inc(const_done, 1)
                pool.wait_ge(const_done, 1)
                pool.affine_select(out=ident[:, :], in_=ident[:, :], compare_op=ALU.not_equal, fill=1.0, base=0, pattern=[[-1, P]],
                                   channel_multiplier=1).then_inc(const_done, 1)
                pool.wait_ge(const_done, 2)
                pool.tensor_copy(identb[:, :], ident[:, :]).then_inc(const_done, 1)
                pool.memset(ones[:, :], 1.0).then_inc(const_done, 1)

        attention_phase(nc, "xattn0", t["x"], t["ctx"], x1, [t["attn0"]], None, ident, identb, B)
        with ExitStack() as moe:
            logits = moe.enter_context(nc.sbuf_tensor("logits0", [P, B, E], F32))
            weights = moe.enter_context(nc.sbuf_tensor("weights0", [P, B, TOP], F32))
            place = moe.enter_context(nc.sbuf_tensor("place0", [P, TOP, B], U32))
            slot_token = moe.enter_context(nc.sbuf_tensor("slot_token0", [P, n_tiles], U32))
            tile_expert = moe.enter_context(nc.sbuf_tensor("tile_expert0", [1, n_tiles], I32))
            route_phase(nc, "route0", x1, normed, True, t["Wg"], None, None, None, logits, ident, ones, B)
            top_two_phase(nc, "top0", logits, weights, None, dict(
                slots=slots, place=place, slot_token=slot_token, tile_expert=tile_expert, tiles=n_tiles, first_slot=B * P, ones=ones), B)
            experts_phase(nc, "experts0", normed, slot_token, tile_expert,
                          [(t["Wu"][e], t["Wd"][e]) for e in range(E)] + [(t["W1"], t["W2"])], y_rows, n_tiles, ident)
            combine_phase(nc, "combine0", x1, y_rows[0:B], y_rows, x2, weights, place, B)

        attention_phase(nc, "xattn1", x2, t["ctx"], x3, [t["attn1"]], None, ident, identb, B)
        route_phase(nc, "norm1", x3, x3_normed, True, None, None, None, None, None, ident, ones, B)
        attention_phase(nc, "mha", x3_normed, None, x4, [t["mha0"], t["mha1"]], t["router1"], ident, identb, B)
        with ExitStack() as moe:
            logits = moe.enter_context(nc.sbuf_tensor("logits1", [P, B, E], F32))
            weights = moe.enter_context(nc.sbuf_tensor("weights1", [P, B, TOP], F32))
            tile_expert = moe.enter_context(nc.sbuf_tensor("tile_expert1", [1, B * TOP], I32))
            route_phase(nc, "route1", x4, normed, False, t["ffn_rw"], t["ffn_rb"], t["ln2_g"], t["ln2_b"], logits, ident, ones, B)
            top_two_phase(nc, "top1", logits, weights, tile_expert, None, B)
            experts_phase(nc, "experts1", normed, None, tile_expert, [(t["fw1"][e], t["fw2"][e]) for e in range(E)], y_rows, B * TOP, ident)
            combine_phase(nc, "combine1", x4, x3, y_rows, t["out"], weights, None, B)


def kernel(**inputs):
    import numpy as np
    import concourse.bacc as bacc
    from concourse.bass_utils import run_bass_kernel_spmd

    a = {k: np.asarray(v) for k, v in inputs.items()}
    B = a["x"].shape[0]

    def headwise(w):
        return w.reshape(D, KC, P // HD, HD).transpose(0, 1, 3, 2).reshape(D, D)

    def headwise_bias(b):
        return b.reshape(KC, P // HD, HD).transpose(2, 1, 0).reshape(P, KC)

    def column(v):
        return v.reshape(KC, P).T

    def unit(name, wq, wk, wv, wo, bq, bk, bv, bo):
        return {f"{name}_wq": headwise(wq), f"{name}_wk": headwise(wk), f"{name}_wv": wv, f"{name}_wo": wo,
                f"{name}_bq": headwise_bias(bq), f"{name}_bk": headwise_bias(bk), f"{name}_bv": bv, f"{name}_bo": bo}

    w = {"x": a["x"], "ctx": a["ctx_1024"]}
    w.update(unit("attn0", a["L0_xattn_Wq"].T, a["L0_xattn_Wk"].T, a["L0_xattn_Wv"].T, a["L0_xattn_Wo"].T,
                  a["L0_xattn_bq"], a["L0_xattn_bk"], a["L0_xattn_bv"], a["L0_xattn_bo"]))
    proj, bias = a["L1_xattn_in_proj_w"], a["L1_xattn_in_proj_b"]
    w.update(unit("attn1", proj[:D].T, proj[D:2 * D].T, proj[2 * D:].T, a["L1_xattn_out_w"].T,
                  bias[:D], bias[D:2 * D], bias[2 * D:], a["L1_xattn_out_b"]))
    for m in range(2):
        w.update(unit(f"mha{m}", a["L1_ffn_mha_wq"][m].reshape(D, D), a["L1_ffn_mha_wk"][m].reshape(D, D),
                      a["L1_ffn_mha_wv"][m].reshape(D, D), a["L1_ffn_mha_wo"][m].reshape(D, D), a["L1_ffn_mha_bq"][m].reshape(D),
                      a["L1_ffn_mha_bk"][m].reshape(D), a["L1_ffn_mha_bv"][m].reshape(D), a["L1_ffn_mha_bo"][m]))
    for k in ("Wg", "Wu", "Wd", "W1", "W2"):
        w[k] = a["L0_ffn_" + k]
    w["ln1_g"], w["ln1_b"] = column(a["L1_ffn_ln1_g"]), column(a["L1_ffn_ln1_b"])
    for k in ("ln2_g", "ln2_b", "mha_rw", "mha_rb", "ffn_rw", "ffn_rb", "fw1", "fw2"):
        w[k] = a["L1_ffn_" + k]

    nc = bacc.Bacc("TRN2", target_bir_lowering=False, num_devices=1)
    arrays = {f"in_{k}": np.ascontiguousarray(v) for k, v in w.items()}
    t = {k: nc.dram_tensor(f"in_{k}", arrays[f"in_{k}"].shape, mybir.dt.from_np(arrays[f"in_{k}"].dtype), kind="ExternalInput").ap() for k in w}
    for u in ("attn0", "attn1", "mha0", "mha1"):
        t[u] = {k: t[f"{u}_{k}"] for k in ("wq", "wk", "wv", "wo", "bq", "bk", "bv", "bo")}
    t["router1"] = {"gamma": t["ln1_g"], "beta": t["ln1_b"], "rw": t["mha_rw"], "rb": t["mha_rb"]}
    t["out"] = nc.dram_tensor("out", (B, P, D), F32, kind="ExternalOutput").ap()
    program(nc, t, B)
    r = run_bass_kernel_spmd(nc, [arrays], core_ids=[0])
    return r.results[0]["out"]
```

```python
from contextlib import ExitStack

import concourse.bass as bass
from concourse import mybir

F32 = mybir.dt.float32
F32R = mybir.dt.float32r
BF16 = mybir.dt.bfloat16
I32 = mybir.dt.int32
ALU = mybir.AluOpType
ACT = mybir.ActivationFunctionType
AX = mybir.AxisListType

P = 128
D = 256
H = 16
HD = D // H
KC = D // P
G = 4
T = G * P
HB = 4
PARTS = 3
Q_SLOTS = (0, 1, 2, 0, 1, 0)
K_SLOTS = (0, 0, 0, 1, 1, 2)
ROWS = 16 * len(Q_SLOTS)
NEWTON = 3
GUESS = 0x5F3759DF
LOOP_FIRST = 5
BODY = 8


def at(step, per_body, turn, const):
    return const if turn is None else const + per_body * turn


def wait(eng, sem, value):
    if isinstance(value, int) and value <= 0:
        return
    eng.wait_ge(sem, value)


def wait_apart(eng, sem, value, passed):
    wait(eng, sem, value)
    eng.sem_inc(passed, 1)


def clear_semaphores(nc, sems):
    nc.all_engine_barrier()
    nc.clear_and_free_semaphores(sems)
    nc.all_engine_barrier()


def steps(eng, n_steps, first_step, loop_first, program):
    turns = (n_steps + first_step - loop_first) // BODY
    last_loop = loop_first + turns * BODY
    for i in range(first_step, loop_first):
        program(i, None)
    with eng.Fori(0, turns) as turn:
        for i in range(loop_first, loop_first + BODY):
            program(i, turn)
    for i in range(last_loop, n_steps + 4):
        program(i, None)


def attention_phase(nc, name, src, context, dst, units, router, ident, identb, B):
    U = len(units)
    NG = B // G
    NM = NG * U
    N = NM * G
    XR = 2 // U
    FILLS0 = [2, 3, 0, 1, 4, 5, 6, 7, 8, 9] if U == 1 else [0, 1, 4, 5, 6, 7, "R", 8, 9]
    FILLS1 = FILLS0 if U == 1 else [4, 5, 6, 7, 8, 9]
    FIRST_FILLS = [2, 3, 0, 1] if U == 1 else [2, 0, 1, 3]
    FPB = len(FILLS0) + len(FILLS1)
    GPB = 2 // U
    lead = U - 1
    first_step = -11 - lead
    loop_first = LOOP_FIRST - lead + (BODY if U == 2 else 0)

    def fidx(m, k):
        return FPB * (m // 2) + (len(FILLS0) if m % 2 else 0) + (FILLS1 if m % 2 else FILLS0).index(k)

    def has(m, k):
        return k in (FILLS1 if m % 2 else FILLS0)

    def v_slot(m):
        return 2 if has(m, "R") else 0

    es = ExitStack()
    with es:
        def sb(n, shape, dt):
            return es.enter_context(nc.sbuf_tensor(f"{name}_{n}", shape, dt))

        def ps(n, shape, dt):
            return es.enter_context(nc.psum_tensor(f"{name}_{n}", shape, dt))

        sems = []

        def sem(n):
            sems.append(nc.alloc_semaphore(name=f"{name}_{n}"))
            return sems[-1]

        w32 = sb("w32", [P, 4, KC, D], F32)
        whi = sb("whi", [P, U, 4, KC, D], F32R)
        wlo = sb("wlo", [P, U, 4, KC, D], F32R)
        bq = sb("bq", [P, U, KC], F32)
        bk = sb("bk", [P, U, KC], F32)
        bv = sb("bv", [P, U, 2, D], F32)
        bo = sb("bo", [P, U, D], F32)

        x_in = sb("x_in", [P, XR, G, D], F32)
        stats = sb("stats", [P, G, 6], F32)
        moments = sb("moments", [P, G, 2], F32)
        rstd = sb("rstd", [P, G], F32)
        var_eps = sb("var_eps", [P, G], F32)
        half_bits = sb("half_bits", [P, G], I32)
        square = sb("square", [P, G], F32)
        n_tok = sb("n_tok", [P, G, D], F32)
        nT_hi = sb("nT_hi", [P, KC, T], F32R)
        nT_lo = sb("nT_lo", [P, KC, T], F32R)
        if U == 1:
            ctx_in = sb("ctx_in", [P, 2, G, D], F32)
            cT_hi = sb("cT_hi", [P, KC, T], F32R)
            cT_lo = sb("cT_lo", [P, KC, T], F32R)
        else:
            cT_hi, cT_lo = nT_hi, nT_lo
            nT = sb("nT", [P, KC, T], F32)
            gamma = sb("gamma", [P, KC], F32)
            beta = sb("beta", [P, KC], F32)
            mean = sb("mean", [P, KC, G], F32)
            rw = sb("rw", [P, KC, U], F32)
            rb = sb("rb", [P, G, U], F32)
            logit = sb("logit", [P, G, U], F32)
            lmax = sb("lmax", [P, G], F32)
            lexp = sb("lexp", [P, G, U], F32)
            lsum = sb("lsum", [P, G], F32)
            p_new = sb("p_new", [P, G, U], F32)
            p_use = sb("p_use", [P, G, U], F32)
        parts = [sb("q_parts", [P, 2, KC, PARTS, T], BF16), sb("k_parts", [P, 2, KC, PARTS, T], BF16)]
        rest = sb("rest", [P, 2, T], F32)
        qs = sb("qs", [ROWS + PARTS, 2, H, T], BF16)
        ks = sb("ks", [ROWS + PARTS, 2, H, T], BF16)
        v_aug = sb("v_aug", [P, 2, G, H, 2 * HD], F32)
        nmax = sb("nmax", [P, 2, H], F32)
        mres = sb("mres", [P, 2, H], F32)
        mparts = sb("mparts", [P, 2, PARTS, H], BF16)
        mT = sb("mT", [PARTS * H, 2, P], BF16)
        probs = sb("probs", [P, 2, H, P], F32)
        o_un = sb("o_un", [P, H // HB, P], F32)
        o_rec = sb("o_rec", [P, H], F32)
        o_tok = sb("o_tok", [P, H, HD], F32)
        oT_hi = sb("oT_hi", [P, KC, P], F32R)
        oT_lo = sb("oT_lo", [P, KC, P], F32R)
        x_res = sb("x_res", [P, G, D], F32)
        y_bias = sb("y_bias", [P, D], F32)
        y_out = sb("y_out", [P, 2, D], F32)

        S = [ps(f"S{j}", [P, HB, P], F32) for j in range(2)]
        ST = [ps(f"ST{j}", [P, HB * P], F32) for j in range(2)]
        PO = ps("PO", [P, H // HB, P], F32)
        X = ps("X", [P, T], F32)
        R = [ps(f"R{j}", [P, T], F32) for j in range(2)]

        w_loaded = [sem(f"w_loaded{u}") for u in range(U)]
        b_loaded = sem("b_loaded")
        w_hi_done, w_lo_done, ones_done = sem("w_hi_done"), sem("w_lo_done"), sem("ones_done")
        x_loaded = [sem(f"x_loaded{k}") for k in range(XR)]
        ctx_loaded = [sem(f"ctx_loaded{k}") for k in range(2)]
        xr_loaded = [sem(f"xr_loaded{b}") for b in range(G)]
        ln_stats, ln_moments, ln_guess, newton_done, n_ready = sem("ln_stats"), sem("ln_moments"), sem("ln_guess"), sem("newton_done"), sem("n_ready")
        fill_ready, fill_freed = sem("fill_ready"), sem("fill_freed")
        xT_hi_done, xT_lo_done = sem("xT_hi_done"), sem("xT_lo_done")
        part1_done, part2_done, part3_done = sem("part1_done"), sem("part2_done"), sem("part3_done")
        stacked = [[sem(f"stacked{k}{f}") for f in range(2)] for k in range(2)]
        s_ready, max_done, mpart_done, mT_ready, mT_done = (
            sem("s_ready"), sem("max_done"), sem("mpart_done"), sem("mT_ready"), sem("mT_done"))
        negmax_stacked = [sem(f"negmax_stacked{k}") for k in range(2)]
        st_ready, exp_done, pv_done, o_un_done = sem("st_ready"), sem("exp_done"), sem("pv_done"), sem("o_un_done")
        o_turned, o_rec_done, o_tok_done, oT_ready, oT_hi_done, oT_lo_done = (
            sem("o_turned"), sem("o_rec_done"), sem("o_tok_done"), sem("oT_ready"), sem("oT_hi_done"), sem("oT_lo_done"))
        y_ready, y_bias_done, y_done = sem("y_ready"), sem("y_bias_done"), sem("y_done")
        y_stored = [sem(f"y_stored{k}") for k in range(2)]
        sp_passed, pe_passed, dve_passed, pool_passed = sem("sp_passed"), sem("pe_passed"), sem("dve_passed"), sem("pool_passed")
        mean_done, rt_done, rt_exp_done, p_copied = sem("mean_done"), sem("rt_done"), sem("rt_exp_done"), sem("p_copied")

        W_IN = 16 * 4
        B_IN = 16 * (4 * U + (4 if U == 2 else 0))
        STACK = 16 * 2 * len(Q_SLOTS)

        def ub(per, i, turn, c=0):
            return at(i, per * BODY, turn, per * i + c)

        def gr(per, m, turn, c=0):
            return at(m, per * GPB, turn, per * (m // U + 1) + c)

        def fl(m, k, turn, c=0):
            return at(m, FPB, turn, fidx(m, k) + 1 + c)

        def ug_valid(m, turn):
            return turn is not None or 0 <= m < NM

        def ub_valid(i, turn):
            return turn is not None or 0 <= i < N

        def pos(turn, n):
            return 0 if turn is None else n * turn

        with nc.Block() as block:

            @block.sync
            def _(sp):
                for u, w in enumerate(units):
                    if u > 0:
                        sp.wait_ge(w_lo_done, u)
                    for k, key in enumerate(("wq", "wk", "wv", "wo")):
                        sp.dma_start(w32[:, k, :, :], w[key].rearrange("(c p) n -> p c n", p=P)).then_inc(w_loaded[u], 16)
                    sp.dma_start(bq[:, u, :], w["bq"]).then_inc(b_loaded, 16)
                    sp.dma_start(bk[:, u, :], w["bk"]).then_inc(b_loaded, 16)
                    sp.dma_start(bv[:, u, :, :], w["bv"].rearrange("(a b n) -> a b n", a=1, b=1).to_broadcast([P, 2, D])).then_inc(b_loaded, 16)
                    sp.dma_start(bo[:, u, :], w["bo"].rearrange("(a n) -> a n", a=1).to_broadcast([P, D])).then_inc(b_loaded, 16)
                if U == 2:
                    sp.dma_start(gamma[:, :], router["gamma"]).then_inc(b_loaded, 16)
                    sp.dma_start(beta[:, :], router["beta"]).then_inc(b_loaded, 16)
                    sp.dma_start(rw[:, :, :], router["rw"].rearrange("(c p) n -> p c n", p=P)).then_inc(b_loaded, 16)
                    sp.dma_start(rb[:, :, :], router["rb"].rearrange("(a b n) -> a b n", a=1, b=1).to_broadcast([P, G, U])).then_inc(b_loaded, 16)

                def program(i, turn):
                    if ub_valid(i + 1, turn):
                        k, b = (i + 1) // G % 2, (i + 1) % G
                        wait(sp, mT_done, ub(1, i + 2, turn))
                        sp.dma_start(qs[ROWS:ROWS + PARTS, k, :, b * P:(b + 1) * P], mT[:, (i + 1) % 2, :]).then_inc(negmax_stacked[(i + 1) % 2], 16)
                    m = (i + 11 + lead) // G
                    if (i + 11 + lead) % G == 0 and ug_valid(m, turn) and m % U == 0:
                        g = m // U
                        wait_apart(sp, n_ready, gr(G, m, turn, -G * XR), sp_passed)
                        sp.dma_start(x_in[:, g % XR, :, :], src[bass.ds(g * G + pos(turn, GPB * G), G)].rearrange("b t d -> t b d")).then_inc(x_loaded[g % XR], 16)
                        if U == 1:
                            if m >= 2:
                                wait_apart(sp, fill_ready, fl(m - 2, 3, turn), sp_passed)
                            sp.dma_start(ctx_in[:, m % 2, :, :], context[bass.ds(m * G + pos(turn, 2 * G), G)].rearrange("b t d -> t b d")).then_inc(ctx_loaded[m % 2], 16)
                    m, stage = (i + 5) // G, (i + 5) % G
                    if ug_valid(m, turn):
                        half, r = stage // 2, stage % 2
                        if m >= 2:
                            wait_apart(sp, st_ready, ub(4, 4 * m - 6 + 2 * half, turn), sp_passed)
                        wait(sp, part3_done, at(m, 8, turn, 4 * m + 2 * r + KC))
                        cols = slice(half * T // 2, (half + 1) * T // 2)
                        tile, slots = (qs, Q_SLOTS) if r == 0 else (ks, K_SLOTS)
                        for s, part in enumerate(slots):
                            sp.dma_start(tile[16 * s:16 * s + 16, m % 2, :, cols], parts[r][:, m % 2, :, part, cols]).then_inc(stacked[m % 2][half], 16)
                    if ub_valid(i, turn) and (i // G) % U == 0:
                        b, m = i % G, i // G
                        wait_apart(sp, y_done, ub(1, i - G + 1, turn), sp_passed)
                        sp.dma_start(x_res[:, b, :], src[bass.ds((m // U) * G + b + pos(turn, GPB * G), 1)].rearrange("b t d -> t (b d)")).then_inc(xr_loaded[b], 16)
                    if ub_valid(i - 3, turn) and ((i - 3) // G) % U == U - 1:
                        b, m = (i - 3) % G, (i - 3) // G
                        wait_apart(sp, y_done, ub(1, i - 2, turn), sp_passed)
                        sp.dma_start(dst[bass.ds((m // U) * G + b + pos(turn, GPB * G), 1)].rearrange("b t d -> t (b d)"), y_out[:, b % 2, :]).then_inc(y_stored[b % 2], 16)

                steps(sp, N, first_step, loop_first, program)
                for k in range(2):
                    sp.wait_ge(y_stored[k], 16 * B // 2)

            @block.tensor
            def _(pe):
                pe.wait_ge(w_lo_done, U)
                pe.wait_ge(ones_done, 2)

                def product(out, pairs, first=True):
                    n = 3 * len(pairs)
                    last = None
                    for q, ((ahi, alo), (bhi, blo)) in enumerate(pairs):
                        for z, (a, b_) in enumerate(((ahi, bhi), (ahi, blo), (alo, bhi))):
                            last = pe.matmul(out, a, b_, start=(q == 0 and z == 0), stop=(q == len(pairs) - 1 and z == 2))
                    return last

                def fill(m, k, turn):
                    if not ug_valid(m, turn) or not has(m, k):
                        return
                    u = m % U
                    f = fidx(m, k)
                    r = R[f % FPB % 2]
                    back = 1 if (U == 2 and f % FPB == 0) else 2
                    wait(pe, fill_freed, fl(m, k, turn, -back))
                    if k in (0, 1):
                        wait(pe, n_ready, gr(G, m, turn))
                        for b in range(G):
                            last = pe.transpose(r[:, b * P:(b + 1) * P], n_tok[:, b, k * P:(k + 1) * P], ident[:, :])
                    elif k in (2, 3):
                        wait(pe, ctx_loaded[m % 2], at(m, 16, turn, 16 * (m // 2 + 1)))
                        for b in range(G):
                            last = pe.transpose(r[:, b * P:(b + 1) * P], ctx_in[:, m % 2, b, (k - 2) * P:(k - 1) * P], ident[:, :])
                    elif k in (4, 5, 6, 7):
                        t, c = (k - 4) // 2, k % 2
                        if U == 1:
                            wait(pe, fill_freed, fl(m, 1, turn))
                        else:
                            wait(pe, xT_lo_done, gr(2, m, turn))
                        hi, lo = (nT_hi, nT_lo) if t == 0 else (cT_hi, cT_lo)
                        last = product(r[:, :], [((whi[:, u, t, kc, c * P:(c + 1) * P], wlo[:, u, t, kc, c * P:(c + 1) * P]),
                                                  (hi[:, kc, :], lo[:, kc, :])) for kc in range(KC)])
                    elif k == "R":
                        wait(pe, mean_done, gr(2, m, turn))
                        for b in range(G):
                            for kc in range(KC):
                                last = pe.matmul(r[:, b * U:(b + 1) * U], mean[:, kc, b:b + 1].to_broadcast([P, P]), rw[:, kc, :],
                                                 start=(kc == 0), stop=(kc == KC - 1))
                    else:
                        for j in range(2):
                            b = 2 * (k - 8) + j
                            last = product(r[:, j * D:(j + 1) * D], [((cT_hi[:, kc, b * P:(b + 1) * P], cT_lo[:, kc, b * P:(b + 1) * P]),
                                                                     (whi[:, u, 2, kc, :], wlo[:, u, 2, kc, :])) for kc in range(KC)])
                    last.then_inc(fill_ready, 1)

                def scores(i, j, turn):
                    k, b = i // G % 2, i % G
                    m = i // G
                    if b % 2 == 0 and j == 0:
                        wait(pe, stacked[k][b // 2], at(m, STACK, turn, STACK * (m // 2 + 1)))
                    wait(pe, max_done, ub(4, i, turn, j - 1))
                    for h in range(HB * j, HB * j + HB):
                        last = pe.matmul(S[j % 2][:, h % HB, :], qs[0:ROWS, k, h, b * P:(b + 1) * P], ks[0:ROWS, k, h, b * P:(b + 1) * P],
                                         start=True, stop=True)
                    last.then_inc(s_ready, 1)

                def scores_turned(i, j, turn):
                    k, b = i // G % 2, i % G
                    if j == 0:
                        wait(pe, negmax_stacked[i % 2], at(i, 16 * BODY // 2, turn, 16 * (i // 2 + 1)))
                    wait(pe, exp_done, ub(4, i, turn, j - 1))
                    for h in range(HB * j, HB * j + HB):
                        last = pe.matmul(ST[j % 2][:, (h % HB) * P:(h % HB + 1) * P], ks[:, k, h, b * P:(b + 1) * P], qs[:, k, h, b * P:(b + 1) * P],
                                         start=True, stop=True)
                    last.then_inc(st_ready, 1)

                def weigh(i, j, turn):
                    k, b, m = i // G % 2, i % G, i // G
                    if j == 0:
                        wait(pe, o_un_done, ub(1, i, turn))
                        wait(pe, fill_freed, fl(m, 8 + b // 2, turn))
                    wait(pe, exp_done, ub(4, i, turn, j + 1))
                    for q in range(HB):
                        h = HB * j + q
                        last = pe.matmul(PO[32 * q:32 * q + 32, j, :], v_aug[:, k, b, h, :], probs[:, i % 2, h, :], start=True, stop=True)
                    last.then_inc(pv_done, 1)

                def turn_normalised(i, turn):
                    d = i - 2
                    wait(pe, o_tok_done, ub(1, d + 1, turn))
                    if ub_valid(i + 1, turn):
                        wait(pe, mT_done, ub(1, i + 2, turn))
                    for c in range(KC):
                        last = pe.transpose(X[:, c * P:(c + 1) * P], o_tok[:, 8 * c:8 * c + 8, :].rearrange("p h d -> p (h d)"), ident[:, :])
                    last.then_inc(oT_ready, 1)

                def program(i, turn):
                    d = i - 2
                    m, r = (i + 7) // G, (i + 7) % G
                    for j in range(4):
                        if ub_valid(i + 2, turn):
                            scores(i + 2, j, turn)
                        if ub_valid(i, turn):
                            scores_turned(i, j, turn)
                        if j == 2 and ub_valid(d, turn) and r not in (1, 2):
                            turn_normalised(i, turn)
                        if j == 0 and ub_valid(d, turn):
                            wait(pe, o_un_done, ub(1, d + 1, turn))
                            if ub_valid(i, turn):
                                wait(pe, mT_done, ub(1, i + 1, turn))
                            wait(pe, y_bias_done, ub(1, d, turn))
                            for q in range(H // HB):
                                last = pe.transpose(X[:, q * P:(q + 1) * P], o_un[:, q, :], ident[:, :])
                            last.then_inc(o_turned, 1)
                        if j == 1 and ub_valid(i + 1, turn):
                            wait(pe, mpart_done, ub(4, i + 2, turn))
                            wait(pe, mT_done, ub(1, i + 1, turn))
                            wait_apart(pe, o_tok_done, ub(1, d + 1, turn), pe_passed)
                            pe.transpose(X[0:PARTS * H, 0:P // 2].bitcast(BF16), mparts[:, (i + 1) % 2, :, :].rearrange("p a h -> p (a h)"),
                                         identb[:, :]).then_inc(mT_ready, 1)
                        if ub_valid(i - 1, turn):
                            weigh(i - 1, j, turn)
                        if j == 2 and ub_valid(d, turn) and r in (1, 2):
                            turn_normalised(i, turn)
                        if r == 0:
                            if j == 0:
                                fill(m - 1, 9, turn)
                            fill(m, FIRST_FILLS[j], turn)
                        elif r in (1, 2) and j in (0, 2):
                            fill(m, 2 + 2 * r + j // 2, turn)
                        elif r == 3 and j == 0 and has(m, "R"):
                            fill(m, "R", turn)
                        elif r == 3 and j == v_slot(m):
                            fill(m, 8, turn)
                        if j == 3 and ub_valid(d, turn):
                            wait(pe, oT_lo_done, ub(1, d + 1, turn))
                            u = (d // G) % U
                            product(X[:, 0:D], [((oT_hi[:, kc, :], oT_lo[:, kc, :]), (whi[:, u, 3, kc, :], wlo[:, u, 3, kc, :]))
                                                for kc in range(KC)]).then_inc(y_ready, 1)

                steps(pe, N, first_step, loop_first, program)

            @block.scalar
            def _(act):
                for u in range(U):
                    act.wait_ge(w_loaded[u], W_IN)
                    act.activation(whi[:, u, :, :, :].rearrange("p k c n -> p (k c n)"), w32[:, :, :, :].rearrange("p k c n -> p (k c n)"),
                                   ACT.Copy).then_inc(w_hi_done, 1)
                act.wait_ge(b_loaded, B_IN)

                def fill_out(m, k, turn):
                    if not ug_valid(m, turn) or not has(m, k):
                        return
                    u = m % U
                    r = R[fidx(m, k) % FPB % 2]
                    if k in (0, 1, 2, 3):
                        if U == 1:
                            hi = nT_hi if k < 2 else cT_hi
                            wait(act, fill_ready, fl(m, k, turn))
                            act.activation(hi[:, k % 2, :], r[:, :], ACT.Copy).then_inc(xT_hi_done, 1)
                        else:
                            wait(act, fill_freed, fl(m, k, turn))
                            act.activation(nT_hi[:, k, :], nT[:, k, :], ACT.Copy).then_inc(xT_hi_done, 1)
                    elif k in (4, 5, 6, 7):
                        t, c = (k - 4) // 2, k % 2
                        bias = (bq, bk)[t]
                        if m >= 2:
                            for half in range(2):
                                wait(act, stacked[m % 2][half], at(m, STACK, turn, STACK * (m // 2)))
                        wait(act, fill_ready, fl(m, k, turn))
                        act.activation(parts[t][:, m % 2, c, 0, :], r[:, :], ACT.Identity, bias=bias[:, u, c:c + 1]).then_inc(part1_done, 1)

                def part2(m, k, turn):
                    if not ug_valid(m, turn):
                        return
                    t, c = (k - 4) // 2, k % 2
                    wait(act, fill_freed, fl(m, k, turn))
                    act.activation(parts[t][:, m % 2, c, 1, :], rest[:, k % 2, :], ACT.Copy).then_inc(part2_done, 1)

                def program(i, turn):
                    m, r = (i + 7) // G, (i + 7) % G
                    for j in range(4):
                        if ub_valid(i, turn):
                            wait(act, st_ready, ub(4, i, turn, j + 1))
                            wait(act, pv_done, ub(4, i - 2, turn, j + 1))
                            act.activation(probs[:, i % 2, HB * j:HB * j + HB, :].rearrange("p h q -> p (h q)"), ST[j % 2][:, :], ACT.Exp,
                                           scale=float(HD) ** -0.5).then_inc(exp_done, 1)
                        if j == 3 and ub_valid(i - 1, turn):
                            wait(act, pv_done, ub(4, i, turn))
                            wait(act, o_turned, ub(1, i - 1, turn))
                            act.activation(o_un[:, :, :].rearrange("p c t -> p (c t)"), PO[:, :, :].rearrange("p c t -> p (c t)"), ACT.Copy).then_inc(o_un_done, 1)
                        if j == 2 and ub_valid(i - 2, turn):
                            wait(act, oT_ready, ub(1, i - 1, turn))
                            act.activation(oT_hi[:, :, :].rearrange("p c t -> p (c t)"), X[:, 0:D], ACT.Copy).then_inc(oT_hi_done, 1)
                        if j == 1 and ub_valid(i + 1, turn):
                            wait(act, mT_ready, ub(1, i + 2, turn))
                            wait(act, negmax_stacked[(i + 1) % 2], at(i, 16 * BODY // 2, turn, 16 * ((i + 1) // 2)))
                            act.activation(mT[:, (i + 1) % 2, :], X[0:PARTS * H, 0:P // 2].bitcast(BF16), ACT.Copy).then_inc(mT_done, 1)
                        if r == 0:
                            fill_out(m, FIRST_FILLS[j], turn)
                        elif r in (1, 2):
                            k = 2 + 2 * r + j // 2
                            if j in (0, 2):
                                fill_out(m, k, turn)
                            else:
                                part2(m, k, turn)
                        elif r == 3 and j == 2 and has(m, "R") and ug_valid(m, turn):
                            wait(act, rt_done, gr(4, m, turn, -1))
                            act.activation(lexp[:, :, :], logit[:, :, :], ACT.Exp).then_inc(rt_exp_done, 1)

                steps(act, N, first_step, loop_first, program)

            @block.vector
            def _(dve):
                for u in range(U):
                    dve.wait_ge(w_hi_done, u + 1)
                    dve.tensor_tensor(wlo[:, u, :, :, :].rearrange("p k c n -> p (k c n)"), w32[:, :, :, :].rearrange("p k c n -> p (k c n)"),
                                      whi[:, u, :, :, :].rearrange("p k c n -> p (k c n)"), ALU.subtract).then_inc(w_lo_done, 1)
                dve.wait_ge(b_loaded, B_IN)

                def statistics(m, b0, turn):
                    g = m // U
                    if b0 == 0:
                        wait(dve, x_loaded[g % XR], at(m, 16, turn, 16 * (g // XR + 1)))
                    for b in range(b0, b0 + 2):
                        dve.bn_stats(stats[:, b, :], x_in[:, g % XR, b, :]).then_inc(ln_stats, 1)

                def guess(m, j, turn):
                    if j == 0:
                        wait(dve, n_ready, gr(G, m, turn, -G))
                        for b in range(G):
                            wait_apart(dve, ln_stats, gr(G, m, turn, b + 1 - G), dve_passed)
                            dve.bn_aggr(moments[:, b, :], stats[:, b, :]).then_inc(ln_moments, 1)
                    elif j == 1:
                        wait(dve, ln_moments, gr(G, m, turn))
                        dve.tensor_scalar(var_eps[:, :], moments[:, :, 1:2].rearrange("p b o -> p (b o)"), 1e-5 if U == 1 else 1e-6, None,
                                          ALU.add).then_inc(ln_guess, 1)
                    elif j == 2:
                        wait(dve, ln_guess, gr(3, m, turn, -2))
                        dve.tensor_scalar(half_bits[:, :], var_eps[:, :].bitcast(I32), 1, None, ALU.logical_shift_right).then_inc(ln_guess, 1)
                    else:
                        wait(dve, ln_guess, gr(3, m, turn, -1))
                        dve.tensor_scalar(rstd[:, :].bitcast(I32), half_bits[:, :], -1, GUESS, ALU.mult, ALU.add).then_inc(ln_guess, 1)

                def normalise(m, b0, turn):
                    g = m // U
                    wait(dve, newton_done, gr(4 * NEWTON, m, turn))
                    if m >= U:
                        wait(dve, fill_ready, fl(m - U, 1, turn))
                    for b in range(b0, b0 + 2):
                        dve.tensor_scalar(n_tok[:, b, :], x_in[:, g % XR, b, :], moments[:, b, 0:1], rstd[:, b:b + 1],
                                          ALU.subtract, ALU.mult).then_inc(n_ready, 1)

                def fill_out(m, k, turn):
                    if not ug_valid(m, turn) or not has(m, k):
                        return
                    u = m % U
                    r = R[fidx(m, k) % FPB % 2]
                    if k in (0, 1, 2, 3):
                        if U == 1:
                            hi, lo = (nT_hi, nT_lo) if k < 2 else (cT_hi, cT_lo)
                            wait(dve, xT_hi_done, gr(4, m, turn, FILLS0.index(k) - 3))
                            dve.tensor_tensor(lo[:, k % 2, :], r[:, :], hi[:, k % 2, :], ALU.subtract).then_inc(fill_freed, 1)
                        else:
                            wait(dve, fill_ready, fl(m, k, turn))
                            wait(dve, xT_lo_done, gr(2, m, turn, -2))
                            dve.tensor_scalar(nT[:, k, :], r[:, :], gamma[:, k:k + 1], beta[:, k:k + 1], ALU.mult, ALU.add).then_inc(fill_freed, 1)
                    elif k in (4, 5, 6, 7):
                        t, c = (k - 4) // 2, k % 2
                        bias = (bq, bk)[t]
                        wait(dve, part1_done, at(m, 8, turn, 4 * m + k - 3))
                        wait(dve, part3_done, at(m, 8, turn, 4 * m + k - 5))
                        dve.scalar_tensor_tensor(rest[:, k % 2, :], r[:, :], bias[:, u, c:c + 1], parts[t][:, m % 2, c, 0, :],
                                                 ALU.add, ALU.subtract).then_inc(fill_freed, 1)
                    elif k == "R":
                        wait(dve, fill_ready, fl(m, k, turn))
                        dve.scalar_tensor_tensor(logit[:, :, :].rearrange("p b u -> p (b u)"), r[:, 0:G * U], 1.0 / P,
                                                 rb[:, :, :].rearrange("p b u -> p (b u)"), ALU.mult, ALU.add).then_inc(fill_freed, 1)
                        wait(dve, fill_freed, fl(m, k, turn))
                        dve.tensor_reduce(lmax[:, :], logit[:, :, :], AX.X, ALU.max).then_inc(rt_done, 1)
                        wait(dve, rt_done, gr(4, m, turn, -3))
                        dve.tensor_tensor(lexp[:, :, :], logit[:, :, :], lmax[:, :].rearrange("p (b o) -> p b o", o=1).to_broadcast([P, G, U]),
                                          ALU.subtract).then_inc(rt_done, 1)
                        wait(dve, rt_done, gr(4, m, turn, -2))
                        dve.tensor_copy(logit[:, :, :], lexp[:, :, :]).then_inc(rt_done, 1)
                    else:
                        wait(dve, fill_ready, fl(m, k, turn))
                        b = 2 * (k - 8)
                        if m >= 2:
                            wait(dve, pv_done, ub(4, 4 * m - 6 + b, turn))
                        dve.tensor_tensor(v_aug[:, m % 2, b:b + 2, :, 0:HD], r[:, :].rearrange("p (b h d) -> p b h d", b=2, h=H),
                                          bv[:, u, :, :].rearrange("p b (h d) -> p b h d", h=H), ALU.add).then_inc(fill_freed, 1)

                def unit_weights(m, turn):
                    wait(dve, rt_exp_done, gr(1, m, turn))
                    dve.tensor_reduce(lsum[:, :], lexp[:, :, :], AX.X, ALU.add).then_inc(rt_done, 1)
                    wait(dve, rt_done, gr(4, m, turn))
                    wait(dve, p_copied, gr(3, m, turn, -3))
                    dve.reciprocal(lmax[:, :], lsum[:, :]).then_inc(p_copied, 1)
                    wait(dve, p_copied, gr(3, m, turn, -2))
                    dve.tensor_tensor(p_new[:, :, :], lexp[:, :, :], lmax[:, :].rearrange("p (b o) -> p b o", o=1).to_broadcast([P, G, U]),
                                      ALU.mult).then_inc(p_copied, 1)

                def maximum(i, j, turn):
                    wait(dve, s_ready, ub(4, i, turn, j + 1))
                    if j == 0:
                        wait(dve, mpart_done, ub(4, i - 1, turn))
                    dve.tensor_reduce(nmax[:, i % 2, HB * j:HB * j + HB], S[j % 2][:, :, :], AX.X, ALU.max, negate=True).then_inc(max_done, 1)

                def program(i, turn):
                    m, r = (i + 7) // G, (i + 7) % G
                    d = i - 2
                    u, b = (d // G) % U, d % G
                    for j in range(4):
                        if ub_valid(i + 2, turn) and j < 3:
                            maximum(i + 2, j, turn)
                        if ub_valid(d, turn):
                            if j == 0:
                                wait(dve, o_turned, ub(1, d + 1, turn))
                                xv = X[:, :].rearrange("p (h e) -> p h e", h=H)
                                dve.reciprocal(o_rec[:, :].rearrange("p (h o) -> p h o", o=1), xv[:, :, HD:HD + 1]).then_inc(o_rec_done, 1)
                                wait(dve, o_rec_done, ub(1, d + 1, turn))
                                dve.tensor_tensor(o_tok[:, :, :], xv[:, :, 0:HD], o_rec[:, :].rearrange("p (h o) -> p h o", o=1).to_broadcast([P, H, HD]),
                                                  ALU.mult).then_inc(o_tok_done, 1)
                            elif j == 2:
                                wait(dve, oT_hi_done, ub(1, d + 1, turn))
                                dve.tensor_tensor(oT_lo[:, :, :].rearrange("p c t -> p (c t)"), X[:, 0:D], oT_hi[:, :, :].rearrange("p c t -> p (c t)"),
                                                  ALU.subtract).then_inc(oT_lo_done, 1)
                            elif j == 3:
                                wait(dve, y_ready, ub(1, d + 1, turn))
                                wait(dve, y_done, ub(1, d, turn))
                                dve.tensor_tensor(y_bias[:, :], X[:, 0:D], bo[:, u, :], ALU.add).then_inc(y_bias_done, 1)
                            if j == 3 and U == 2:
                                if u == 0 and b == 0:
                                    wait(dve, p_copied, gr(3, d // G, turn, -1))
                                    wait(dve, y_done, ub(1, d, turn))
                                    dve.tensor_copy(p_use[:, :, :], p_new[:, :, :]).then_inc(p_copied, 1)
                                if b == 0 and u == 0:
                                    wait(dve, p_copied, gr(3, d // G, turn))
                                wait(dve, y_bias_done, ub(1, d + 1, turn))
                                if u == 0:
                                    wait(dve, xr_loaded[b], gr(16, d // G, turn))
                                else:
                                    wait(dve, y_stored[b % 2], at(d, 32, turn, 16 * (2 * (d // 8) + b // 2)))
                                    wait(dve, y_done, ub(1, d - 3, turn))
                                out = x_res[:, b, :] if u == 0 else y_out[:, b % 2, :]
                                dve.scalar_tensor_tensor(out, y_bias[:, :], p_use[:, b, u:u + 1], x_res[:, b, :], ALU.mult, ALU.add).then_inc(y_done, 1)
                        if ub_valid(i + 2, turn) and j == 3:
                            maximum(i + 2, j, turn)
                        mn, rn = (i + 7 + lead) // G, (i + 7 + lead) % G
                        if mn % U == 0 and ug_valid(mn, turn) and rn == 0 and j == U - 1:
                            normalise(mn, 2, turn)
                        if r == 0:
                            if j == 0:
                                fill_out(m - 1, 9, turn)
                            fill_out(m, FIRST_FILLS[j], turn)
                        elif r in (1, 2) and j in (0, 2):
                            fill_out(m, 2 + 2 * r + j // 2, turn)
                        elif r == 1 and j == 1 and U == 2 and ug_valid(m, turn) and m % 2 == 0:
                            if m >= U:
                                wait(dve, fill_ready, fl(m - U, "R", turn))
                            for c in range(KC):
                                dve.tensor_reduce(mean[:, c, :], nT[:, c, :].rearrange("p (b t) -> p b t", b=G), AX.X, ALU.add).then_inc(mean_done, 1)
                        elif r == 3 and j == v_slot(m):
                            fill_out(m, 8, turn)
                        elif r == 3 and U == 2 and ug_valid(m, turn) and m % 2 == 0:
                            if j == 0:
                                fill_out(m, "R", turn)
                            elif j == 3:
                                unit_weights(m, turn)
                        if (mn + 1) % U == 0 and ug_valid(mn + 1, turn):
                            if rn == 1 and j in (1, 3):
                                statistics(mn + 1, j - 1, turn)
                            elif rn == 2:
                                guess(mn + 1, j, turn)
                            elif rn == 3 and j == 3:
                                normalise(mn + 1, 0, turn)

                steps(dve, N, first_step, loop_first, program)

            @block.gpsimd
            def _(pool):
                pool.memset(v_aug[:, :, :, :, HD:2 * HD], 1.0).then_inc(ones_done, 1)
                pool.wait_ge(ones_done, 1)
                pool.memset(ks[ROWS:ROWS + PARTS, :, :, :], 1.0).then_inc(ones_done, 1)
                pool.wait_ge(ones_done, 2)

                def rstd_newton(m, turn):
                    done = 0

                    def stepped(instruction):
                        nonlocal done
                        done += 1
                        instruction.then_inc(newton_done, 1)
                        wait_apart(pool, newton_done, gr(4 * NEWTON, m, turn, done - 4 * NEWTON), pool_passed)

                    wait(pool, ln_guess, gr(3, m, turn))
                    for _ in range(NEWTON):
                        stepped(pool.tensor_tensor(square[:, :], rstd[:, :], rstd[:, :], ALU.mult))
                        stepped(pool.tensor_tensor(square[:, :], square[:, :], var_eps[:, :], ALU.mult))
                        stepped(pool.tensor_scalar(square[:, :], square[:, :], -0.5, 1.5, ALU.mult, ALU.add))
                        stepped(pool.tensor_tensor(rstd[:, :], rstd[:, :], square[:, :], ALU.mult))

                def part3(m, r, c, turn):
                    if r in (1, 2) and ug_valid(m, turn):
                        wait(pool, part2_done, at(m, 8, turn, 4 * m + 2 * (r - 1) + c + 1))
                        pool.tensor_tensor(parts[r - 1][:, m % 2, c, 2, :], rest[:, c, :], parts[r - 1][:, m % 2, c, 1, :],
                                           ALU.subtract).then_inc(part3_done, 1)

                def program(i, turn):
                    m, r = (i + 7) // G, (i + 7) % G
                    mn, rn = (i + 7 + lead) // G, (i + 7 + lead) % G
                    if rn == 3 and ug_valid(mn + 1, turn) and (mn + 1) % U == 0:
                        rstd_newton(mn + 1, turn)
                    if U == 2 and r == 0 and ug_valid(m, turn) and m % 2 == 0:
                        for c in range(KC):
                            wait(pool, xT_hi_done, gr(2, m, turn, c - 1))
                            pool.tensor_tensor(nT_lo[:, c, :], nT[:, c, :], nT_hi[:, c, :], ALU.subtract).then_inc(xT_lo_done, 1)
                    part3(m, r, 0, turn)
                    if ub_valid(i + 2, turn):
                        e, z = i + 2, i % 2
                        wait(pool, max_done, ub(4, e + 1, turn))
                        wait_apart(pool, mT_ready, ub(1, e - 1, turn), pool_passed)
                        pool.tensor_copy(mparts[:, z, 0, :], nmax[:, z, :]).then_inc(mpart_done, 1)
                        wait(pool, mpart_done, ub(4, e, turn, 1))
                        pool.tensor_tensor(mres[:, z, :], nmax[:, z, :], mparts[:, z, 0, :], ALU.subtract).then_inc(mpart_done, 1)
                        wait_apart(pool, mpart_done, ub(4, e, turn, 2), pool_passed)
                        pool.tensor_copy(mparts[:, z, 1, :], mres[:, z, :]).then_inc(mpart_done, 1)
                        wait(pool, mpart_done, ub(4, e, turn, 3))
                        pool.tensor_tensor(mparts[:, z, 2, :], mres[:, z, :], mparts[:, z, 1, :], ALU.subtract).then_inc(mpart_done, 1)
                    part3(m, r, 1, turn)
                    if U == 1 and ub_valid(i - 2, turn):
                        d = i - 2
                        wait(pool, y_bias_done, ub(1, d + 1, turn))
                        wait(pool, xr_loaded[d % G], gr(16, d // G, turn))
                        wait(pool, y_stored[d % 2], at(d, 16 * BODY // 2, turn, 16 * (d // 2)))
                        pool.tensor_tensor(y_out[:, d % 2, :], y_bias[:, :], x_res[:, d % G, :], ALU.add).then_inc(y_done, 1)

                steps(pool, N, first_step, loop_first, program)
        clear_semaphores(nc, sems)


E = 8
F = 512
FC = F // P
TOP = 2
U32 = mybir.dt.uint32
BELOW_ALL = -3.0e38


def newton_steps(eng, done, counted, rstd, square, minus_half_var):
    n = 0
    for _ in range(NEWTON):
        for out, a, b, op in ((square, rstd, rstd, ALU.mult), (square, square, minus_half_var, ALU.mult)):
            eng.tensor_tensor(out[:, :], a[:, :], b[:, :], op).then_inc(done, 1)
            n += 1
            counted(n)
        eng.scalar_tensor_tensor(rstd[:, :], square[:, :], 1.5, rstd[:, :], ALU.add, ALU.mult).then_inc(done, 1)
        n += 1
        counted(n)


def route_phase(nc, name, src, n_dst, by_token, w_router, b_router, gamma, beta, logits, ident, ones, B, preload=None):
    NG = B // G
    with ExitStack() as es:
        def sb(n, shape, dt):
            return es.enter_context(nc.sbuf_tensor(f"{name}_{n}", shape, dt))

        def ps(n, shape, dt):
            return es.enter_context(nc.psum_tensor(f"{name}_{n}", shape, dt))

        sems = []

        def sem(n):
            sems.append(nc.alloc_semaphore(name=f"{name}_{n}"))
            return sems[-1]

        x_in = sb("x_in", [P, 2, G, D], F32)
        n_tok = sb("n_tok", [P, 2, G, D], F32)
        stats = sb("stats", [P, G, 6], F32)
        moments = sb("moments", [P, G, 2], F32)
        var_eps = sb("var_eps", [P, G], F32)
        half_bits = sb("half_bits", [P, G], I32)
        square = sb("square", [P, G], F32)
        rstd = sb("rstd", [P, G], F32)
        rw = sb("rw", [P, KC, E], F32)
        rb = sb("rb", [P, G, E], F32)
        cols = sb("cols", [P, KC, T if by_token else G], F32)
        PT = [ps(f"PT{c}", [P, T], F32) for c in range(KC)]
        PL = [ps(f"PL{k}", [P, T], F32) for k in range(2)]
        if not by_token:
            gam = sb("gam", [P, D], F32)
            bet = sb("bet", [P, D], F32)

        w_loaded = sem("w_loaded")
        x_loaded = [sem(f"x_loaded{k}") for k in range(2)]
        n_stored = [sem(f"n_stored{k}") for k in range(2)]
        ln_stats, ln_moments, ln_guess, newton_done = sem("ln_stats"), sem("ln_moments"), sem("ln_guess"), sem("newton_done")
        n_plain, n_scaled, n_ready = sem("n_plain"), sem("n_scaled"), sem("n_ready")
        pt_ready, cols_done, pl_ready, logits_done = sem("pt_ready"), sem("cols_done"), sem("pl_ready"), sem("logits_done")
        sp_passed, dve_passed = sem("sp_passed"), sem("dve_passed")
        pre_loaded = [sem(f"pre_loaded{k}") for k in range(2)]
        pre_hi_done, pre_lo_done = sem("pre_hi_done"), sem("pre_lo_done")
        W_IN = 16 if by_token else 64
        routed = logits is not None

        def cnt(per, turn, k, c=0):
            return per * (2 * turn + k + 1) + c

        with nc.Block() as block:

            @block.sync
            def _(sp):
                if routed:
                    sp.dma_start(rw[:, :, :], w_router.rearrange("(c p) e -> p c e", p=P)).then_inc(w_loaded, 16)
                if not by_token:
                    sp.dma_start(rb[:, :, :], b_router.rearrange("(a b e) -> a b e", a=1, b=1).to_broadcast([P, G, E])).then_inc(w_loaded, 16)
                    sp.dma_start(gam[:, :], gamma.rearrange("(a n) -> a n", a=1).to_broadcast([P, D])).then_inc(w_loaded, 16)
                    sp.dma_start(bet[:, :], beta.rearrange("(a n) -> a n", a=1).to_broadcast([P, D])).then_inc(w_loaded, 16)
                for k in range(2):
                    sp.dma_start(x_in[:, k, :, :], src[k * G:k * G + G].rearrange("b t d -> t b d")).then_inc(x_loaded[k], 16)
                with sp.Fori(0, NG // 2 - 1) as turn:
                    for k in range(2):
                        wait_apart(sp, n_ready, cnt(1, turn, k), sp_passed)
                        sp.dma_start(n_dst[bass.ds((2 * turn + k) * G, G)].rearrange("b t d -> t b d"), n_tok[:, k, :, :]).then_inc(n_stored[k], 16)
                        sp.dma_start(x_in[:, k, :, :], src[bass.ds((2 * turn + k + 2) * G, G)].rearrange("b t d -> t b d")).then_inc(x_loaded[k], 16)
                for k in range(2):
                    sp.wait_ge(n_ready, NG - 1 + k)
                    sp.dma_start(n_dst[(NG - 2 + k) * G:(NG - 1 + k) * G].rearrange("b t d -> t b d"), n_tok[:, k, :, :]).then_inc(n_stored[k], 16)
                for k in range(2):
                    sp.wait_ge(n_stored[k], 16 * NG // 2)

            if preload is not None:
                @block.gpsimd
                def _(pool):
                    n = len(preload["sources"])
                    for q in range(2):
                        load_matrix(pool, preload, q, pre_loaded, pre_lo_done)
                    for q in range(n):
                        pool.wait_ge(pre_loaded[q % 2], 16 * (q // 2 + 1))
                        pool.tensor_copy(half_of(preload["hi"], q), preload["w32"][:, q % 2, :]).then_inc(pre_hi_done, 1)
                        pool.wait_ge(pre_hi_done, q + 1)
                        pool.tensor_tensor(half_of(preload["lo"], q), preload["w32"][:, q % 2, :], half_of(preload["hi"], q), ALU.subtract).then_inc(pre_lo_done, 1)
                        if q + 2 < n:
                            load_matrix(pool, preload, q + 2, pre_loaded, pre_lo_done)

            @block.vector
            def _(dve):
                if routed:
                    dve.wait_ge(w_loaded, W_IN)

                def group(turn, k, first):
                    dve.wait_ge(x_loaded[k], 16 * (turn + 1))
                    for b in range(G):
                        dve.bn_stats(stats[:, b, :], x_in[:, k, b, :]).then_inc(ln_stats, 1)
                    for b in range(G):
                        wait_apart(dve, ln_stats, cnt(G, turn, k, b + 1 - G), dve_passed)
                        dve.bn_aggr(moments[:, b, :], stats[:, b, :]).then_inc(ln_moments, 1)
                    dve.wait_ge(ln_moments, cnt(G, turn, k))
                    var = moments[:, :, 1:2].rearrange("p b o -> p (b o)")
                    eps = 1e-5 if by_token else 1e-6
                    dve.tensor_scalar(var_eps[:, :], var, eps, None, ALU.add).then_inc(ln_guess, 1)
                    dve.wait_ge(ln_guess, cnt(4, turn, k, -3))
                    dve.tensor_scalar(half_bits[:, :], var_eps[:, :].bitcast(I32), 1, None, ALU.logical_shift_right).then_inc(ln_guess, 1)
                    dve.wait_ge(ln_guess, cnt(4, turn, k, -2))
                    dve.tensor_scalar(rstd[:, :].bitcast(I32), half_bits[:, :], -1, GUESS, ALU.mult, ALU.add).then_inc(ln_guess, 1)
                    dve.tensor_scalar(var_eps[:, :], var, eps, -0.5, ALU.add, ALU.mult).then_inc(ln_guess, 1)
                    dve.wait_ge(ln_guess, cnt(4, turn, k))
                    per = 3 * NEWTON
                    newton_steps(dve, newton_done, lambda n: dve.wait_ge(newton_done, cnt(per, turn, k, n - per)), rstd, square, var_eps)
                    if not first:
                        dve.wait_ge(n_stored[k], 16 * turn)
                        if routed:
                            dve.wait_ge(cols_done, cnt(KC if by_token else 1, turn, k, -2 * (KC if by_token else 1)))
                    for b in range(G):
                        ins = dve.tensor_scalar(n_tok[:, k, b, :], x_in[:, k, b, :], moments[:, b, 0:1], rstd[:, b:b + 1], ALU.subtract, ALU.mult)
                        ins.then_inc(n_plain, 1)
                    dve.wait_ge(n_plain, cnt(G, turn, k))
                    if by_token:
                        dve.sem_inc(n_ready, 1)
                    else:
                        v = n_tok[:, k, :, :]
                        dve.tensor_tensor(v, v, gam[:, :].rearrange("p (o n) -> p o n", o=1).to_broadcast([P, G, D]), ALU.mult).then_inc(n_scaled, 1)
                        dve.wait_ge(n_scaled, cnt(1, turn, k))
                        dve.tensor_tensor(v, v, bet[:, :].rearrange("p (o n) -> p o n", o=1).to_broadcast([P, G, D]), ALU.add).then_inc(n_ready, 1)

                def logits_out(turn, k):
                    if not routed:
                        return
                    dve.wait_ge(pl_ready, cnt(1, turn, k))
                    out = logits[:, bass.ds((2 * turn + k) * G, G), :]
                    pl = PL[k][:, 0:G * E].rearrange("p (b e) -> p b e", b=G)
                    if by_token:
                        dve.tensor_copy(out, pl).then_inc(logits_done, 1)
                    else:
                        dve.tensor_tensor(out, pl, rb[:, :, :], ALU.add).then_inc(logits_done, 1)

                group(0, 0, True)
                group(0, 1, True)
                logits_out(0, 0)
                with dve.Fori(1, NG // 2) as turn:
                    group(turn, 0, False)
                    logits_out(turn - 1, 1)
                    group(turn, 1, False)
                    logits_out(turn, 0)
                logits_out(NG // 2 - 1, 1)

            if routed:
                @block.tensor
                def _(pe):
                    pe.wait_ge(w_loaded, W_IN)

                    def group(turn, k, first):
                        pe.wait_ge(n_ready, cnt(1, turn, k))
                        if by_token:
                            for c in range(KC):
                                if not (first and k == 0):
                                    pe.wait_ge(cols_done, cnt(KC, turn, k, c + 1 - 2 * KC))
                                for b in range(G):
                                    last = pe.transpose(PT[c][:, b * P:(b + 1) * P], n_tok[:, k, b, c * P:(c + 1) * P], ident[:, :])
                                last.then_inc(pt_ready, 1)
                            pe.wait_ge(cols_done, cnt(KC, turn, k))
                        else:
                            if not (first and k == 0):
                                pe.wait_ge(cols_done, cnt(1, turn, k, -1))
                            for c in range(KC):
                                for b in range(G):
                                    last = pe.matmul(PT[0][:, c * G + b:c * G + b + 1], n_tok[:, k, b, c * P:(c + 1) * P], ones[:, 0:1], start=True, stop=True)
                            last.then_inc(pt_ready, 1)
                            pe.wait_ge(cols_done, cnt(1, turn, k))
                        if not first:
                            pe.wait_ge(logits_done, cnt(1, turn, k, -2))
                        for b in range(G):
                            for c in range(KC):
                                a = cols[:, c, b * P:(b + 1) * P] if by_token else cols[:, c, b:b + 1].to_broadcast([P, P])
                                last = pe.matmul(PL[k][:, b * E:(b + 1) * E], a, rw[:, c, :], start=(c == 0), stop=(c == KC - 1))
                        last.then_inc(pl_ready, 1)

                    for k in range(2):
                        group(0, k, True)
                    with pe.Fori(1, NG // 2) as turn:
                        for k in range(2):
                            group(turn, k, False)

                @block.scalar
                def _(act):
                    def group(turn, k, first):
                        if not (first and k == 0):
                            act.wait_ge(pl_ready, cnt(1, turn, k, -1))
                        if by_token:
                            for c in range(KC):
                                act.wait_ge(pt_ready, cnt(KC, turn, k, c + 1 - KC))
                                act.activation(cols[:, c, :], PT[c][:, :], ACT.Copy).then_inc(cols_done, 1)
                        else:
                            act.wait_ge(pt_ready, cnt(1, turn, k))
                            act.activation(cols[:, :, :].rearrange("p c b -> p (c b)"), PT[0][:, 0:KC * G], ACT.Copy, scale=1.0 / P).then_inc(cols_done, 1)

                    for k in range(2):
                        group(0, k, True)
                    with act.Fori(1, NG // 2) as turn:
                        for k in range(2):
                            group(turn, k, False)
        clear_semaphores(nc, sems)


def top_two_phase(nc, name, logits, weights, experts, tokens_sorted, preload, B):
    with ExitStack() as es:
        def sb(n, shape, dt):
            return es.enter_context(nc.sbuf_tensor(f"{name}_{n}", shape, dt))

        sems = []

        def sem(n):
            sems.append(nc.alloc_semaphore(name=f"{name}_{n}"))
            return sems[-1]

        rev = sb("rev", [P, B, E], F32)
        eq = sb("eq", [P, B, E], F32)
        best = sb("best", [P, TOP, B], F32)
        pick = sb("pick", [P, TOP, B], F32)
        onehot = [sb(f"onehot{k}", [P, B, E], F32) for k in range(TOP)]
        rest = sb("rest", [P, B, E], F32)
        ratio = sb("ratio", [P, B], F32)
        step, gone, exp_done, rev_done = sem("step"), sem("gone"), sem("exp_done"), sem("rev_done")
        if tokens_sorted:
            n_dram, place, slot_token, tile_expert = (tokens_sorted[k] for k in ("slots", "place", "slot_token", "tile_expert"))
            NT = tokens_sorted["tiles"]
            ones_tri = sb("ones_tri", [P, P], F32)
            both = sb("both", [P, B, E], F32)
            before = sb("before", [P, E, B], F32)
            carry = sb("carry", [P, E, B + 1], F32)
            zero = sb("zero", [P, B + 1], F32)
            padded = sb("padded", [P, E], F32)
            padded_i = sb("padded_i", [P, E], I32)
            base = sb("base", [P, E + 1], F32)
            posf = sb("posf", [P, B, E], F32)
            token = sb("token", [P, B], I32)
            slot = sb("slot", [P, TOP, B], U32)
            slot_now = sb("slot_now", [P, TOP, 4], U32)
            token_now = sb("token_now", [P, 4], I32)
            taken, scatter_passed = sem("taken"), sem("scatter_passed")
            row = sb("row", [P, B], I32)
            rowf = sb("rowf", [P, B], F32)
            zeros_i = sb("zeros_i", [P, NT], I32)
            tile_row = sb("tile_row", [1, NT], F32)
            tile_sum = sb("tile_sum", [1, NT], F32)
            tile_ge = sb("tile_ge", [1, NT], F32)
            PR = es.enter_context(nc.psum_tensor(f"{name}_PR", [P, B * E], F32))
            PC = es.enter_context(nc.psum_tensor(f"{name}_PC", [P, B * E], F32))
            w_loaded = [sem(f"w_loaded{k}") for k in range(2)]
            w_hi_done, w_lo_done = sem("w_hi_done"), sem("w_lo_done")
            tri_done, ranks_ready, cleared, scattered, listed = (
                sem("tri_done"), sem("ranks_ready"), sem("cleared"), sem("scattered"), sem("listed"))

        def wide(v):
            return v.rearrange("p (b o) -> p b o", o=1).to_broadcast([P, B, E])

        with nc.Block() as block:

            @block.vector
            def _(dve):
                n = 0

                def then(instruction):
                    nonlocal n
                    n += 1
                    instruction.then_inc(step, 1)
                    dve.wait_ge(step, n)

                dve.wait_ge(rev_done, 1)
                scores = logits
                for k in range(TOP):
                    then(dve.tensor_reduce(best[:, k, :], scores[:, :, :], AX.X, ALU.max))
                    then(dve.tensor_tensor(eq[:, :, :], scores[:, :, :], wide(best[:, k, :]), ALU.is_equal))
                    then(dve.tensor_tensor(eq[:, :, :], eq[:, :, :], rev[:, :, :], ALU.mult))
                    then(dve.tensor_reduce(pick[:, k, :], eq[:, :, :], AX.X, ALU.max))
                    then(dve.tensor_tensor(onehot[k][:, :, :], eq[:, :, :], wide(pick[:, k, :]), ALU.is_equal))
                    if k == 0:
                        then(dve.scalar_tensor_tensor(rest[:, :, :].rearrange("p b e -> p (b e)"), onehot[0][:, :, :].rearrange("p b e -> p (b e)"), BELOW_ALL,
                                                      logits[:, :, :].rearrange("p b e -> p (b e)"), ALU.mult, ALU.add))
                        scores = rest
                dve.tensor_tensor(ratio[:, :], best[:, 1, :], best[:, 0, :], ALU.subtract).then_inc(gone, 1)
                dve.wait_ge(exp_done, 1)
                then(dve.tensor_scalar(best[:, 0, :], ratio[:, :], 1.0, None, ALU.add))
                then(dve.reciprocal(best[:, 1, :], best[:, 0, :]))
                then(dve.tensor_copy(weights[:, :, 0:1].rearrange("p b o -> p (b o)"), best[:, 1, :]))
                then(dve.tensor_tensor(weights[:, :, 1:2].rearrange("p b o -> p (b o)"), best[:, 1, :], ratio[:, :], ALU.mult))
                if not tokens_sorted:
                    for k in range(TOP):
                        then(dve.tensor_scalar(experts[0:1, :].rearrange("p (b k) -> p b k", k=TOP)[:, :, k], pick[0:1, k, :], -1.0, float(E), ALU.mult, ALU.add))
                    return
                then(dve.tensor_tensor(both[:, :, :], onehot[0][:, :, :], onehot[1][:, :, :], ALU.add))
                dve.sem_inc(gone, 1)
                then(dve.memset(zero[:, :], 0.0))
                then(dve.memset(carry[:, :, 0:1], 0.0))
                then(dve.memset(base[:, 0:1], float(tokens_sorted["first_slot"])))
                dve.wait_ge(ranks_ready, 2)
                for e in range(E):
                    then(dve.tensor_tensor_scan(carry[:, e, 1:B + 1], PC[:, :].rearrange("p (b e) -> p e b", e=E)[:, e, :], zero[:, 1:B + 1], 0.0, ALU.add, ALU.add))
                then(dve.tensor_scalar(padded_i[:, :], carry[:, :, B:B + 1].rearrange("p e o -> p (e o)"), float(P - 1), None, ALU.add))
                then(dve.tensor_scalar(padded_i[:, :], padded_i[:, :], 7, 7, ALU.logical_shift_right, ALU.logical_shift_left))
                then(dve.tensor_copy(padded[:, :], padded_i[:, :]))
                for e in range(E):
                    then(dve.tensor_tensor(base[:, e + 1:e + 2], base[:, e:e + 1], padded[:, e:e + 1], ALU.add))
                then(dve.tensor_tensor(posf[:, :, :], PR[:, :].rearrange("p (b e) -> p b e", e=E), carry[:, :, 0:B].rearrange("p e b -> p b e"), ALU.add))
                then(dve.tensor_tensor(posf[:, :, :], posf[:, :, :], base[:, 0:E].rearrange("p (o e) -> p o e", o=1).to_broadcast([P, B, E]), ALU.add))
                for k in range(TOP):
                    then(dve.tensor_tensor(onehot[k][:, :, :], onehot[k][:, :, :], posf[:, :, :], ALU.mult))
                    then(dve.tensor_reduce(pick[:, k, :], onehot[k][:, :, :], AX.X, ALU.add))
                    then(dve.tensor_copy(place[:, k, :], pick[:, k, :]))
                    then(dve.tensor_scalar(row[:, :], place[:, k, :].bitcast(I32), P - 1, None, ALU.bitwise_and))
                    then(dve.tensor_copy(rowf[:, :], row[:, :]))
                    then(dve.tensor_tensor(pick[:, k, :], pick[:, k, :], rowf[:, :], ALU.subtract))
                    then(dve.tensor_scalar(pick[:, k, :], pick[:, k, :], 1.0 / P, None, ALU.mult))
                    then(dve.scalar_tensor_tensor(pick[:, k, :], rowf[:, :], float(NT), pick[:, k, :], ALU.mult, ALU.add))
                    then(dve.tensor_copy(slot[:, k, :], pick[:, k, :]))
                dve.sem_inc(gone, 1)
                dve.wait_ge(rev_done, 2)
                then(dve.memset(tile_sum[:, :], 0.0))
                for e in range(1, E + 1):
                    then(dve.tensor_scalar(tile_ge[:, :], tile_row[:, :], base[0:1, e:e + 1], None, ALU.is_ge))
                    then(dve.tensor_tensor(tile_sum[:, :], tile_sum[:, :], tile_ge[:, :], ALU.add))
                then(dve.tensor_scalar(tile_sum[:, :], tile_sum[:, :], float(E - 1), None, ALU.min))
                first = tokens_sorted["first_slot"] // P
                then(dve.tensor_copy(tile_expert[0:1, :], tile_sum[:, :]))
                then(dve.memset(tile_sum[:, 0:first], float(E)))
                then(dve.tensor_copy(tile_expert[0:1, 0:first], tile_sum[:, 0:first]))
                for q in range(len(preload["sources"])):
                    dve.wait_ge(w_hi_done, q + 1)
                    dve.tensor_tensor(half_of(preload["lo"], q), preload["w32"][:, q % 2, :], half_of(preload["hi"], q), ALU.subtract).then_inc(w_lo_done, 1)

            @block.scalar
            def _(act):
                act.wait_ge(gone, 1)
                act.activation(ratio[:, :], ratio[:, :], ACT.Exp).then_inc(exp_done, 1)
                if tokens_sorted:
                    for q in range(len(preload["sources"])):
                        act.wait_ge(w_loaded[q % 2], 16 * (q // 2 + 1))
                        act.activation(half_of(preload["hi"], q), preload["w32"][:, q % 2, :], ACT.Copy).then_inc(w_hi_done, 1)

            @block.gpsimd
            def _(pool):
                pool.iota(rev[:, :, :], [[0, B], [-1, E]], base=E, channel_multiplier=0, allow_small_or_imprecise_dtypes=True).then_inc(rev_done, 1)
                if not tokens_sorted:
                    return
                pool.wait_ge(rev_done, 1)
                pool.iota(tile_row[:, :], [[P, NT]], base=0, channel_multiplier=0, allow_small_or_imprecise_dtypes=True).then_inc(rev_done, 1)
                pool.wait_ge(rev_done, 2)
                pool.memset(ones_tri[:, :], 1.0).then_inc(tri_done, 1)
                pool.wait_ge(tri_done, 1)
                pool.affine_select(out=ones_tri[:, :], in_=ones_tri[:, :], compare_op=ALU.is_gt, fill=0.0, base=0, pattern=[[1, P]], channel_multiplier=-1).then_inc(tri_done, 1)
                pool.iota(token[:, :], [[P, B]], base=0, channel_multiplier=1).then_inc(tri_done, 1)
                pool.memset(zeros_i[:, :], 0).then_inc(tri_done, 1)
                pool.wait_ge(tri_done, 4)
                first = tokens_sorted["first_slot"] // P
                pool.dma_start(n_dram[:, 0:first], token[:, 0:first]).then_inc(cleared, 16)
                pool.dma_start(n_dram[:, first:NT], zeros_i[:, first:NT]).then_inc(cleared, 16)
                pool.wait_ge(cleared, 32)
                pool.wait_ge(gone, 3)
                flat = n_dram.rearrange("p (b o) -> (p b) o", o=1)
                def scatter(turn, first):
                    if not first:
                        wait_apart(pool, scattered, 16 * 4 * TOP * turn, scatter_passed)
                    for k in range(TOP):
                        pool.tensor_copy(slot_now[:, k, :], slot[:, k, bass.ds(4 * turn, 4)]).then_inc(taken, 1)
                    pool.tensor_copy(token_now[:, :], token[:, bass.ds(4 * turn, 4)]).then_inc(taken, 1)
                    wait_apart(pool, taken, 3 * turn + 3, scatter_passed)
                    for k in range(TOP):
                        for b in range(4):
                            pool.indirect_dma_start(flat, bass.IndirectOffsetOnAxis(ap=slot_now[:, k, b:b + 1], axis=0), token_now[:, b:b + 1], None).then_inc(scattered, 16)

                scatter(0, True)
                with pool.Fori(1, B // 4) as turn:
                    scatter(turn, False)
                pool.wait_ge(scattered, 16 * B * TOP)
                pool.dma_start(slot_token[:, :], n_dram[:, :]).then_inc(listed, 16)
                pool.wait_ge(listed, 16)

            if tokens_sorted:
                @block.sync
                def _(sp):
                    for q in range(len(preload["sources"])):
                        load_matrix(sp, preload, q, w_loaded, w_lo_done)

                @block.tensor
                def _(pe):
                    pe.wait_ge(tri_done, 2)
                    pe.wait_ge(gone, 2)
                    v = both[:, :, :].rearrange("p b e -> p (b e)")
                    pe.matmul(PR[:, :], ones_tri[:, :], v, start=True, stop=True).then_inc(ranks_ready, 1)
                    pe.matmul(PC[:, :], tokens_sorted["ones"][:, :], v, start=True, stop=True).then_inc(ranks_ready, 1)
        clear_semaphores(nc, sems)


def expert_weights(nc, es, name, sources):
    NE = len(sources)

    def sb(n, shape, dt):
        return es.enter_context(nc.sbuf_tensor(f"{name}_{n}", shape, dt))

    return dict(sources=[w for pair in sources for w in pair], w32=sb("w32", [P, 2, KC * F], F32),
                hi=(sb("wu_hi", [P, NE, KC, F], F32R), sb("wd_hi", [P, NE, FC, D], F32R)),
                lo=(sb("wu_lo", [P, NE, KC, F], F32R), sb("wd_lo", [P, NE, FC, D], F32R)))


def half_of(halves, q):
    return halves[q % 2][:, q // 2, :, :].rearrange("p c n -> p (c n)")


def load_matrix(eng, W, q, loaded, split):
    if q >= 2:
        eng.wait_ge(split, q - 1)
    c = KC if q % 2 == 0 else FC
    eng.dma_start(W["w32"][:, q % 2, :].rearrange("p (c n) -> p c n", c=c), W["sources"][q].rearrange("(c p) n -> p c n", p=P)).then_inc(loaded[q % 2], 16)


def experts_phase(nc, name, rows, gather, tile_expert, weights, y_dst, n_tiles, ident, residual=None):
    NE = len(weights["sources"]) // 2
    with ExitStack() as es:
        def sb(n, shape, dt):
            return es.enter_context(nc.sbuf_tensor(f"{name}_{n}", shape, dt))

        def ps(n, shape, dt):
            return es.enter_context(nc.psum_tensor(f"{name}_{n}", shape, dt))

        sems = []

        def sem(n):
            sems.append(nc.alloc_semaphore(name=f"{name}_{n}"))
            return sems[-1]

        (wu_hi, wd_hi), (wu_lo, wd_lo) = weights["hi"], weights["lo"]
        x_in = sb("x_in", [P, 4, D], F32)
        xT_hi = sb("xT_hi", [P, 2, KC, P], F32R)
        xT_lo = sb("xT_lo", [P, 2, KC, P], F32R)
        hid = sb("hid", [P, 2, F], F32)
        hT_hi = sb("hT_hi", [P, 2, FC, P], F32R)
        hT_lo = sb("hT_lo", [P, 2, FC, P], F32R)
        y_out = sb("y_out", [P, 4, D], F32)
        gather_now = sb("gather_now", [P, 4], U32)
        if residual is not None:
            res = [sb(f"res{k}", [P, 2, D], F32) for k in range(2)]
            y_first = sb("y_first", [P, 2, D], F32)
            res_loaded = [sem(f"res_loaded{k}") for k in range(2)]
            res_added, pool_passed = sem("res_added"), sem("pool_passed")
        taken = sem("taken")
        PX = [ps(f"PX{k}", [P, T], F32) for k in range(2)]
        PH = [ps(f"PH{k}", [P, F], F32) for k in range(2)]
        PT = [ps(f"PT{k}", [P, F], F32) for k in range(2)]
        PY = [ps(f"PY{k}", [P, T], F32) for k in range(2)]
        x_loaded = [sem(f"x_loaded{k}") for k in range(4)]
        xT_ready, xT_hi_done, xT_lo_done = sem("xT_ready"), sem("xT_hi_done"), sem("xT_lo_done")
        h_ready, gelu_done, hT_ready, hT_hi_done, hT_lo_done = (
            sem("h_ready"), sem("gelu_done"), sem("hT_ready"), sem("hT_hi_done"), sem("hT_lo_done"))
        y_ready, y_copied = sem("y_ready"), sem("y_copied")
        y_stored = [sem(f"y_stored{k}") for k in range(4)]
        passed, pe_passed = sem("passed"), sem("pe_passed")
        STEP0, LOOP0, PER = -3, 6, 4
        turns = (n_tiles - 4 - LOOP0) // PER
        LOOP1 = LOOP0 + PER * turns

        def run(eng, program):
            for i in range(STEP0, LOOP0):
                program(i, None)
            with eng.Fori(0, turns) as turn:
                for i in range(LOOP0, LOOP0 + PER):
                    program(i, turn)
            for i in range(LOOP1, n_tiles + 4):
                program(i, None)

        def done(i, turn, per=1, c=0):
            return at(i, per * PER, turn, per * (i + 1) + c)

        def ring4(i, turn):
            return at(i, 16, turn, 16 * (i // 4 + 1))

        def valid(i, turn):
            return turn is not None or 0 <= i < n_tiles

        def off(turn):
            return 0 if turn is None else PER * turn

        with nc.Block() as block:

            @block.sync
            def _(sp):
                def program(i, turn):
                    if gather is None and valid(i + 3, turn):
                        wait_apart(sp, xT_ready, done(i - 1, turn), passed)
                        b = (i + 3) // TOP
                        sp.dma_start(x_in[:, (i + 3) % 4, :], rows[bass.ds(b + (0 if turn is None else PER // TOP * turn), 1)].rearrange("b t d -> t (b d)")
                                     ).then_inc(x_loaded[(i + 3) % 4], 16)
                    if residual is not None:
                        if i % TOP == 1 and valid(i + 1, turn):
                            b = (i + 1) // TOP
                            wait_apart(sp, y_copied, done(i - 3, turn), passed)
                            for k in range(2):
                                sp.dma_start(res[k][:, b % 2, :], residual[k][bass.ds(b + (0 if turn is None else PER // TOP * turn), 1)].rearrange("b t d -> t (b d)")
                                             ).then_inc(res_loaded[b % 2], 16)
                        if (i - 3) % TOP == 1 and valid(i - 3, turn):
                            b = (i - 3) // TOP
                            wait_apart(sp, y_copied, done(i - 3, turn), passed)
                            sp.dma_start(y_dst[bass.ds(b + (0 if turn is None else PER // TOP * turn), 1)].rearrange("b t d -> t (b d)"), y_out[:, b % 2, :]
                                         ).then_inc(y_stored[b % 2], 16)
                    elif valid(i - 3, turn):
                        wait_apart(sp, y_copied, done(i - 3, turn), passed)
                        sp.dma_start(y_dst[bass.ds(i - 3 + off(turn), 1)].rearrange("b t d -> t (b d)"), y_out[:, (i - 3) % 4, :]).then_inc(y_stored[(i - 3) % 4], 16)

                run(sp, program)
                for k in range(2 if residual is not None else 4):
                    sp.wait_ge(y_stored[k], 16 * (n_tiles // 4))

            if residual is not None:
                @block.gpsimd
                def _(pool):
                    def program(i, turn):
                        if i % TOP == 0 and valid(i, turn):
                            b = i // TOP
                            wait(pool, res_loaded[b % 2], at(i, 32, turn, 32 * (b // 2 + 1)))
                            pool.tensor_tensor(res[0][:, b % 2, :], res[0][:, b % 2, :], res[1][:, b % 2, :], ALU.add).then_inc(res_added, 1)

                    run(pool, program)

            if gather is not None:
                @block.gpsimd
                def _(pool):
                    def program(i, turn):
                        if valid(i + 3, turn):
                            wait_apart(pool, xT_ready, done(i - 1, turn), passed)
                            k = (i + 3) % 4
                            pool.tensor_copy(gather_now[:, k:k + 1], gather[:, bass.ds(i + 3 + off(turn), 1)]).then_inc(taken, 1)
                            wait_apart(pool, taken, done(i + 3, turn), passed)
                            pool.indirect_dma_start(x_in[:, k, :], None, rows.rearrange("b t d -> (b t) d"),
                                                    bass.IndirectOffsetOnAxis(ap=gather_now[:, k:k + 1], axis=0)).then_inc(x_loaded[k], 16)

                    run(pool, program)

            @block.tensor
            def _(pe):
                numbers = [pe.alloc_register(f"{name}_expert{k}") for k in range(4)]

                def load_expert(i, turn):
                    pe.reg_load(numbers[i % 4], tile_expert[0:1, bass.ds(i + off(turn), 1)])

                def expert(i):
                    return pe.snap(numbers[i % 4], min_val=0, max_val=NE - 1)

                def program(i, turn):
                    if valid(i, turn):
                        wait(pe, xT_lo_done, done(i, turn))
                        wait(pe, gelu_done, done(i - 2, turn))
                        for c in range(KC):
                            for z, (a, w) in enumerate(((xT_hi, wu_hi), (xT_hi, wu_lo), (xT_lo, wu_hi))):
                                last = pe.matmul(PH[i % 2][:, :], a[:, i % 2, c, :], w[:, bass.ds(expert(i), 1), c, :].rearrange("p o n -> p (o n)"),
                                                 start=(c == 0 and z == 0), stop=(c == KC - 1 and z == 2))
                        last.then_inc(h_ready, 1)
                    if valid(i + 1, turn):
                        k = (i + 1) % 2
                        wait(pe, x_loaded[(i + 1) % 4], ring4(i + 1, turn))
                        wait_apart(pe, xT_lo_done, done(i - 1, turn), pe_passed)
                        load_expert(i + 1, turn)
                        for c in range(KC):
                            last = pe.transpose(PX[k][:, c * P:(c + 1) * P], x_in[:, (i + 1) % 4, c * P:(c + 1) * P], ident[:, :])
                        last.then_inc(xT_ready, 1)
                    if valid(i - 1, turn):
                        wait(pe, gelu_done, done(i - 1, turn))
                        wait(pe, hT_lo_done, done(i - 3, turn))
                        for c in range(FC):
                            last = pe.transpose(PT[(i - 1) % 2][:, c * P:(c + 1) * P], hid[:, (i - 1) % 2, c * P:(c + 1) * P], ident[:, :])
                        last.then_inc(hT_ready, 1)
                    if valid(i - 2, turn):
                        k = i % 2
                        wait(pe, hT_lo_done, done(i - 2, turn))
                        wait(pe, y_copied, done(i - 4, turn))
                        for c in range(FC):
                            for z, (a, w) in enumerate(((hT_hi, wd_hi), (hT_hi, wd_lo), (hT_lo, wd_hi))):
                                last = pe.matmul(PY[k][:, 0:D], a[:, k, c, :], w[:, bass.ds(expert(i - 2), 1), c, :].rearrange("p o n -> p (o n)"),
                                                 start=(c == 0 and z == 0), stop=(c == FC - 1 and z == 2))
                        last.then_inc(y_ready, 1)

                run(pe, program)

            @block.scalar
            def _(act):
                def program(i, turn):
                    if valid(i, turn):
                        wait(act, hT_ready, done(i - 2, turn))
                        wait(act, h_ready, done(i, turn))
                        act.activation(hid[:, i % 2, :], PH[i % 2][:, :], ACT.Gelu).then_inc(gelu_done, 1)
                    if valid(i + 1, turn):
                        k = (i + 1) % 2
                        wait(act, xT_ready, done(i + 1, turn))
                        wait(act, h_ready, done(i - 1, turn))
                        act.activation(xT_hi[:, k, :, :].rearrange("p c t -> p (c t)"), PX[k][:, 0:D], ACT.Copy).then_inc(xT_hi_done, 1)
                    if valid(i - 1, turn):
                        k = (i - 1) % 2
                        wait(act, hT_ready, done(i - 1, turn))
                        wait(act, y_ready, done(i - 3, turn))
                        act.activation(hT_hi[:, k, :, :].rearrange("p c t -> p (c t)"), PT[k][:, :], ACT.Copy).then_inc(hT_hi_done, 1)

                run(act, program)

            @block.vector
            def _(dve):
                def program(i, turn):
                    if valid(i + 1, turn):
                        k = (i + 1) % 2
                        wait(dve, xT_hi_done, done(i + 1, turn))
                        dve.tensor_tensor(xT_lo[:, k, :, :].rearrange("p c t -> p (c t)"), PX[k][:, 0:D], xT_hi[:, k, :, :].rearrange("p c t -> p (c t)"),
                                          ALU.subtract).then_inc(xT_lo_done, 1)
                    if valid(i - 1, turn):
                        k = (i - 1) % 2
                        wait(dve, hT_hi_done, done(i - 1, turn))
                        dve.tensor_tensor(hT_lo[:, k, :, :].rearrange("p c t -> p (c t)"), PT[k][:, :], hT_hi[:, k, :, :].rearrange("p c t -> p (c t)"),
                                          ALU.subtract).then_inc(hT_lo_done, 1)
                    if valid(i - 2, turn) and residual is not None:
                        b, k = (i - 2) // TOP, i % TOP
                        factor = residual[2][:, bass.ds(b + (0 if turn is None else PER // TOP * turn), 1), k:k + 1].rearrange("p o n -> p (o n)")
                        if k == 0:
                            wait(dve, res_added, at(i, PER // TOP, turn, b + 1))
                        else:
                            wait(dve, y_stored[b % 2], at(i, 16, turn, 16 * (b // 2)))
                            wait(dve, y_copied, done(i - 3, turn))
                        wait_apart(dve, y_ready, done(i - 2, turn), pe_passed)
                        out, base = (y_first, res[0]) if k == 0 else (y_out, y_first)
                        dve.scalar_tensor_tensor(out[:, b % 2, :], PY[i % 2][:, 0:D], factor, base[:, b % 2, :], ALU.mult, ALU.add).then_inc(y_copied, 1)
                    elif valid(i - 2, turn):
                        wait(dve, y_ready, done(i - 2, turn))
                        wait(dve, y_stored[(i - 2) % 4], at(i, 16, turn, 16 * ((i - 2) // 4)))
                        dve.tensor_copy(y_out[:, (i - 2) % 4, :], PY[i % 2][:, 0:D]).then_inc(y_copied, 1)

                run(dve, program)
        clear_semaphores(nc, sems)


def combine_phase(nc, name, src, added_rows, y, dst, weights, place, B):
    with ExitStack() as es:
        def sb(n, shape, dt):
            return es.enter_context(nc.sbuf_tensor(f"{name}_{n}", shape, dt))

        sems = []

        def sem(n):
            sems.append(nc.alloc_semaphore(name=f"{name}_{n}"))
            return sems[-1]

        R4 = 4
        x = sb("x", [P, R4, D], F32)
        ysh = sb("ysh", [P, R4, D], F32)
        yk = sb("yk", [P, R4, TOP, D], F32)
        out = sb("out", [P, R4, D], F32)
        loaded = [sem(f"loaded{k}") for k in range(R4)]
        gathered = [sem(f"gathered{k}") for k in range(R4)]
        summed, added = sem("summed"), sem("added")
        stored = [sem(f"stored{k}") for k in range(R4)]
        passed = sem("passed")
        place_now = sb("place_now", [P, R4, TOP], U32)
        taken = sem("taken")
        NTURN = B // R4

        with nc.Block() as block:

            @block.sync
            def _(sp):
                def load(b, k):
                    sp.dma_start(x[:, k, :], src[bass.ds(b, 1)].rearrange("b t d -> t (b d)")).then_inc(loaded[k], 16)
                    sp.dma_start(ysh[:, k, :], added_rows[bass.ds(b, 1)].rearrange("b t d -> t (b d)")).then_inc(loaded[k], 16)
                    if place is None:
                        sp.dma_start(yk[:, k, :, :], y[bass.ds(b * TOP, TOP)].rearrange("b t d -> t b d")).then_inc(loaded[k], 16)

                def store(b, k, turn):
                    wait_apart(sp, added, R4 * turn + k + 1, passed)
                    sp.dma_start(dst[bass.ds(b, 1)].rearrange("b t d -> t (b d)"), out[:, k, :]).then_inc(stored[k], 16)

                for k in range(R4):
                    load(k, k)
                with sp.Fori(0, NTURN - 1) as turn:
                    for k in range(R4):
                        store(R4 * turn + k, k, turn)
                        load(R4 * turn + k + R4, k)
                for k in range(R4):
                    store(B - R4 + k, k, NTURN - 1)
                for k in range(R4):
                    sp.wait_ge(stored[k], 16 * NTURN)

            if place is not None:
                @block.gpsimd
                def _(pool):
                    flat = y.rearrange("b t d -> (b t) d")

                    def gather(b, k):
                        for q in range(TOP):
                            pool.tensor_copy(place_now[:, k, q:q + 1], place[:, q, bass.ds(b, 1)]).then_inc(taken, 1)
                        wait_apart(pool, taken, TOP * (b + 1), passed)
                        for q in range(TOP):
                            pool.indirect_dma_start(yk[:, k, q, :], None, flat, bass.IndirectOffsetOnAxis(ap=place_now[:, k, q:q + 1], axis=0)).then_inc(gathered[k], 16)

                    for k in range(R4):
                        gather(k, k)
                    with pool.Fori(0, NTURN - 1) as turn:
                        for k in range(R4):
                            wait_apart(pool, added, R4 * turn + k + 1, passed)
                            gather(R4 * turn + k + R4, k)

            @block.vector
            def _(dve):
                def add(turn, k, first):
                    dve.wait_ge(loaded[k], (32 if place is not None else 48) * (turn + 1))
                    if place is not None:
                        dve.wait_ge(gathered[k], 32 * (turn + 1))
                    if not first:
                        dve.wait_ge(stored[k], 16 * turn)
                    b = R4 * turn + k
                    dve.tensor_tensor(out[:, k, :], x[:, k, :], ysh[:, k, :], ALU.add).then_inc(summed, 1)
                    dve.wait_ge(summed, TOP * b + 1)
                    for q in range(TOP):
                        dve.scalar_tensor_tensor(out[:, k, :], yk[:, k, q, :], weights[:, bass.ds(b, 1), q:q + 1].rearrange("p o n -> p (o n)"), out[:, k, :], ALU.mult, ALU.add
                                                 ).then_inc(summed if q < TOP - 1 else added, 1)
                        if q < TOP - 1:
                            dve.wait_ge(summed, TOP * (b + 1))

                for k in range(R4):
                    add(0, k, True)
                with dve.Fori(1, NTURN) as turn:
                    for k in range(R4):
                        add(turn, k, False)
        clear_semaphores(nc, sems)


def program(nc, t, B):
    def scratch(n, shape, dt=F32):
        return nc.dram_tensor(n, shape, dt, kind="Internal").ap()

    x1, x2, x3, x4 = (scratch(f"x{k}_scratch", (B, P, D)) for k in range(1, 5))
    x3_normed = scratch("x3_normed_scratch", (B, P, D))
    normed = scratch("normed_scratch", (B, P, D))
    list_tiles = B * TOP + E
    n_tiles = B + list_tiles
    y_rows = scratch("expert_rows_scratch", (n_tiles, P, D))
    slots = scratch("slots_scratch", (P, n_tiles), U32)

    with ExitStack() as es:
        ident = es.enter_context(nc.sbuf_tensor("ident", [P, P], F32))
        identb = es.enter_context(nc.sbuf_tensor("identb", [P, P], BF16))
        ones = es.enter_context(nc.sbuf_tensor("ones", [P, P], F32))
        const_done = es.enter_context(nc.semaphore("const_done"))
        with nc.Block() as block:
            @block.gpsimd
            def _(pool):
                pool.memset(ident[:, :], 0.0).then_inc(const_done, 1)
                pool.wait_ge(const_done, 1)
                pool.affine_select(out=ident[:, :], in_=ident[:, :], compare_op=ALU.not_equal, fill=1.0, base=0, pattern=[[-1, P]],
                                   channel_multiplier=1).then_inc(const_done, 1)
                pool.wait_ge(const_done, 2)
                pool.tensor_copy(identb[:, :], ident[:, :]).then_inc(const_done, 1)
                pool.memset(ones[:, :], 1.0).then_inc(const_done, 1)

        attention_phase(nc, "xattn0", t["x"], t["ctx"], x1, [t["attn0"]], None, ident, identb, B)
        with ExitStack() as moe:
            logits = moe.enter_context(nc.sbuf_tensor("logits0", [P, B, E], F32))
            weights = moe.enter_context(nc.sbuf_tensor("weights0", [P, B, TOP], F32))
            place = moe.enter_context(nc.sbuf_tensor("place0", [P, TOP, B], U32))
            slot_token = moe.enter_context(nc.sbuf_tensor("slot_token0", [P, n_tiles], U32))
            tile_expert = moe.enter_context(nc.sbuf_tensor("tile_expert0", [1, n_tiles], I32))
            route_phase(nc, "route0", x1, normed, True, t["Wg"], None, None, None, logits, ident, ones, B)
            matrices = expert_weights(nc, moe, "experts0", [(t["Wu"][e], t["Wd"][e]) for e in range(E)] + [(t["W1"], t["W2"])])
            top_two_phase(nc, "top0", logits, weights, None, dict(
                slots=slots, place=place, slot_token=slot_token, tile_expert=tile_expert, tiles=n_tiles, first_slot=B * P, ones=ones), matrices, B)
            experts_phase(nc, "experts0", normed, slot_token, tile_expert,
                          matrices, y_rows, n_tiles, ident)
            combine_phase(nc, "combine0", x1, y_rows[0:B], y_rows, x2, weights, place, B)

        attention_phase(nc, "xattn1", x2, t["ctx"], x3, [t["attn1"]], None, ident, identb, B)
        route_phase(nc, "norm1", x3, x3_normed, True, None, None, None, None, None, ident, ones, B)
        attention_phase(nc, "mha", x3_normed, None, x4, [t["mha0"], t["mha1"]], t["router1"], ident, identb, B)
        with ExitStack() as moe:
            logits = moe.enter_context(nc.sbuf_tensor("logits1", [P, B, E], F32))
            weights = moe.enter_context(nc.sbuf_tensor("weights1", [P, B, TOP], F32))
            tile_expert = moe.enter_context(nc.sbuf_tensor("tile_expert1", [1, B * TOP], I32))
            matrices = expert_weights(nc, moe, "experts1", [(t["fw1"][e], t["fw2"][e]) for e in range(E)])
            route_phase(nc, "route1", x4, normed, False, t["ffn_rw"], t["ffn_rb"], t["ln2_g"], t["ln2_b"], logits, ident, ones, B, matrices)
            top_two_phase(nc, "top1", logits, weights, tile_expert, None, None, B)
            experts_phase(nc, "experts1", normed, None, tile_expert, matrices, t["out"], B * TOP, ident, (x4, x3, weights))


def kernel(**inputs):
    import numpy as np
    import concourse.bacc as bacc
    from concourse.bass_utils import run_bass_kernel_spmd

    a = {k: np.asarray(v) for k, v in inputs.items()}
    B = a["x"].shape[0]

    def headwise(w):
        return w.reshape(D, P // HD, KC, HD).transpose(0, 2, 3, 1).reshape(D, D)

    def headwise_bias(b):
        return b.reshape(P // HD, KC, HD).transpose(2, 0, 1).reshape(P, KC)

    def column(v):
        return v.reshape(KC, P).T

    def unit(name, wq, wk, wv, wo, bq, bk, bv, bo):
        return {f"{name}_wq": headwise(wq), f"{name}_wk": headwise(wk), f"{name}_wv": wv, f"{name}_wo": wo,
                f"{name}_bq": headwise_bias(bq), f"{name}_bk": headwise_bias(bk), f"{name}_bv": bv, f"{name}_bo": bo}

    w = {"x": a["x"], "ctx": a["ctx_1024"]}
    w.update(unit("attn0", a["L0_xattn_Wq"].T, a["L0_xattn_Wk"].T, a["L0_xattn_Wv"].T, a["L0_xattn_Wo"].T,
                  a["L0_xattn_bq"], a["L0_xattn_bk"], a["L0_xattn_bv"], a["L0_xattn_bo"]))
    proj, bias = a["L1_xattn_in_proj_w"], a["L1_xattn_in_proj_b"]
    w.update(unit("attn1", proj[:D].T, proj[D:2 * D].T, proj[2 * D:].T, a["L1_xattn_out_w"].T,
                  bias[:D], bias[D:2 * D], bias[2 * D:], a["L1_xattn_out_b"]))
    for m in range(2):
        w.update(unit(f"mha{m}", a["L1_ffn_mha_wq"][m].reshape(D, D), a["L1_ffn_mha_wk"][m].reshape(D, D),
                      a["L1_ffn_mha_wv"][m].reshape(D, D), a["L1_ffn_mha_wo"][m].reshape(D, D), a["L1_ffn_mha_bq"][m].reshape(D),
                      a["L1_ffn_mha_bk"][m].reshape(D), a["L1_ffn_mha_bv"][m].reshape(D), a["L1_ffn_mha_bo"][m]))
    for k in ("Wg", "Wu", "Wd", "W1", "W2"):
        w[k] = a["L0_ffn_" + k]
    w["ln1_g"], w["ln1_b"] = column(a["L1_ffn_ln1_g"]), column(a["L1_ffn_ln1_b"])
    for k in ("ln2_g", "ln2_b", "mha_rw", "mha_rb", "ffn_rw", "ffn_rb", "fw1", "fw2"):
        w[k] = a["L1_ffn_" + k]

    nc = bacc.Bacc("TRN2", target_bir_lowering=False, num_devices=1)
    arrays = {f"in_{k}": np.ascontiguousarray(v) for k, v in w.items()}
    t = {k: nc.dram_tensor(f"in_{k}", arrays[f"in_{k}"].shape, mybir.dt.from_np(arrays[f"in_{k}"].dtype), kind="ExternalInput").ap() for k in w}
    for u in ("attn0", "attn1", "mha0", "mha1"):
        t[u] = {k: t[f"{u}_{k}"] for k in ("wq", "wk", "wv", "wo", "bq", "bk", "bv", "bo")}
    t["router1"] = {"gamma": t["ln1_g"], "beta": t["ln1_b"], "rw": t["mha_rw"], "rb": t["mha_rb"]}
    t["out"] = nc.dram_tensor("out", (B, P, D), F32, kind="ExternalOutput").ap()
    program(nc, t, B)
    r = run_bass_kernel_spmd(nc, [arrays], core_ids=[0])
    return r.results[0]["out"]
```

```python
from contextlib import ExitStack

import concourse.bass as bass
from concourse import mybir

F32 = mybir.dt.float32
F32R = mybir.dt.float32r
BF16 = mybir.dt.bfloat16
I32 = mybir.dt.int32
U32 = mybir.dt.uint32
ALU = mybir.AluOpType
ACT = mybir.ActivationFunctionType
AX = mybir.AxisListType

P = 128
D = 256
H = 16
HD = D // H
KC = D // P
G = 4
T = G * P
TOP = 2
HB = 4
PARTS = 3
Q_SLOTS = (0, 1, 2, 0, 1, 0)
K_SLOTS = (0, 0, 0, 1, 1, 2)
ROWS = 16 * len(Q_SLOTS)
EPS_OUTER = 1e-5
EPS_INNER = 1e-6
NEWTON = 3
GUESS = 0x5F3759DF
LOOP_FIRST = 5
BODY = 8


def at(step, per_body, turn, const):
    return const if turn is None else const + per_body * turn


def wait(eng, sem, value):
    if isinstance(value, int) and value <= 0:
        return
    eng.wait_ge(sem, value)


def wait_apart(eng, sem, value, passed):
    wait(eng, sem, value)
    eng.sem_inc(passed, 1)


def clear_semaphores(nc, sems):
    nc.all_engine_barrier()
    nc.clear_and_free_semaphores(sems)
    nc.all_engine_barrier()


def steps(eng, n_steps, first_step, loop_first, program):
    turns = (n_steps + first_step - loop_first) // BODY
    last_loop = loop_first + turns * BODY
    for i in range(first_step, loop_first):
        program(i, None)
    with eng.Fori(0, turns) as turn:
        for i in range(loop_first, loop_first + BODY):
            program(i, turn)
    for i in range(last_loop, n_steps + 4):
        program(i, None)


def attention_phase(nc, name, src, context, dst, units, router, ident, identb, B, mix=None):
    U = len(units)
    NG = B // G
    NM = NG * U
    N = NM * G
    XR = 2 // U
    FILLS0 = [2, 3, 0, 1, 4, 5, 6, 7, 8, 9] if U == 1 else [0, 1, 4, 5, 6, 7, "R", 8, 9]
    FILLS1 = FILLS0 if U == 1 else [4, 5, 6, 7, 8, 9]
    FIRST_FILLS = [2, 3, 0, 1] if U == 1 else [2, 0, 1, 3]
    FPB = len(FILLS0) + len(FILLS1)
    GPB = 2 // U
    lead = U - 1
    mix_lead = G if mix is not None else 0
    first_step = -11 - lead - mix_lead
    loop_first = LOOP_FIRST - lead + (BODY if U == 2 else 0)

    def fidx(m, k):
        return FPB * (m // 2) + (len(FILLS0) if m % 2 else 0) + (FILLS1 if m % 2 else FILLS0).index(k)

    def has(m, k):
        return k in (FILLS1 if m % 2 else FILLS0)

    v_late = U == 2 or mix is not None

    def v_slot(m):
        return 2 if has(m, "R") else 0

    es = ExitStack()
    with es:
        def sb(n, shape, dt):
            return es.enter_context(nc.sbuf_tensor(f"{name}_{n}", shape, dt))

        def ps(n, shape, dt):
            return es.enter_context(nc.psum_tensor(f"{name}_{n}", shape, dt))

        sems = []

        def sem(n):
            sems.append(nc.alloc_semaphore(name=f"{name}_{n}"))
            return sems[-1]

        w32 = sb("w32", [P, 4, KC, D], F32)
        whi = sb("whi", [P, U, 4, KC, D], F32R)
        wlo = sb("wlo", [P, U, 4, KC, D], F32R)
        bq = sb("bq", [P, U, KC], F32)
        bk = sb("bk", [P, U, KC], F32)
        bv = sb("bv", [P, U, 2, D], F32)
        bo = sb("bo", [P, U, D], F32)

        x_in = sb("x_in", [P, XR, G, D], F32)
        if mix is not None:
            rows_in = sb("rows_in", [P, TOP, 2, D], F32)
            place_now = sb("place_now", [P, G, TOP], U32)
            place_taken, mixed = sem("place_taken"), sem("mixed")
            gathered = [sem(f"gathered{k}") for k in range(2)]
            mix_stored = [sem(f"mix_stored{k}") for k in range(2)]
        stats = sb("stats", [P, G, 6], F32)
        moments = sb("moments", [P, G, 2], F32)
        rstd = sb("rstd", [P, U, G], F32)
        var_eps = sb("var_eps", [P, U, G], F32)
        half_bits = sb("half_bits", [P, U, G], I32)
        square = sb("square", [P, U, G], F32)
        n_tok = sb("n_tok", [P, G, D], F32)
        nT_hi = sb("nT_hi", [P, KC, T], F32R)
        nT_lo = sb("nT_lo", [P, KC, T], F32R)
        if U == 1:
            ctx_in = sb("ctx_in", [P, 2, G, D], F32)
            cT_hi = sb("cT_hi", [P, KC, T], F32R)
            cT_lo = sb("cT_lo", [P, KC, T], F32R)
        else:
            cT_hi, cT_lo = nT_hi, nT_lo
            nT = sb("nT", [P, KC, T], F32)
            gamma = sb("gamma", [P, KC], F32)
            beta = sb("beta", [P, KC], F32)
            mean = sb("mean", [P, KC, G], F32)
            rw = sb("rw", [P, KC, U], F32)
            rb = sb("rb", [P, G, U], F32)
            logit = sb("logit", [P, G, U], F32)
            lmax = sb("lmax", [P, G], F32)
            lexp = sb("lexp", [P, G, U], F32)
            lsum = sb("lsum", [P, G], F32)
            p_new = sb("p_new", [P, G, U], F32)
            p_use = sb("p_use", [P, G, U], F32)
        parts = [sb("q_parts", [P, 2, KC, PARTS, T], BF16), sb("k_parts", [P, 2, KC, PARTS, T], BF16)]
        rest = sb("rest", [P, 2, T], F32)
        qs = sb("qs", [ROWS + PARTS, 2, H, T], BF16)
        ks = sb("ks", [ROWS + PARTS, 2, H, T], BF16)
        v_aug = sb("v_aug", [P, 2, G, H, 2 * HD], F32)
        nmax = sb("nmax", [P, 2, H], F32)
        mres = sb("mres", [P, 2, H], F32)
        one_row = sb("one_row", [PARTS, T // 4], BF16)
        mparts = sb("mparts", [P, 2, PARTS, H], BF16)
        mT = sb("mT", [PARTS * H, 2, P], BF16)
        probs = sb("probs", [P, 2, H, P], F32)
        o_un = sb("o_un", [P, H // HB, P], F32)
        o_rec = sb("o_rec", [P, H], F32)
        o_tok = sb("o_tok", [P, H, HD], F32)
        oT_hi = sb("oT_hi", [P, KC, P], F32R)
        oT_lo = sb("oT_lo", [P, KC, P], F32R)
        x_res = sb("x_res", [P, G, D], F32)
        y_bias = sb("y_bias", [P, D], F32)
        y_out = sb("y_out", [P, 2, D], F32)

        S = [ps(f"S{j}", [P, HB, P], F32) for j in range(2)]
        ST = [ps(f"ST{j}", [P, HB * P], F32) for j in range(2)]
        PO = ps("PO", [P, H // HB, P], F32)
        X = ps("X", [P, T], F32)
        R = [ps(f"R{j}", [P, T], F32) for j in range(2)]

        w_loaded = [sem(f"w_loaded{u}") for u in range(U)]
        b_loaded = sem("b_loaded")
        w_hi_done, w_lo_done, ones_done, ones_stacked = sem("w_hi_done"), sem("w_lo_done"), sem("ones_done"), sem("ones_stacked")
        x_loaded = [sem(f"x_loaded{k}") for k in range(XR)]
        ctx_loaded = [sem(f"ctx_loaded{k}") for k in range(2)]
        xr_loaded = [sem(f"xr_loaded{b}") for b in range(G)]
        ln_stats, ln_moments, ln_guess, newton_done, n_ready = sem("ln_stats"), sem("ln_moments"), sem("ln_guess"), sem("newton_done"), sem("n_ready")
        z_ready, z_stored = sem("z_ready"), sem("z_stored")
        fill_ready, fill_freed = sem("fill_ready"), sem("fill_freed")
        xT_hi_done, xT_lo_done = sem("xT_hi_done"), sem("xT_lo_done")
        part1_done, part2_done, part3_done = sem("part1_done"), sem("part2_done"), sem("part3_done")
        stacked = [[sem(f"stacked{k}{f}") for f in range(2)] for k in range(2)]
        s_ready, max_done, mpart_done, mT_ready, mT_done = (
            sem("s_ready"), sem("max_done"), sem("mpart_done"), sem("mT_ready"), sem("mT_done"))
        negmax_stacked = [sem(f"negmax_stacked{k}") for k in range(2)]
        st_ready, exp_done, pv_done, o_un_done = sem("st_ready"), sem("exp_done"), sem("pv_done"), sem("o_un_done")
        o_turned, o_rec_done, o_tok_done, oT_ready, oT_hi_done, oT_lo_done = (
            sem("o_turned"), sem("o_rec_done"), sem("o_tok_done"), sem("oT_ready"), sem("oT_hi_done"), sem("oT_lo_done"))
        y_ready, y_bias_done, y_done = sem("y_ready"), sem("y_bias_done"), sem("y_done")
        y_stored = [sem(f"y_stored{k}") for k in range(2)]
        sp_passed, pe_passed, dve_passed, pool_passed = sem("sp_passed"), sem("pe_passed"), sem("dve_passed"), sem("pool_passed")
        mean_done, rt_done, rt_exp_done, p_copied = sem("mean_done"), sem("rt_done"), sem("rt_exp_done"), sem("p_copied")

        GUESSES = 2 + U
        W_IN = 16 * 4
        B_IN = 16 * (4 * U + (4 if U == 2 else 0))
        STACK = 16 * 2 * len(Q_SLOTS)

        def ub(per, i, turn, c=0):
            return at(i, per * BODY, turn, per * i + c)

        def gr(per, m, turn, c=0):
            return at(m, per * GPB, turn, per * (m // U + 1) + c)

        def fl(m, k, turn, c=0):
            return at(m, FPB, turn, fidx(m, k) + 1 + c)

        def flat(tile):
            return tile[:, :, :].rearrange("p u b -> p (u b)")

        def ug_valid(m, turn):
            return turn is not None or 0 <= m < NM

        def ub_valid(i, turn):
            return turn is not None or 0 <= i < N

        def pos(turn, n):
            return 0 if turn is None else n * turn

        with nc.Block() as block:

            @block.sync
            def _(sp):
                for u, w in enumerate(units):
                    if u > 0:
                        sp.wait_ge(w_lo_done, u)
                    for k, key in enumerate(("wq", "wk", "wv", "wo")):
                        sp.dma_start(w32[:, k, :, :], w[key].rearrange("(c p) n -> p c n", p=P)).then_inc(w_loaded[u], 16)
                    sp.dma_start(bq[:, u, :], w["bq"]).then_inc(b_loaded, 16)
                    sp.dma_start(bk[:, u, :], w["bk"]).then_inc(b_loaded, 16)
                    sp.dma_start(bv[:, u, :, :], w["bv"].rearrange("(a b n) -> a b n", a=1, b=1).to_broadcast([P, 2, D])).then_inc(b_loaded, 16)
                    sp.dma_start(bo[:, u, :], w["bo"].rearrange("(a n) -> a n", a=1).to_broadcast([P, D])).then_inc(b_loaded, 16)
                if U == 2:
                    sp.dma_start(gamma[:, :], router["gamma"]).then_inc(b_loaded, 16)
                    sp.dma_start(beta[:, :], router["beta"]).then_inc(b_loaded, 16)
                    sp.dma_start(rw[:, :, :], router["rw"].rearrange("(c p) n -> p c n", p=P)).then_inc(b_loaded, 16)
                    sp.dma_start(rb[:, :, :], router["rb"].rearrange("(a b n) -> a b n", a=1, b=1).to_broadcast([P, G, U])).then_inc(b_loaded, 16)

                sp.wait_ge(ones_done, 1)
                rows = ks[ROWS:ROWS + PARTS, :, :, :].rearrange("p k h (c t) -> p (k h c) t", t=T // 4)
                sp.dma_start(rows, one_row[:, :].rearrange("p (o t) -> p o t", o=1).to_broadcast([PARTS, 2 * H * 4, T // 4])).then_inc(ones_stacked, 16)

                def program(i, turn):
                    if ub_valid(i + 1, turn):
                        k, b = (i + 1) // G % 2, (i + 1) % G
                        wait(sp, mT_done, ub(1, i + 2, turn))
                        sp.dma_start(qs[ROWS:ROWS + PARTS, k, :, b * P:(b + 1) * P], mT[:, (i + 1) % 2, :]).then_inc(negmax_stacked[(i + 1) % 2], 16)
                    mn = (i + 7 + lead) // G - 1
                    if U == 2 and (i + 7 + lead) % G == 0 and mn % U == 0 and ug_valid(mn, turn):
                        wait_apart(sp, z_ready, gr(G, mn, turn), sp_passed)
                        sp.dma_start(router["z"][bass.ds((mn // U) * G + pos(turn, GPB * G), G)].rearrange("b t d -> t b d"), x_in[:, 0, :, :]).then_inc(z_stored, 16)
                    m = (i + 9) // G
                    if mix is not None and (i + 9) % G == 0 and ug_valid(m, turn):
                        wait_apart(sp, mixed, at(m, 2 * G * TOP, turn, G * TOP * (m + 1)), sp_passed)
                        sp.dma_start(mix["dst"][bass.ds(m * G + pos(turn, 2 * G), G)].rearrange("b t d -> t b d"), x_in[:, m % 2, :, :]).then_inc(mix_stored[m % 2], 16)
                    m = (i + 11 + lead + mix_lead) // G
                    if (i + 11 + lead + mix_lead) % G == 0 and ug_valid(m, turn) and m % U == 0:
                        g = m // U
                        if mix is not None and m >= 2:
                            wait_apart(sp, mix_stored[m % 2], at(m, 16, turn, 16 * (m // 2)), sp_passed)
                        if U == 1:
                            wait_apart(sp, n_ready, gr(G, m, turn, -G * XR), sp_passed)
                        else:
                            wait_apart(sp, z_stored, gr(16, m, turn, -16), sp_passed)
                        sp.dma_start(x_in[:, g % XR, :, :], src[bass.ds(g * G + pos(turn, GPB * G), G)].rearrange("b t d -> t b d")).then_inc(x_loaded[g % XR], 16)
                    m = (i + 11) // G
                    if U == 1 and (i + 11) % G == 0 and ug_valid(m, turn):
                        if m >= 2:
                            wait_apart(sp, fill_ready, fl(m - 2, 3, turn), sp_passed)
                        sp.dma_start(ctx_in[:, m % 2, :, :], context[bass.ds(m * G + pos(turn, 2 * G), G)].rearrange("b t d -> t b d")).then_inc(ctx_loaded[m % 2], 16)
                    m, stage = (i + 5) // G, (i + 5) % G
                    if ug_valid(m, turn):
                        half, r = stage // 2, stage % 2
                        if m >= 2:
                            wait_apart(sp, st_ready, ub(4, 4 * m - 6 + 2 * half, turn), sp_passed)
                        wait(sp, part3_done, at(m, 8, turn, 4 * m + 2 * r + KC))
                        cols = slice(half * T // 2, (half + 1) * T // 2)
                        tile, slots = (qs, Q_SLOTS) if r == 0 else (ks, K_SLOTS)
                        for s, part in enumerate(slots):
                            sp.dma_start(tile[16 * s:16 * s + 16, m % 2, :, cols], parts[r][:, m % 2, :, part, cols]).then_inc(stacked[m % 2][half], 16)
                    if ub_valid(i, turn) and (i // G) % U == 0:
                        b, m = i % G, i // G
                        wait_apart(sp, y_done, ub(1, i - G + 1, turn), sp_passed)
                        if U == 2:
                            wait_apart(sp, z_stored, gr(16, m, turn), sp_passed)
                        if mix is not None:
                            wait_apart(sp, mix_stored[m % 2], at(m, 16, turn, 16 * (m // 2 + 1)), sp_passed)
                        residual = router["z"] if U == 2 else src if mix is None else mix["dst"]
                        sp.dma_start(x_res[:, b, :], residual[bass.ds((m // U) * G + b + pos(turn, GPB * G), 1)].rearrange("b t d -> t (b d)")).then_inc(xr_loaded[b], 16)
                    if ub_valid(i - 3, turn) and ((i - 3) // G) % U == U - 1:
                        b, m = (i - 3) % G, (i - 3) // G
                        wait_apart(sp, y_done, ub(1, i - 2, turn), sp_passed)
                        sp.dma_start(dst[bass.ds((m // U) * G + b + pos(turn, GPB * G), 1)].rearrange("b t d -> t (b d)"), y_out[:, b % 2, :]).then_inc(y_stored[b % 2], 16)

                steps(sp, N, first_step, loop_first, program)
                for k in range(2):
                    sp.wait_ge(y_stored[k], 16 * B // 2)

            @block.tensor
            def _(pe):
                pe.wait_ge(w_lo_done, U)
                pe.wait_ge(ones_done, 2)
                pe.wait_ge(ones_stacked, 16)

                def product(out, pairs, first=True):
                    n = 3 * len(pairs)
                    last = None
                    for q, ((ahi, alo), (bhi, blo)) in enumerate(pairs):
                        for z, (a, b_) in enumerate(((ahi, bhi), (ahi, blo), (alo, bhi))):
                            last = pe.matmul(out, a, b_, start=(q == 0 and z == 0), stop=(q == len(pairs) - 1 and z == 2))
                    return last

                def fill(m, k, turn):
                    if not ug_valid(m, turn) or not has(m, k):
                        return
                    u = m % U
                    f = fidx(m, k)
                    r = R[f % FPB % 2]
                    back = 1 if (U == 2 and f % FPB == 0) else 2
                    wait(pe, fill_freed, fl(m, k, turn, -back))
                    if k in (0, 1):
                        wait(pe, n_ready, gr(G, m, turn))
                        for b in range(G):
                            last = pe.transpose(r[:, b * P:(b + 1) * P], n_tok[:, b, k * P:(k + 1) * P], ident[:, :])
                    elif k in (2, 3):
                        wait(pe, ctx_loaded[m % 2], at(m, 16, turn, 16 * (m // 2 + 1)))
                        for b in range(G):
                            last = pe.transpose(r[:, b * P:(b + 1) * P], ctx_in[:, m % 2, b, (k - 2) * P:(k - 1) * P], ident[:, :])
                    elif k in (4, 5, 6, 7):
                        t, c = (k - 4) // 2, k % 2
                        if U == 1:
                            wait(pe, fill_freed, fl(m, 1, turn))
                        else:
                            wait(pe, xT_lo_done, gr(2, m, turn))
                        hi, lo = (nT_hi, nT_lo) if t == 0 else (cT_hi, cT_lo)
                        last = product(r[:, :], [((whi[:, u, t, kc, c * P:(c + 1) * P], wlo[:, u, t, kc, c * P:(c + 1) * P]),
                                                  (hi[:, kc, :], lo[:, kc, :])) for kc in range(KC)])
                    elif k == "R":
                        wait(pe, mean_done, gr(2, m, turn))
                        for b in range(G):
                            for kc in range(KC):
                                last = pe.matmul(r[:, b * U:(b + 1) * U], mean[:, kc, b:b + 1].to_broadcast([P, P]), rw[:, kc, :],
                                                 start=(kc == 0), stop=(kc == KC - 1))
                    else:
                        for j in range(2):
                            b = 2 * (k - 8) + j
                            last = product(r[:, j * D:(j + 1) * D], [((cT_hi[:, kc, b * P:(b + 1) * P], cT_lo[:, kc, b * P:(b + 1) * P]),
                                                                     (whi[:, u, 2, kc, :], wlo[:, u, 2, kc, :])) for kc in range(KC)])
                    last.then_inc(fill_ready, 1)

                def scores(i, j, turn):
                    k, b = i // G % 2, i % G
                    m = i // G
                    if b % 2 == 0 and j == 0:
                        wait(pe, stacked[k][b // 2], at(m, STACK, turn, STACK * (m // 2 + 1)))
                    wait(pe, max_done, ub(4, i, turn, j - 1))
                    for h in range(HB * j, HB * j + HB):
                        last = pe.matmul(S[j % 2][:, h % HB, :], qs[0:ROWS, k, h, b * P:(b + 1) * P], ks[0:ROWS, k, h, b * P:(b + 1) * P],
                                         start=True, stop=True)
                    last.then_inc(s_ready, 1)

                def scores_turned(i, j, turn):
                    k, b = i // G % 2, i % G
                    if j == 0:
                        wait(pe, negmax_stacked[i % 2], at(i, 16 * BODY // 2, turn, 16 * (i // 2 + 1)))
                    wait(pe, exp_done, ub(4, i, turn, j - 1))
                    for h in range(HB * j, HB * j + HB):
                        last = pe.matmul(ST[j % 2][:, (h % HB) * P:(h % HB + 1) * P], ks[:, k, h, b * P:(b + 1) * P], qs[:, k, h, b * P:(b + 1) * P],
                                         start=True, stop=True)
                    last.then_inc(st_ready, 1)

                def weigh(i, j, turn):
                    k, b, m = i // G % 2, i % G, i // G
                    if j == 0:
                        wait(pe, o_un_done, ub(1, i, turn))
                        wait(pe, fill_freed, fl(m, 8 + b // 2, turn))
                    wait(pe, exp_done, ub(4, i, turn, j + 1))
                    for q in range(HB):
                        h = HB * j + q
                        last = pe.matmul(PO[32 * q:32 * q + 32, j, :], v_aug[:, k, b, h, :], probs[:, i % 2, h, :], start=True, stop=True)
                    last.then_inc(pv_done, 1)

                def turn_normalised(i, turn):
                    d = i - 2
                    wait(pe, o_tok_done, ub(1, d + 1, turn))
                    if ub_valid(i + 1, turn):
                        wait(pe, mT_done, ub(1, i + 2, turn))
                    for c in range(KC):
                        last = pe.transpose(X[:, c * P:(c + 1) * P], o_tok[:, 8 * c:8 * c + 8, :].rearrange("p h d -> p (h d)"), ident[:, :])
                    last.then_inc(oT_ready, 1)

                def program(i, turn):
                    d = i - 2
                    m, r = (i + 7) // G, (i + 7) % G
                    for j in range(4):
                        if ub_valid(i + 2, turn):
                            scores(i + 2, j, turn)
                        if ub_valid(i, turn):
                            scores_turned(i, j, turn)
                        if j == 2 and ub_valid(d, turn) and r not in (1, 2):
                            turn_normalised(i, turn)
                        if j == 0 and ub_valid(d, turn):
                            wait(pe, o_un_done, ub(1, d + 1, turn))
                            if ub_valid(i, turn):
                                wait(pe, mT_done, ub(1, i + 1, turn))
                            wait(pe, y_bias_done, ub(1, d, turn))
                            for q in range(H // HB):
                                last = pe.transpose(X[:, q * P:(q + 1) * P], o_un[:, q, :], ident[:, :])
                            last.then_inc(o_turned, 1)
                        if j == 1 and ub_valid(i + 1, turn):
                            wait(pe, mpart_done, ub(4, i + 2, turn))
                            wait(pe, mT_done, ub(1, i + 1, turn))
                            wait_apart(pe, o_tok_done, ub(1, d + 1, turn), pe_passed)
                            pe.transpose(X[0:PARTS * H, 0:P // 2].bitcast(BF16), mparts[:, (i + 1) % 2, :, :].rearrange("p a h -> p (a h)"),
                                         identb[:, :]).then_inc(mT_ready, 1)
                        if ub_valid(i - 1, turn):
                            weigh(i - 1, j, turn)
                        if j == 2 and ub_valid(d, turn) and r in (1, 2):
                            turn_normalised(i, turn)
                        if r == 0:
                            if j == 0 and v_late:
                                fill(m - 1, 9, turn)
                            fill(m, FIRST_FILLS[j], turn)
                        elif r in (1, 2) and j in (0, 2):
                            fill(m, 2 + 2 * r + j // 2, turn)
                        elif r == 3 and j == 0 and has(m, "R"):
                            fill(m, "R", turn)
                        elif r == 3 and j == v_slot(m):
                            fill(m, 8, turn)
                        if j == 3 and ub_valid(d, turn):
                            wait(pe, oT_lo_done, ub(1, d + 1, turn))
                            u = (d // G) % U
                            product(X[:, 0:D], [((oT_hi[:, kc, :], oT_lo[:, kc, :]), (whi[:, u, 3, kc, :], wlo[:, u, 3, kc, :]))
                                                for kc in range(KC)]).then_inc(y_ready, 1)
                        if r == 3 and j == 3 and not v_late:
                            fill(m, 9, turn)

                steps(pe, N, first_step, loop_first, program)

            @block.scalar
            def _(act):
                for u in range(U):
                    act.wait_ge(w_loaded[u], W_IN)
                    act.activation(whi[:, u, :, :, :].rearrange("p k c n -> p (k c n)"), w32[:, :, :, :].rearrange("p k c n -> p (k c n)"),
                                   ACT.Copy).then_inc(w_hi_done, 1)
                act.wait_ge(b_loaded, B_IN)

                def fill_out(m, k, turn):
                    if not ug_valid(m, turn) or not has(m, k):
                        return
                    u = m % U
                    r = R[fidx(m, k) % FPB % 2]
                    if k in (0, 1, 2, 3):
                        if U == 1:
                            hi = nT_hi if k < 2 else cT_hi
                            wait(act, fill_ready, fl(m, k, turn))
                            act.activation(hi[:, k % 2, :], r[:, :], ACT.Copy).then_inc(xT_hi_done, 1)
                        else:
                            wait(act, fill_freed, fl(m, k, turn))
                            act.activation(nT_hi[:, k, :], nT[:, k, :], ACT.Copy).then_inc(xT_hi_done, 1)
                    elif k in (4, 5, 6, 7):
                        t, c = (k - 4) // 2, k % 2
                        bias = (bq, bk)[t]
                        if m >= 2:
                            for half in range(2):
                                wait(act, stacked[m % 2][half], at(m, STACK, turn, STACK * (m // 2)))
                        wait(act, fill_ready, fl(m, k, turn))
                        act.activation(parts[t][:, m % 2, c, 0, :], r[:, :], ACT.Identity, bias=bias[:, u, c:c + 1]).then_inc(part1_done, 1)

                def part2(m, k, turn):
                    if not ug_valid(m, turn):
                        return
                    t, c = (k - 4) // 2, k % 2
                    wait(act, fill_freed, fl(m, k, turn))
                    act.activation(parts[t][:, m % 2, c, 1, :], rest[:, k % 2, :], ACT.Copy).then_inc(part2_done, 1)

                def program(i, turn):
                    m, r = (i + 7) // G, (i + 7) % G
                    for j in range(4):
                        if ub_valid(i, turn):
                            wait(act, st_ready, ub(4, i, turn, j + 1))
                            wait(act, pv_done, ub(4, i - 2, turn, j + 1))
                            act.activation(probs[:, i % 2, HB * j:HB * j + HB, :].rearrange("p h q -> p (h q)"), ST[j % 2][:, :], ACT.Exp,
                                           scale=float(HD) ** -0.5).then_inc(exp_done, 1)
                        if j == 3 and ub_valid(i - 1, turn):
                            wait(act, pv_done, ub(4, i, turn))
                            wait(act, o_turned, ub(1, i - 1, turn))
                            act.activation(o_un[:, :, :].rearrange("p c t -> p (c t)"), PO[:, :, :].rearrange("p c t -> p (c t)"), ACT.Copy).then_inc(o_un_done, 1)
                        if j == 2 and ub_valid(i - 2, turn):
                            wait(act, oT_ready, ub(1, i - 1, turn))
                            act.activation(oT_hi[:, :, :].rearrange("p c t -> p (c t)"), X[:, 0:D], ACT.Copy).then_inc(oT_hi_done, 1)
                        if j == 1 and ub_valid(i + 1, turn):
                            wait(act, mT_ready, ub(1, i + 2, turn))
                            wait(act, negmax_stacked[(i + 1) % 2], at(i, 16 * BODY // 2, turn, 16 * ((i + 1) // 2)))
                            act.activation(mT[:, (i + 1) % 2, :], X[0:PARTS * H, 0:P // 2].bitcast(BF16), ACT.Copy).then_inc(mT_done, 1)
                        if r == 0:
                            if U == 1 or j > 0:
                                fill_out(m, FIRST_FILLS[j - (U - 1)], turn)
                        elif r in (1, 2):
                            k = 2 + 2 * r + j // 2
                            if j in (0, 2):
                                fill_out(m, k, turn)
                            else:
                                part2(m, k, turn)
                        elif r == 3 and j == 2 and has(m, "R") and ug_valid(m, turn):
                            wait(act, rt_done, gr(4, m, turn, -1))
                            act.activation(lexp[:, :, :], logit[:, :, :], ACT.Exp).then_inc(rt_exp_done, 1)

                steps(act, N, first_step, loop_first, program)

            @block.vector
            def _(dve):
                for u in range(U):
                    dve.wait_ge(w_hi_done, u + 1)
                    dve.tensor_tensor(wlo[:, u, :, :, :].rearrange("p k c n -> p (k c n)"), w32[:, :, :, :].rearrange("p k c n -> p (k c n)"),
                                      whi[:, u, :, :, :].rearrange("p k c n -> p (k c n)"), ALU.subtract).then_inc(w_lo_done, 1)
                dve.wait_ge(b_loaded, B_IN)

                def add_rows(m, b, q, turn):
                    if q == 0:
                        wait(dve, x_loaded[m % 2], at(m, 16, turn, 16 * (m // 2 + 1)))
                        wait(dve, gathered[b % 2], at(m, G * 16 * TOP, turn, 16 * TOP * ((G * m + b) // 2 + 1)))
                    else:
                        wait(dve, mixed, at(m, 2 * G * TOP, turn, TOP * (G * m + b) + 1))
                    factor = mix["weights"][:, bass.ds(G * m + b + pos(turn, 2 * G), 1), q:q + 1].rearrange("p o n -> p (o n)")
                    x = x_in[:, m % 2, b, :]
                    dve.scalar_tensor_tensor(x, rows_in[:, q, b % 2, :], factor, x, ALU.mult, ALU.add).then_inc(mixed, 1)

                def statistics(m, b0, turn):
                    g = m // U
                    if mix is not None:
                        wait(dve, mixed, at(m, 2 * G * TOP, turn, TOP * (G * m + b0 + 2)))
                    elif b0 == 0:
                        wait(dve, x_loaded[g % XR], at(m, 16, turn, 16 * (g // XR + 1)))
                    for b in range(b0, b0 + 2):
                        dve.bn_stats(stats[:, b, :], x_in[:, g % XR, b, :]).then_inc(ln_stats, 1)

                def guess(m, j, turn):
                    if j == 0:
                        wait(dve, n_ready, gr(G, m, turn, -G))
                        if U == 2:
                            wait(dve, z_ready, gr(G, m, turn, -G))
                        for b in range(G):
                            wait_apart(dve, ln_stats, gr(G, m, turn, b + 1 - G), dve_passed)
                            dve.bn_aggr(moments[:, b, :], stats[:, b, :]).then_inc(ln_moments, 1)
                    elif j == 1:
                        wait(dve, ln_moments, gr(G, m, turn))
                        var = moments[:, :, 1:2].rearrange("p b o -> p (b o)")
                        last = dve.tensor_scalar(var_eps[:, 0, :], var, EPS_OUTER, None, ALU.add)
                        if U == 2:
                            last.then_inc(ln_guess, 1)
                            last = dve.tensor_scalar(var_eps[:, 1, :], var, 1.0 + EPS_INNER, EPS_OUTER * EPS_INNER, ALU.mult, ALU.add)
                        last.then_inc(ln_guess, 1)
                    elif j == 2:
                        wait(dve, ln_guess, gr(GUESSES, m, turn, -2))
                        dve.tensor_scalar(flat(half_bits), flat(var_eps).bitcast(I32), 1, None, ALU.logical_shift_right).then_inc(ln_guess, 1)
                    else:
                        wait(dve, ln_guess, gr(GUESSES, m, turn, -1))
                        dve.tensor_scalar(flat(rstd).bitcast(I32), flat(half_bits), -1, GUESS, ALU.mult, ALU.add).then_inc(ln_guess, 1)

                def normalise(m, b0, turn):
                    g = m // U
                    wait(dve, newton_done, gr(4 * NEWTON, m, turn))
                    if m >= U:
                        wait(dve, fill_ready, fl(m - U, 1, turn))
                    for b in range(b0, b0 + 2):
                        dve.tensor_scalar(n_tok[:, b, :], x_in[:, g % XR, b, :], moments[:, b, 0:1], rstd[:, U - 1, b:b + 1],
                                          ALU.subtract, ALU.mult).then_inc(n_ready, 1)

                def fill_out(m, k, turn):
                    if not ug_valid(m, turn) or not has(m, k):
                        return
                    u = m % U
                    r = R[fidx(m, k) % FPB % 2]
                    if k in (0, 1, 2, 3):
                        if U == 1:
                            hi, lo = (nT_hi, nT_lo) if k < 2 else (cT_hi, cT_lo)
                            wait(dve, xT_hi_done, gr(4, m, turn, FILLS0.index(k) - 3))
                            dve.tensor_tensor(lo[:, k % 2, :], r[:, :], hi[:, k % 2, :], ALU.subtract).then_inc(fill_freed, 1)
                        else:
                            wait(dve, fill_ready, fl(m, k, turn))
                            wait(dve, xT_lo_done, gr(2, m, turn, -2))
                            dve.tensor_scalar(nT[:, k, :], r[:, :], gamma[:, k:k + 1], beta[:, k:k + 1], ALU.mult, ALU.add).then_inc(fill_freed, 1)
                    elif k in (4, 5, 6, 7):
                        t, c = (k - 4) // 2, k % 2
                        bias = (bq, bk)[t]
                        wait(dve, part1_done, at(m, 8, turn, 4 * m + k - 3))
                        wait(dve, part3_done, at(m, 8, turn, 4 * m + k - 5))
                        dve.scalar_tensor_tensor(rest[:, k % 2, :], r[:, :], bias[:, u, c:c + 1], parts[t][:, m % 2, c, 0, :],
                                                 ALU.add, ALU.subtract).then_inc(fill_freed, 1)
                    elif k == "R":
                        wait(dve, fill_ready, fl(m, k, turn))
                        dve.scalar_tensor_tensor(logit[:, :, :].rearrange("p b u -> p (b u)"), r[:, 0:G * U], 1.0 / P,
                                                 rb[:, :, :].rearrange("p b u -> p (b u)"), ALU.mult, ALU.add).then_inc(fill_freed, 1)
                        wait(dve, fill_freed, fl(m, k, turn))
                        dve.tensor_reduce(lmax[:, :], logit[:, :, :], AX.X, ALU.max).then_inc(rt_done, 1)
                        wait(dve, rt_done, gr(4, m, turn, -3))
                        dve.tensor_tensor(lexp[:, :, :], logit[:, :, :], lmax[:, :].rearrange("p (b o) -> p b o", o=1).to_broadcast([P, G, U]),
                                          ALU.subtract).then_inc(rt_done, 1)
                        wait(dve, rt_done, gr(4, m, turn, -2))
                        dve.tensor_copy(logit[:, :, :], lexp[:, :, :]).then_inc(rt_done, 1)
                    else:
                        wait(dve, fill_ready, fl(m, k, turn))
                        b = 2 * (k - 8)
                        if m >= 2:
                            wait(dve, pv_done, ub(4, 4 * m - 6 + b, turn))
                        dve.tensor_tensor(v_aug[:, m % 2, b:b + 2, :, 0:HD], r[:, :].rearrange("p (b h d) -> p b h d", b=2, h=H),
                                          bv[:, u, :, :].rearrange("p b (h d) -> p b h d", h=H), ALU.add).then_inc(fill_freed, 1)

                def unit_weights(m, turn):
                    wait(dve, rt_exp_done, gr(1, m, turn))
                    dve.tensor_reduce(lsum[:, :], lexp[:, :, :], AX.X, ALU.add).then_inc(rt_done, 1)
                    wait(dve, rt_done, gr(4, m, turn))
                    wait(dve, p_copied, gr(3, m, turn, -3))
                    dve.reciprocal(lmax[:, :], lsum[:, :]).then_inc(p_copied, 1)
                    wait(dve, p_copied, gr(3, m, turn, -2))
                    dve.tensor_tensor(p_new[:, :, :], lexp[:, :, :], lmax[:, :].rearrange("p (b o) -> p b o", o=1).to_broadcast([P, G, U]),
                                      ALU.mult).then_inc(p_copied, 1)

                def maximum(i, j, turn):
                    wait(dve, s_ready, ub(4, i, turn, j + 1))
                    if j == 0:
                        wait(dve, mpart_done, ub(4, i - 1, turn))
                    dve.tensor_reduce(nmax[:, i % 2, HB * j:HB * j + HB], S[j % 2][:, :, :], AX.X, ALU.max, negate=True).then_inc(max_done, 1)

                def program(i, turn):
                    m, r = (i + 7) // G, (i + 7) % G
                    d = i - 2
                    u, b = (d // G) % U, d % G
                    for j in range(4):
                        if ub_valid(i + 2, turn) and j < 3:
                            maximum(i + 2, j, turn)
                        if ub_valid(d, turn):
                            if j == 0:
                                wait(dve, o_turned, ub(1, d + 1, turn))
                                xv = X[:, :].rearrange("p (h e) -> p h e", h=H)
                                dve.reciprocal(o_rec[:, :].rearrange("p (h o) -> p h o", o=1), xv[:, :, HD:HD + 1]).then_inc(o_rec_done, 1)
                                wait(dve, o_rec_done, ub(1, d + 1, turn))
                                dve.tensor_tensor(o_tok[:, :, :], xv[:, :, 0:HD], o_rec[:, :].rearrange("p (h o) -> p h o", o=1).to_broadcast([P, H, HD]),
                                                  ALU.mult).then_inc(o_tok_done, 1)
                            elif j == 2:
                                wait(dve, oT_hi_done, ub(1, d + 1, turn))
                                dve.tensor_tensor(oT_lo[:, :, :].rearrange("p c t -> p (c t)"), X[:, 0:D], oT_hi[:, :, :].rearrange("p c t -> p (c t)"),
                                                  ALU.subtract).then_inc(oT_lo_done, 1)
                            elif j == 3:
                                wait(dve, y_ready, ub(1, d + 1, turn))
                                wait(dve, y_done, ub(1, d, turn))
                                dve.tensor_tensor(y_bias[:, :], X[:, 0:D], bo[:, u, :], ALU.add).then_inc(y_bias_done, 1)
                            if j == 3 and U == 2:
                                if u == 0 and b == 0:
                                    wait(dve, p_copied, gr(3, d // G, turn, -1))
                                    wait(dve, y_done, ub(1, d, turn))
                                    dve.tensor_copy(p_use[:, :, :], p_new[:, :, :]).then_inc(p_copied, 1)
                                if b == 0 and u == 0:
                                    wait(dve, p_copied, gr(3, d // G, turn))
                                wait(dve, y_bias_done, ub(1, d + 1, turn))
                                if u == 0:
                                    wait(dve, xr_loaded[b], gr(16, d // G, turn))
                                else:
                                    wait(dve, y_stored[b % 2], at(d, 32, turn, 16 * (2 * (d // 8) + b // 2)))
                                    wait(dve, y_done, ub(1, d - 3, turn))
                                out = x_res[:, b, :] if u == 0 else y_out[:, b % 2, :]
                                dve.scalar_tensor_tensor(out, y_bias[:, :], p_use[:, b, u:u + 1], x_res[:, b, :], ALU.mult, ALU.add).then_inc(y_done, 1)
                        if ub_valid(i + 2, turn) and j == 3:
                            maximum(i + 2, j, turn)
                        mn, rn = (i + 7 + lead) // G, (i + 7 + lead) % G
                        if mn % U == 0 and ug_valid(mn, turn) and rn == 0 and j == U - 1:
                            normalise(mn, 2, turn)
                        if r == 0:
                            if j == 0 and v_late:
                                fill_out(m - 1, 9, turn)
                            fill_out(m, FIRST_FILLS[j], turn)
                        elif r in (1, 2) and j in (0, 2):
                            fill_out(m, 2 + 2 * r + j // 2, turn)
                        elif r == 1 and j == 1 and U == 2 and ug_valid(m, turn) and m % 2 == 0:
                            if m >= U:
                                wait(dve, fill_ready, fl(m - U, "R", turn))
                            for c in range(KC):
                                dve.tensor_reduce(mean[:, c, :], nT[:, c, :].rearrange("p (b t) -> p b t", b=G), AX.X, ALU.add).then_inc(mean_done, 1)
                        elif r == 3 and j == v_slot(m):
                            fill_out(m, 8, turn)
                        elif r == 3 and U == 2 and ug_valid(m, turn) and m % 2 == 0:
                            if j == 0:
                                fill_out(m, "R", turn)
                            elif j == 3:
                                unit_weights(m, turn)
                        if r == 3 and j == 3 and not v_late:
                            fill_out(m, 9, turn)
                        mm, bm = (i + 14) // G, (i + 14) % G
                        if mix is not None and j in (1, 3) and ug_valid(mm, turn):
                            add_rows(mm, bm, j // 3, turn)
                        if (mn + 1) % U == 0 and ug_valid(mn + 1, turn):
                            if rn == 1 and j in (1, 3):
                                statistics(mn + 1, j - 1, turn)
                            elif rn == 2:
                                guess(mn + 1, j, turn)
                            elif rn == 3 and j == 3:
                                normalise(mn + 1, 0, turn)

                steps(dve, N, first_step, loop_first, program)

            @block.gpsimd
            def _(pool):
                pool.memset(one_row[:, :], 1.0).then_inc(ones_done, 1)
                pool.wait_ge(ones_done, 1)
                pool.memset(v_aug[:, :, :, :, HD:2 * HD], 1.0).then_inc(ones_done, 1)
                pool.wait_ge(ones_done, 2)

                def rstd_newton(m, turn):
                    done = 0

                    def stepped(instruction):
                        nonlocal done
                        done += 1
                        instruction.then_inc(newton_done, 1)
                        wait_apart(pool, newton_done, gr(4 * NEWTON, m, turn, done - 4 * NEWTON), pool_passed)

                    wait(pool, ln_guess, gr(GUESSES, m, turn))
                    for _ in range(NEWTON):
                        stepped(pool.tensor_tensor(flat(square), flat(rstd), flat(rstd), ALU.mult))
                        stepped(pool.tensor_tensor(flat(square), flat(square), flat(var_eps), ALU.mult))
                        stepped(pool.tensor_scalar(flat(square), flat(square), -0.5, 1.5, ALU.mult, ALU.add))
                        stepped(pool.tensor_tensor(flat(rstd), flat(rstd), flat(square), ALU.mult))

                def part3(m, r, c, turn):
                    if r in (1, 2) and ug_valid(m, turn):
                        wait(pool, part2_done, at(m, 8, turn, 4 * m + 2 * (r - 1) + c + 1))
                        pool.tensor_tensor(parts[r - 1][:, m % 2, c, 2, :], rest[:, c, :], parts[r - 1][:, m % 2, c, 1, :],
                                           ALU.subtract).then_inc(part3_done, 1)

                def program(i, turn):
                    m, r = (i + 7) // G, (i + 7) % G
                    mg, b = (i + 15) // G, (i + 15) % G
                    if mix is not None and ug_valid(mg, turn):
                        wait_apart(pool, mixed, at(mg, 2 * G * TOP, turn, TOP * (G * mg + b - 1)), pool_passed)
                        for q in range(TOP):
                            pool.tensor_copy(place_now[:, b, q:q + 1], mix["place"][:, q, bass.ds(G * mg + b + pos(turn, 2 * G), 1)]).then_inc(place_taken, 1)
                        wait_apart(pool, place_taken, at(mg, 2 * G * TOP, turn, TOP * (G * mg + b + 1)), pool_passed)
                        for q in range(TOP):
                            pool.indirect_dma_start(rows_in[:, q, b % 2, :], None, mix["rows"].rearrange("b t d -> (b t) d"),
                                                    bass.IndirectOffsetOnAxis(ap=place_now[:, b, q:q + 1], axis=0)).then_inc(gathered[b % 2], 16)
                    mn, rn = (i + 7 + lead) // G, (i + 7 + lead) % G
                    if U == 2 and r == 0 and ug_valid(m, turn) and m % 2 == 0:
                        for c in range(KC):
                            wait(pool, xT_hi_done, gr(2, m, turn, c - 1))
                            pool.tensor_tensor(nT_lo[:, c, :], nT[:, c, :], nT_hi[:, c, :], ALU.subtract).then_inc(xT_lo_done, 1)
                    part3(m, r, 0, turn)
                    if ub_valid(i + 2, turn):
                        e, z = i + 2, i % 2
                        wait(pool, max_done, ub(4, e + 1, turn))
                        wait_apart(pool, mT_ready, ub(1, e - 1, turn), pool_passed)
                        pool.tensor_copy(mparts[:, z, 0, :], nmax[:, z, :]).then_inc(mpart_done, 1)
                        wait(pool, mpart_done, ub(4, e, turn, 1))
                        pool.tensor_tensor(mres[:, z, :], nmax[:, z, :], mparts[:, z, 0, :], ALU.subtract).then_inc(mpart_done, 1)
                        wait_apart(pool, mpart_done, ub(4, e, turn, 2), pool_passed)
                        pool.tensor_copy(mparts[:, z, 1, :], mres[:, z, :]).then_inc(mpart_done, 1)
                        wait(pool, mpart_done, ub(4, e, turn, 3))
                        pool.tensor_tensor(mparts[:, z, 2, :], mres[:, z, :], mparts[:, z, 1, :], ALU.subtract).then_inc(mpart_done, 1)
                    part3(m, r, 1, turn)
                    if U == 2 and mn % U == 0 and ug_valid(mn, turn):
                        wait_apart(pool, n_ready, gr(G, mn, turn), pool_passed)
                        pool.tensor_scalar(x_in[:, 0, rn, :], x_in[:, 0, rn, :], moments[:, rn, 0:1], rstd[:, 0, rn:rn + 1], ALU.subtract, ALU.mult).then_inc(z_ready, 1)
                    if U == 1 and ub_valid(i - 2, turn):
                        d = i - 2
                        wait(pool, y_bias_done, ub(1, d + 1, turn))
                        wait(pool, xr_loaded[d % G], gr(16, d // G, turn))
                        wait(pool, y_stored[d % 2], at(d, 16 * BODY // 2, turn, 16 * (d // 2)))
                        pool.tensor_tensor(y_out[:, d % 2, :], y_bias[:, :], x_res[:, d % G, :], ALU.add).then_inc(y_done, 1)
                    if rn == 2 and ug_valid(mn + 1, turn) and (mn + 1) % U == 0:
                        rstd_newton(mn + 1, turn)

                steps(pool, N, first_step, loop_first, program)
        clear_semaphores(nc, sems)


E = 8
F = 512
FC = F // P
MATRIX = KC * F
BELOW_ALL = -3.0e38


def newton_steps(eng, done, counted, rstd, square, minus_half_var):
    n = 0
    for _ in range(NEWTON):
        for out, a, b, op in ((square, rstd, rstd, ALU.mult), (square, square, minus_half_var, ALU.mult)):
            eng.tensor_tensor(out[:, :], a[:, :], b[:, :], op).then_inc(done, 1)
            n += 1
            counted(n)
        eng.scalar_tensor_tensor(rstd[:, :], square[:, :], 1.5, rstd[:, :], ALU.add, ALU.mult).then_inc(done, 1)
        n += 1
        counted(n)


def route_phase(nc, name, src, n_dst, by_token, w_router, b_router, gamma, beta, logits, ident, ones, B, preload=None):
    NG = B // G
    with ExitStack() as es:
        def sb(n, shape, dt):
            return es.enter_context(nc.sbuf_tensor(f"{name}_{n}", shape, dt))

        def ps(n, shape, dt):
            return es.enter_context(nc.psum_tensor(f"{name}_{n}", shape, dt))

        sems = []

        def sem(n):
            sems.append(nc.alloc_semaphore(name=f"{name}_{n}"))
            return sems[-1]

        x_in = sb("x_in", [P, 2, G, D], F32)
        n_tok = sb("n_tok", [P, 2, G, D], F32)
        stats = sb("stats", [P, G, 6], F32)
        moments = sb("moments", [P, G, 2], F32)
        var_eps = sb("var_eps", [P, G], F32)
        half_bits = sb("half_bits", [P, G], I32)
        square = sb("square", [P, G], F32)
        rstd = sb("rstd", [P, G], F32)
        rw = sb("rw", [P, KC, E], F32)
        rb = sb("rb", [P, G, E], F32)
        cols = sb("cols", [P, KC, T if by_token else G], F32)
        PT = [ps(f"PT{c}", [P, T], F32) for c in range(KC)]
        PL = [ps(f"PL{k}", [P, T], F32) for k in range(2)]
        if not by_token:
            gam = sb("gam", [P, D], F32)
            bet = sb("bet", [P, D], F32)

        w_loaded = sem("w_loaded")
        x_loaded = [sem(f"x_loaded{k}") for k in range(2)]
        n_stored = [sem(f"n_stored{k}") for k in range(2)]
        ln_stats, ln_moments, ln_guess, newton_done = sem("ln_stats"), sem("ln_moments"), sem("ln_guess"), sem("newton_done")
        n_plain, n_scaled, n_ready = sem("n_plain"), sem("n_scaled"), sem("n_ready")
        pt_ready, cols_done, pl_ready, logits_done = sem("pt_ready"), sem("cols_done"), sem("pl_ready"), sem("logits_done")
        sp_passed, dve_passed = sem("sp_passed"), sem("dve_passed")
        pre_loaded = [sem(f"pre_loaded{k}") for k in range(2)]
        pre_hi_done, pre_lo_done = sem("pre_hi_done"), sem("pre_lo_done")
        W_IN = 16 if by_token else 64
        routed = logits is not None

        def cnt(per, turn, k, c=0):
            return per * (2 * turn + k + 1) + c

        with nc.Block() as block:

            @block.sync
            def _(sp):
                if routed:
                    sp.dma_start(rw[:, :, :], w_router.rearrange("(c p) e -> p c e", p=P)).then_inc(w_loaded, 16)
                if not by_token:
                    sp.dma_start(rb[:, :, :], b_router.rearrange("(a b e) -> a b e", a=1, b=1).to_broadcast([P, G, E])).then_inc(w_loaded, 16)
                    sp.dma_start(gam[:, :], gamma.rearrange("(a n) -> a n", a=1).to_broadcast([P, D])).then_inc(w_loaded, 16)
                    sp.dma_start(bet[:, :], beta.rearrange("(a n) -> a n", a=1).to_broadcast([P, D])).then_inc(w_loaded, 16)
                for k in range(2):
                    sp.dma_start(x_in[:, k, :, :], src[k * G:k * G + G].rearrange("b t d -> t b d")).then_inc(x_loaded[k], 16)
                with sp.Fori(0, NG // 2 - 1) as turn:
                    for k in range(2):
                        wait_apart(sp, n_ready, cnt(1, turn, k), sp_passed)
                        sp.dma_start(n_dst[bass.ds((2 * turn + k) * G, G)].rearrange("b t d -> t b d"), n_tok[:, k, :, :]).then_inc(n_stored[k], 16)
                        sp.dma_start(x_in[:, k, :, :], src[bass.ds((2 * turn + k + 2) * G, G)].rearrange("b t d -> t b d")).then_inc(x_loaded[k], 16)
                for k in range(2):
                    sp.wait_ge(n_ready, NG - 1 + k)
                    sp.dma_start(n_dst[(NG - 2 + k) * G:(NG - 1 + k) * G].rearrange("b t d -> t b d"), n_tok[:, k, :, :]).then_inc(n_stored[k], 16)
                for k in range(2):
                    sp.wait_ge(n_stored[k], 16 * NG // 2)

            if preload is not None:
                @block.gpsimd
                def _(pool):
                    n = len(preload["sources"])
                    for q in range(2):
                        load_matrix(pool, preload, q, pre_loaded, pre_lo_done)
                    for q in range(n):
                        pool.wait_ge(pre_loaded[q % 2], 16 * (q // 2 + 1))
                        pool.tensor_copy(half_of(preload["hi"], q), preload["w32"][:, q % 2, :]).then_inc(pre_hi_done, 1)
                        pool.wait_ge(pre_hi_done, q + 1)
                        pool.tensor_tensor(half_of(preload["lo"], q), preload["w32"][:, q % 2, :], half_of(preload["hi"], q), ALU.subtract).then_inc(pre_lo_done, 1)
                        if q + 2 < n:
                            load_matrix(pool, preload, q + 2, pre_loaded, pre_lo_done)

            @block.vector
            def _(dve):
                if routed:
                    dve.wait_ge(w_loaded, W_IN)

                def group(turn, k, first):
                    dve.wait_ge(x_loaded[k], 16 * (turn + 1))
                    for b in range(G):
                        dve.bn_stats(stats[:, b, :], x_in[:, k, b, :]).then_inc(ln_stats, 1)
                    for b in range(G):
                        wait_apart(dve, ln_stats, cnt(G, turn, k, b + 1 - G), dve_passed)
                        dve.bn_aggr(moments[:, b, :], stats[:, b, :]).then_inc(ln_moments, 1)
                    dve.wait_ge(ln_moments, cnt(G, turn, k))
                    var = moments[:, :, 1:2].rearrange("p b o -> p (b o)")
                    eps = 1e-5 if by_token else 1e-6
                    dve.tensor_scalar(var_eps[:, :], var, eps, None, ALU.add).then_inc(ln_guess, 1)
                    dve.wait_ge(ln_guess, cnt(4, turn, k, -3))
                    dve.tensor_scalar(half_bits[:, :], var_eps[:, :].bitcast(I32), 1, None, ALU.logical_shift_right).then_inc(ln_guess, 1)
                    dve.wait_ge(ln_guess, cnt(4, turn, k, -2))
                    dve.tensor_scalar(rstd[:, :].bitcast(I32), half_bits[:, :], -1, GUESS, ALU.mult, ALU.add).then_inc(ln_guess, 1)
                    dve.tensor_scalar(var_eps[:, :], var, eps, -0.5, ALU.add, ALU.mult).then_inc(ln_guess, 1)
                    dve.wait_ge(ln_guess, cnt(4, turn, k))
                    if not first:
                        dve.wait_ge(n_stored[k], 16 * turn)
                        if routed:
                            dve.wait_ge(cols_done, cnt(KC if by_token else 1, turn, k, -2 * (KC if by_token else 1)))
                    per = 3 * NEWTON

                    def stepped(n):
                        b = n // 2
                        if not by_token and n % 2 == 1 and b < G:
                            dve.scalar_tensor_tensor(n_tok[:, k, b, :], x_in[:, k, b, :], moments[:, b, 0:1], gam[:, :], ALU.subtract, ALU.mult).then_inc(n_plain, 1)
                        dve.wait_ge(newton_done, cnt(per, turn, k, n - per))

                    newton_steps(dve, newton_done, stepped, rstd, square, var_eps)
                    for b in range(G):
                        if by_token:
                            dve.tensor_scalar(n_tok[:, k, b, :], x_in[:, k, b, :], moments[:, b, 0:1], rstd[:, b:b + 1], ALU.subtract, ALU.mult).then_inc(n_plain, 1)
                        else:
                            if b == 0:
                                dve.wait_ge(n_plain, cnt(G, turn, k))
                            dve.scalar_tensor_tensor(n_tok[:, k, b, :], n_tok[:, k, b, :], rstd[:, b:b + 1], bet[:, :], ALU.mult, ALU.add).then_inc(n_scaled, 1)
                    dve.wait_ge(n_plain if by_token else n_scaled, cnt(G, turn, k))
                    dve.sem_inc(n_ready, 1)

                def logits_out(turn, k):
                    if not routed:
                        return
                    dve.wait_ge(pl_ready, cnt(1, turn, k))
                    out = logits[:, bass.ds((2 * turn + k) * G, G), :]
                    pl = PL[k][:, 0:G * E].rearrange("p (b e) -> p b e", b=G)
                    if by_token:
                        dve.tensor_copy(out, pl).then_inc(logits_done, 1)
                    else:
                        dve.tensor_tensor(out, pl, rb[:, :, :], ALU.add).then_inc(logits_done, 1)

                group(0, 0, True)
                group(0, 1, True)
                logits_out(0, 0)
                with dve.Fori(1, NG // 2) as turn:
                    group(turn, 0, False)
                    logits_out(turn - 1, 1)
                    group(turn, 1, False)
                    logits_out(turn, 0)
                logits_out(NG // 2 - 1, 1)

            if routed:
                @block.tensor
                def _(pe):
                    pe.wait_ge(w_loaded, W_IN)

                    def group(turn, k, first):
                        pe.wait_ge(n_ready, cnt(1, turn, k))
                        if by_token:
                            for c in range(KC):
                                if not (first and k == 0):
                                    pe.wait_ge(cols_done, cnt(KC, turn, k, c + 1 - 2 * KC))
                                for b in range(G):
                                    last = pe.transpose(PT[c][:, b * P:(b + 1) * P], n_tok[:, k, b, c * P:(c + 1) * P], ident[:, :])
                                last.then_inc(pt_ready, 1)
                            pe.wait_ge(cols_done, cnt(KC, turn, k))
                        else:
                            if not (first and k == 0):
                                pe.wait_ge(cols_done, cnt(1, turn, k, -1))
                            for c in range(KC):
                                for b in range(G):
                                    last = pe.matmul(PT[0][:, c * G + b:c * G + b + 1], n_tok[:, k, b, c * P:(c + 1) * P], ones[:, 0:1], start=True, stop=True)
                            last.then_inc(pt_ready, 1)
                            pe.wait_ge(cols_done, cnt(1, turn, k))
                        if not first:
                            pe.wait_ge(logits_done, cnt(1, turn, k, -2))
                        for b in range(G):
                            for c in range(KC):
                                a = cols[:, c, b * P:(b + 1) * P] if by_token else cols[:, c, b:b + 1].to_broadcast([P, P])
                                last = pe.matmul(PL[k][:, b * E:(b + 1) * E], a, rw[:, c, :], start=(c == 0), stop=(c == KC - 1))
                        last.then_inc(pl_ready, 1)

                    for k in range(2):
                        group(0, k, True)
                    with pe.Fori(1, NG // 2) as turn:
                        for k in range(2):
                            group(turn, k, False)

                @block.scalar
                def _(act):
                    def group(turn, k, first):
                        if not (first and k == 0):
                            act.wait_ge(pl_ready, cnt(1, turn, k, -1))
                        if by_token:
                            for c in range(KC):
                                act.wait_ge(pt_ready, cnt(KC, turn, k, c + 1 - KC))
                                act.activation(cols[:, c, :], PT[c][:, :], ACT.Copy).then_inc(cols_done, 1)
                        else:
                            act.wait_ge(pt_ready, cnt(1, turn, k))
                            act.activation(cols[:, :, :].rearrange("p c b -> p (c b)"), PT[0][:, 0:KC * G], ACT.Copy, scale=1.0 / P).then_inc(cols_done, 1)

                    for k in range(2):
                        group(0, k, True)
                    with act.Fori(1, NG // 2) as turn:
                        for k in range(2):
                            group(turn, k, False)
        clear_semaphores(nc, sems)


def top_two(nc, es, sem, name, logits, weights, experts, tokens_sorted, B):
    def sb(n, shape, dt):
        return es.enter_context(nc.sbuf_tensor(f"{name}_{n}", shape, dt))

    rev = sb("rev", [P, B, E], F32)
    eq = sb("eq", [P, B, E], F32)
    best = sb("best", [P, TOP, B], F32)
    pick = sb("pick", [P, TOP, B], F32)
    onehot = [sb(f"onehot{k}", [P, B, E], F32) for k in range(TOP)]
    rest = sb("rest", [P, B, E], F32)
    ratio = sb("ratio", [P, B], F32)
    step, gone, exp_done, rev_done = sem("step"), sem("gone"), sem("exp_done"), sem("rev_done")
    banks = []
    if tokens_sorted:
        n_dram, place, slot_token, tile_expert = (tokens_sorted[k] for k in ("slots", "place", "slot_token", "tile_expert"))
        NT = tokens_sorted["tiles"]
        ones_tri = sb("ones_tri", [P, P], F32)
        both = sb("both", [P, B, E], F32)
        carry = sb("carry", [P, E, B + 1], F32)
        zero = sb("zero", [P, B + 1], F32)
        padded = sb("padded", [P, E], F32)
        padded_i = sb("padded_i", [P, E], I32)
        base = sb("base", [P, E + 1], F32)
        posf = sb("posf", [P, B, E], F32)
        token = sb("token", [P, B], I32)
        slot = sb("slot", [P, TOP, B], U32)
        slot_now = sb("slot_now", [P, TOP, 4], U32)
        token_now = sb("token_now", [P, 4], I32)
        taken, scatter_passed = sem("taken"), sem("scatter_passed")
        row = sb("row", [P, B], I32)
        rowf = sb("rowf", [P, B], F32)
        zeros_i = sb("zeros_i", [P, NT], I32)
        tile_row = sb("tile_row", [1, NT], F32)
        tile_sum = sb("tile_sum", [1, NT], F32)
        tile_ge = sb("tile_ge", [1, NT], F32)
        banks = [es.enter_context(nc.psum_tensor(f"{name}_{n}", [P, T], F32)) for n in ("ranks", "totals")]
        PR, PC = (bank[:, 0:B * E] for bank in banks)
        tri_done, ranks_ready, ranks_read, cleared, scattered, listed = (
            sem("tri_done"), sem("ranks_ready"), sem("ranks_read"), sem("cleared"), sem("scattered"), sem("listed"))

    def wide(v):
        return v.rearrange("p (b o) -> p b o", o=1).to_broadcast([P, B, E])

    def vector(dve):
        n = 0

        def then(instruction):
            nonlocal n
            n += 1
            instruction.then_inc(step, 1)
            dve.wait_ge(step, n)

        dve.wait_ge(rev_done, 1)
        scores = logits
        for k in range(TOP):
            then(dve.tensor_reduce(best[:, k, :], scores[:, :, :], AX.X, ALU.max))
            then(dve.tensor_tensor(eq[:, :, :], scores[:, :, :], wide(best[:, k, :]), ALU.is_equal))
            then(dve.tensor_tensor(eq[:, :, :], eq[:, :, :], rev[:, :, :], ALU.mult))
            then(dve.tensor_reduce(pick[:, k, :], eq[:, :, :], AX.X, ALU.max))
            then(dve.tensor_tensor(onehot[k][:, :, :], eq[:, :, :], wide(pick[:, k, :]), ALU.is_equal))
            if k == 0:
                then(dve.scalar_tensor_tensor(rest[:, :, :].rearrange("p b e -> p (b e)"), onehot[0][:, :, :].rearrange("p b e -> p (b e)"), BELOW_ALL,
                                              logits[:, :, :].rearrange("p b e -> p (b e)"), ALU.mult, ALU.add))
                scores = rest
        dve.tensor_tensor(ratio[:, :], best[:, 1, :], best[:, 0, :], ALU.subtract).then_inc(gone, 1)
        dve.wait_ge(exp_done, 1)
        then(dve.tensor_scalar(best[:, 0, :], ratio[:, :], 1.0, None, ALU.add))
        then(dve.reciprocal(best[:, 1, :], best[:, 0, :]))
        then(dve.tensor_copy(weights[:, :, 0:1].rearrange("p b o -> p (b o)"), best[:, 1, :]))
        then(dve.tensor_tensor(weights[:, :, 1:2].rearrange("p b o -> p (b o)"), best[:, 1, :], ratio[:, :], ALU.mult))
        if not tokens_sorted:
            for k in range(TOP):
                then(dve.tensor_scalar(experts[0:1, :].rearrange("p (b k) -> p b k", k=TOP)[:, :, k], pick[0:1, k, :],
                                       -float(MATRIX), float(E * MATRIX), ALU.mult, ALU.add))
            return
        then(dve.tensor_tensor(both[:, :, :], onehot[0][:, :, :], onehot[1][:, :, :], ALU.add))
        dve.sem_inc(gone, 1)
        then(dve.memset(zero[:, :], 0.0))
        then(dve.memset(carry[:, :, 0:1], 0.0))
        then(dve.memset(base[:, 0:1], 0.0))
        dve.wait_ge(ranks_ready, 2)
        for e in range(E):
            then(dve.tensor_tensor_scan(carry[:, e, 1:B + 1], PC.rearrange("p (b e) -> p e b", e=E)[:, e, :], zero[:, 1:B + 1], 0.0, ALU.add, ALU.add))
        then(dve.tensor_scalar(padded_i[:, :], carry[:, :, B:B + 1].rearrange("p e o -> p (e o)"), float(P - 1), None, ALU.add))
        then(dve.tensor_scalar(padded_i[:, :], padded_i[:, :], 7, 7, ALU.logical_shift_right, ALU.logical_shift_left))
        then(dve.tensor_copy(padded[:, :], padded_i[:, :]))
        for e in range(E):
            then(dve.tensor_tensor(base[:, e + 1:e + 2], base[:, e:e + 1], padded[:, e:e + 1], ALU.add))
        then(dve.tensor_tensor(posf[:, :, :], PR.rearrange("p (b e) -> p b e", e=E), carry[:, :, 0:B].rearrange("p e b -> p b e"), ALU.add))
        dve.sem_inc(ranks_read, 1)
        then(dve.tensor_tensor(posf[:, :, :], posf[:, :, :], base[:, 0:E].rearrange("p (o e) -> p o e", o=1).to_broadcast([P, B, E]), ALU.add))
        for k in range(TOP):
            then(dve.tensor_tensor(onehot[k][:, :, :], onehot[k][:, :, :], posf[:, :, :], ALU.mult))
            then(dve.tensor_reduce(pick[:, k, :], onehot[k][:, :, :], AX.X, ALU.add))
            then(dve.tensor_copy(place[:, k, :], pick[:, k, :]))
            then(dve.tensor_scalar(row[:, :], place[:, k, :].bitcast(I32), P - 1, None, ALU.bitwise_and))
            then(dve.tensor_copy(rowf[:, :], row[:, :]))
            then(dve.tensor_tensor(pick[:, k, :], pick[:, k, :], rowf[:, :], ALU.subtract))
            then(dve.tensor_scalar(pick[:, k, :], pick[:, k, :], 1.0 / P, None, ALU.mult))
            then(dve.scalar_tensor_tensor(pick[:, k, :], rowf[:, :], float(NT), pick[:, k, :], ALU.mult, ALU.add))
            then(dve.tensor_copy(slot[:, k, :], pick[:, k, :]))
        dve.sem_inc(gone, 1)
        dve.wait_ge(rev_done, 2)
        then(dve.memset(tile_sum[:, :], 0.0))
        for e in range(1, E + 1):
            then(dve.tensor_scalar(tile_ge[:, :], tile_row[:, :], base[0:1, e:e + 1], None, ALU.is_ge))
            then(dve.tensor_tensor(tile_sum[:, :], tile_sum[:, :], tile_ge[:, :], ALU.add))
        then(dve.tensor_scalar(tile_sum[:, :], tile_sum[:, :], float(E - 1), float(MATRIX), ALU.min, ALU.mult))
        then(dve.tensor_copy(tile_expert[0:1, :], tile_sum[:, :]))

    def scalar(act):
        act.wait_ge(gone, 1)
        act.activation(ratio[:, :], ratio[:, :], ACT.Exp).then_inc(exp_done, 1)

    def gpsimd(pool):
        pool.iota(rev[:, :, :], [[0, B], [-1, E]], base=E, channel_multiplier=0, allow_small_or_imprecise_dtypes=True).then_inc(rev_done, 1)
        if not tokens_sorted:
            return
        pool.wait_ge(rev_done, 1)
        pool.iota(tile_row[:, :], [[P, NT]], base=0, channel_multiplier=0, allow_small_or_imprecise_dtypes=True).then_inc(rev_done, 1)
        pool.wait_ge(rev_done, 2)
        pool.memset(ones_tri[:, :], 1.0).then_inc(tri_done, 1)
        pool.wait_ge(tri_done, 1)
        pool.affine_select(out=ones_tri[:, :], in_=ones_tri[:, :], compare_op=ALU.is_gt, fill=0.0, base=0, pattern=[[1, P]], channel_multiplier=-1).then_inc(tri_done, 1)
        pool.iota(token[:, :], [[P, B]], base=0, channel_multiplier=1).then_inc(tri_done, 1)
        pool.memset(zeros_i[:, :], 0).then_inc(tri_done, 1)
        pool.wait_ge(tri_done, 4)
        pool.dma_start(n_dram[:, :], zeros_i[:, :]).then_inc(cleared, 16)
        pool.wait_ge(cleared, 16)
        pool.wait_ge(gone, 3)
        flat = n_dram.rearrange("p (b o) -> (p b) o", o=1)
        def scatter(turn, first):
            if not first:
                wait_apart(pool, scattered, 16 * 4 * TOP * turn, scatter_passed)
            for k in range(TOP):
                pool.tensor_copy(slot_now[:, k, :], slot[:, k, bass.ds(4 * turn, 4)]).then_inc(taken, 1)
            pool.tensor_copy(token_now[:, :], token[:, bass.ds(4 * turn, 4)]).then_inc(taken, 1)
            wait_apart(pool, taken, 3 * turn + 3, scatter_passed)
            for k in range(TOP):
                for b in range(4):
                    pool.indirect_dma_start(flat, bass.IndirectOffsetOnAxis(ap=slot_now[:, k, b:b + 1], axis=0), token_now[:, b:b + 1], None).then_inc(scattered, 16)

        scatter(0, True)
        with pool.Fori(1, B // 4) as turn:
            scatter(turn, False)
        pool.wait_ge(scattered, 16 * B * TOP)
        pool.dma_start(slot_token[:, :], n_dram[:, :]).then_inc(listed, 16)
        pool.wait_ge(listed, 16)

    def tensor(pe):
        if tokens_sorted:
            pe.wait_ge(tri_done, 2)
            pe.wait_ge(gone, 2)
            v = both[:, :, :].rearrange("p b e -> p (b e)")
            pe.matmul(PR, ones_tri[:, :], v, start=True, stop=True).then_inc(ranks_ready, 1)
            pe.matmul(PC, tokens_sorted["ones"][:, :], v, start=True, stop=True).then_inc(ranks_ready, 1)
            pe.wait_ge(ranks_read, 1)

    return dict(vector=vector, scalar=scalar, gpsimd=gpsimd, tensor=tensor, banks=banks)


def top_two_phase(nc, name, logits, weights, experts, B):
    with ExitStack() as es:
        sems = []

        def sem(n):
            sems.append(nc.alloc_semaphore(name=f"{name}_{n}"))
            return sems[-1]

        programs = top_two(nc, es, sem, name, logits, weights, experts, None, B)
        with nc.Block() as block:

            @block.vector
            def _(dve):
                programs["vector"](dve)

            @block.scalar
            def _(act):
                programs["scalar"](act)

            @block.gpsimd
            def _(pool):
                programs["gpsimd"](pool)

        clear_semaphores(nc, sems)


def expert_weights(nc, es, name, sources):
    NE = len(sources)

    def sb(n, shape, dt):
        return es.enter_context(nc.sbuf_tensor(f"{name}_{n}", shape, dt))

    return dict(sources=[w for pair in sources for w in pair], w32=sb("w32", [P, 2, KC * F], F32),
                hi=(sb("wu_hi", [P, NE, KC, F], F32R), sb("wd_hi", [P, NE, FC, D], F32R)),
                lo=(sb("wu_lo", [P, NE, KC, F], F32R), sb("wd_lo", [P, NE, FC, D], F32R)))


def half_of(halves, q):
    return halves[q % 2][:, q // 2, :, :].rearrange("p c n -> p (c n)")


def load_matrix(eng, W, q, loaded, split):
    if q >= 2:
        eng.wait_ge(split, q - 1)
    c = KC if q % 2 == 0 else FC
    eng.dma_start(W["w32"][:, q % 2, :].rearrange("p (c n) -> p c n", c=c), W["sources"][q].rearrange("(c p) n -> p c n", p=P)).then_inc(loaded[q % 2], 16)


def experts_phase(nc, name, rows, gather, tile_expert, weights, y_dst, n_tiles, ident, residual=None, base=None, before=None):
    NE = len(weights["sources"]) // 2
    with ExitStack() as es:
        def sb(n, shape, dt):
            return es.enter_context(nc.sbuf_tensor(f"{name}_{n}", shape, dt))

        def ps(n, shape, dt):
            return es.enter_context(nc.psum_tensor(f"{name}_{n}", shape, dt))

        sems = []

        def sem(n):
            sems.append(nc.alloc_semaphore(name=f"{name}_{n}"))
            return sems[-1]

        (wu_hi, wd_hi), (wu_lo, wd_lo) = weights["hi"], weights["lo"]
        x_in = sb("x_in", [P, 4, D], F32)
        xT_hi = sb("xT_hi", [P, 2, KC, P], F32R)
        xT_lo = sb("xT_lo", [P, 2, KC, P], F32R)
        hid = sb("hid", [P, 2, F], F32)
        hT_hi = sb("hT_hi", [P, 2, FC, P], F32R)
        hT_lo = sb("hT_lo", [P, 2, FC, P], F32R)
        y_out = sb("y_out", [P, 4, D], F32)
        gather_now = sb("gather_now", [P, 4], U32)
        each = TOP if residual is not None else 1
        base_in = sb("base_in", [P, 4, D], F32) if base is not None else None
        base_loaded = [sem(f"base_loaded{k}") for k in range(4)]
        if residual is not None:
            res = [sb(f"res{k}", [P, 2, D], F32) for k in range(2)]
            y_first = sb("y_first", [P, 2, D], F32)
            res_loaded = [sem(f"res_loaded{k}") for k in range(2)]
            res_added, pool_passed = sem("res_added"), sem("pool_passed")
        taken = sem("taken")
        PX = before["banks"] if before else [ps(f"PX{k}", [P, T], F32) for k in range(2)]
        PH = [ps(f"PH{k}", [P, F], F32) for k in range(2)]
        PT = [ps(f"PT{k}", [P, F], F32) for k in range(2)]
        PY = [ps(f"PY{k}", [P, T], F32) for k in range(2)]
        x_loaded = [sem(f"x_loaded{k}") for k in range(4)]
        xT_ready, xT_hi_done, xT_lo_done = sem("xT_ready"), sem("xT_hi_done"), sem("xT_lo_done")
        h_ready, gelu_done, hT_ready, hT_hi_done, hT_lo_done = (
            sem("h_ready"), sem("gelu_done"), sem("hT_ready"), sem("hT_hi_done"), sem("hT_lo_done"))
        y_ready, y_copied = sem("y_ready"), sem("y_copied")
        y_stored = [sem(f"y_stored{k}") for k in range(4)]
        passed, pe_passed = sem("passed"), sem("pe_passed")
        STEP0, LOOP0, PER = -3, 6, 4
        turns = (n_tiles - 4 - LOOP0) // PER
        LOOP1 = LOOP0 + PER * turns

        def run(eng, program):
            for i in range(STEP0, LOOP0):
                program(i, None)
            with eng.Fori(0, turns) as turn:
                for i in range(LOOP0, LOOP0 + PER):
                    program(i, turn)
            for i in range(LOOP1, n_tiles + 4):
                program(i, None)

        def done(i, turn, per=1, c=0):
            return at(i, per * PER, turn, per * (i + 1) + c)

        def ring4(i, turn):
            return at(i, 16, turn, 16 * (i // 4 + 1))

        def valid(i, turn):
            return turn is not None or 0 <= i < n_tiles

        def off(turn):
            return 0 if turn is None else PER * turn

        with nc.Block() as block:

            @block.sync
            def _(sp):
                def program(i, turn):
                    if gather is None and valid(i + 3, turn):
                        wait_apart(sp, xT_ready, done(i - 1, turn), passed)
                        b = (i + 3) // each
                        sp.dma_start(x_in[:, (i + 3) % 4, :], rows[bass.ds(b + (0 if turn is None else PER // each * turn), 1)].rearrange("b t d -> t (b d)")
                                     ).then_inc(x_loaded[(i + 3) % 4], 16)
                    if residual is not None:
                        if i % TOP == 1 and valid(i + 1, turn):
                            b = (i + 1) // TOP
                            wait_apart(sp, y_copied, done(i - 3, turn), passed)
                            for k in range(2):
                                sp.dma_start(res[k][:, b % 2, :], residual[k][bass.ds(b + (0 if turn is None else PER // TOP * turn), 1)].rearrange("b t d -> t (b d)")
                                             ).then_inc(res_loaded[b % 2], 16)
                        if (i - 3) % TOP == 1 and valid(i - 3, turn):
                            b = (i - 3) // TOP
                            wait_apart(sp, y_copied, done(i - 3, turn), passed)
                            sp.dma_start(y_dst[bass.ds(b + (0 if turn is None else PER // TOP * turn), 1)].rearrange("b t d -> t (b d)"), y_out[:, b % 2, :]
                                         ).then_inc(y_stored[b % 2], 16)
                    elif valid(i - 3, turn):
                        wait_apart(sp, y_copied, done(i - 3, turn), passed)
                        sp.dma_start(y_dst[bass.ds(i - 3 + off(turn), 1)].rearrange("b t d -> t (b d)"), y_out[:, (i - 3) % 4, :]).then_inc(y_stored[(i - 3) % 4], 16)

                    if base is not None and valid(i + 1, turn):
                        wait_apart(sp, y_copied, done(i - 3, turn), passed)
                        sp.dma_start(base_in[:, (i + 1) % 4, :], base[bass.ds(i + 1 + off(turn), 1)].rearrange("b t d -> t (b d)")).then_inc(base_loaded[(i + 1) % 4], 16)

                run(sp, program)
                for k in range(2 if residual is not None else 4):
                    sp.wait_ge(y_stored[k], 16 * (n_tiles // 4))

            if before is not None:
                @block.gpsimd
                def _(pool):
                    before["gpsimd"](pool)

            if residual is not None:
                @block.gpsimd
                def _(pool):
                    def program(i, turn):
                        if i % TOP == 0 and valid(i, turn):
                            b = i // TOP
                            wait(pool, res_loaded[b % 2], at(i, 32, turn, 32 * (b // 2 + 1)))
                            pool.tensor_tensor(res[0][:, b % 2, :], res[0][:, b % 2, :], res[1][:, b % 2, :], ALU.add).then_inc(res_added, 1)

                    run(pool, program)

            if gather is not None:
                @block.gpsimd
                def _(pool):
                    def program(i, turn):
                        if valid(i + 3, turn):
                            wait_apart(pool, xT_ready, done(i - 1, turn), passed)
                            k = (i + 3) % 4
                            pool.tensor_copy(gather_now[:, k:k + 1], gather[:, bass.ds(i + 3 + off(turn), 1)]).then_inc(taken, 1)
                            wait_apart(pool, taken, done(i + 3, turn), passed)
                            pool.indirect_dma_start(x_in[:, k, :], None, rows.rearrange("b t d -> (b t) d"),
                                                    bass.IndirectOffsetOnAxis(ap=gather_now[:, k:k + 1], axis=0)).then_inc(x_loaded[k], 16)

                    run(pool, program)

            @block.tensor
            def _(pe):
                if before is not None:
                    before["tensor"](pe)
                numbers = [pe.alloc_register(f"{name}_expert{k}") for k in range(4)]

                def load_expert(i, turn):
                    if tile_expert is None:
                        return
                    pe.reg_load(numbers[i % 4], tile_expert[0:1, bass.ds(i + off(turn), 1)])

                def first_column(i):
                    if tile_expert is None:
                        return (NE - 1) * MATRIX
                    return pe.snap(numbers[i % 4], min_val=0, max_val=(NE - 1) * MATRIX)

                def matrix(w, first, c, n):
                    return w[:, :, :, :].rearrange("p e c n -> p (e c n)")[:, bass.ds(first + c * n, n)]

                def program(i, turn):
                    if valid(i, turn):
                        wait(pe, xT_lo_done, done(i, turn))
                        wait(pe, gelu_done, done(i - 2, turn))
                        first = first_column(i)
                        for c in range(KC):
                            for z, (a, w) in enumerate(((xT_hi, wu_hi), (xT_hi, wu_lo), (xT_lo, wu_hi))):
                                last = pe.matmul(PH[i % 2][:, :], a[:, i % 2, c, :], matrix(w, first, c, F),
                                                 start=(c == 0 and z == 0), stop=(c == KC - 1 and z == 2))
                        last.then_inc(h_ready, 1)
                    if valid(i + 1, turn):
                        k = (i + 1) % 2
                        wait(pe, x_loaded[(i + 1) % 4], ring4(i + 1, turn))
                        wait_apart(pe, xT_lo_done, done(i - 1, turn), pe_passed)
                        load_expert(i + 1, turn)
                        for c in range(KC):
                            last = pe.transpose(PX[k][:, c * P:(c + 1) * P], x_in[:, (i + 1) % 4, c * P:(c + 1) * P], ident[:, :])
                        last.then_inc(xT_ready, 1)
                    if valid(i - 1, turn):
                        wait(pe, gelu_done, done(i - 1, turn))
                        wait(pe, hT_lo_done, done(i - 3, turn))
                        for c in range(FC):
                            last = pe.transpose(PT[(i - 1) % 2][:, c * P:(c + 1) * P], hid[:, (i - 1) % 2, c * P:(c + 1) * P], ident[:, :])
                        last.then_inc(hT_ready, 1)
                    if valid(i - 2, turn):
                        k = i % 2
                        wait(pe, hT_lo_done, done(i - 2, turn))
                        wait(pe, y_copied, done(i - 4, turn))
                        first = first_column(i - 2)
                        for c in range(FC):
                            for z, (a, w) in enumerate(((hT_hi, wd_hi), (hT_hi, wd_lo), (hT_lo, wd_hi))):
                                last = pe.matmul(PY[k][:, 0:D], a[:, k, c, :], matrix(w, first, c, D),
                                                 start=(c == 0 and z == 0), stop=(c == FC - 1 and z == 2))
                        last.then_inc(y_ready, 1)

                run(pe, program)

            @block.scalar
            def _(act):
                if before is not None:
                    before["scalar"](act)

                def program(i, turn):
                    if valid(i, turn):
                        wait(act, hT_ready, done(i - 2, turn))
                        wait(act, h_ready, done(i, turn))
                        act.activation(hid[:, i % 2, :], PH[i % 2][:, :], ACT.Gelu).then_inc(gelu_done, 1)
                    if valid(i + 1, turn):
                        k = (i + 1) % 2
                        wait(act, xT_ready, done(i + 1, turn))
                        wait(act, h_ready, done(i - 1, turn))
                        act.activation(xT_hi[:, k, :, :].rearrange("p c t -> p (c t)"), PX[k][:, 0:D], ACT.Copy).then_inc(xT_hi_done, 1)
                    if valid(i - 1, turn):
                        k = (i - 1) % 2
                        wait(act, hT_ready, done(i - 1, turn))
                        wait(act, y_ready, done(i - 3, turn))
                        act.activation(hT_hi[:, k, :, :].rearrange("p c t -> p (c t)"), PT[k][:, :], ACT.Copy).then_inc(hT_hi_done, 1)

                run(act, program)

            @block.vector
            def _(dve):
                if before is not None:
                    before["vector"](dve)

                def program(i, turn):
                    if valid(i + 1, turn):
                        k = (i + 1) % 2
                        wait(dve, xT_hi_done, done(i + 1, turn))
                        dve.tensor_tensor(xT_lo[:, k, :, :].rearrange("p c t -> p (c t)"), PX[k][:, 0:D], xT_hi[:, k, :, :].rearrange("p c t -> p (c t)"),
                                          ALU.subtract).then_inc(xT_lo_done, 1)
                    if valid(i - 1, turn):
                        k = (i - 1) % 2
                        wait(dve, hT_hi_done, done(i - 1, turn))
                        dve.tensor_tensor(hT_lo[:, k, :, :].rearrange("p c t -> p (c t)"), PT[k][:, :], hT_hi[:, k, :, :].rearrange("p c t -> p (c t)"),
                                          ALU.subtract).then_inc(hT_lo_done, 1)
                    if valid(i - 2, turn) and residual is not None:
                        b, k = (i - 2) // TOP, i % TOP
                        factor = residual[2][:, bass.ds(b + (0 if turn is None else PER // TOP * turn), 1), k:k + 1].rearrange("p o n -> p (o n)")
                        if k == 0:
                            wait(dve, res_added, at(i, PER // TOP, turn, b + 1))
                        else:
                            wait(dve, y_stored[b % 2], at(i, 16, turn, 16 * (b // 2)))
                            wait(dve, y_copied, done(i - 3, turn))
                        wait_apart(dve, y_ready, done(i - 2, turn), pe_passed)
                        out, addend = (y_first, res[0]) if k == 0 else (y_out, y_first)
                        dve.scalar_tensor_tensor(out[:, b % 2, :], PY[i % 2][:, 0:D], factor, addend[:, b % 2, :], ALU.mult, ALU.add).then_inc(y_copied, 1)
                    elif valid(i - 2, turn):
                        wait(dve, y_ready, done(i - 2, turn))
                        wait(dve, y_stored[(i - 2) % 4], at(i, 16, turn, 16 * ((i - 2) // 4)))
                        if base is not None:
                            wait_apart(dve, base_loaded[(i - 2) % 4], ring4(i - 2, turn), pe_passed)
                            dve.tensor_tensor(y_out[:, (i - 2) % 4, :], PY[i % 2][:, 0:D], base_in[:, (i - 2) % 4, :], ALU.add).then_inc(y_copied, 1)
                        else:
                            dve.tensor_copy(y_out[:, (i - 2) % 4, :], PY[i % 2][:, 0:D]).then_inc(y_copied, 1)

                run(dve, program)
        clear_semaphores(nc, sems)


def program(nc, t, B):
    def scratch(n, shape, dt=F32):
        return nc.dram_tensor(n, shape, dt, kind="Internal").ap()

    x1, x2, x3, x4 = (scratch(f"x{k}_scratch", (B, P, D)) for k in range(1, 5))
    x3_normed = scratch("x3_normed_scratch", (B, P, D))
    normed = scratch("normed_scratch", (B, P, D))
    list_tiles = B * TOP + E
    y_rows = scratch("expert_rows_scratch", (list_tiles, P, D))
    x_shared = scratch("x_shared_scratch", (B, P, D))
    slots = scratch("slots_scratch", (P, list_tiles), U32)

    with ExitStack() as es:
        ident = es.enter_context(nc.sbuf_tensor("ident", [P, P], F32))
        identb = es.enter_context(nc.sbuf_tensor("identb", [P, P], BF16))
        ones = es.enter_context(nc.sbuf_tensor("ones", [P, P], F32))
        const_done = es.enter_context(nc.semaphore("const_done"))
        with nc.Block() as block:
            @block.gpsimd
            def _(pool):
                pool.memset(ident[:, :], 0.0).then_inc(const_done, 1)
                pool.wait_ge(const_done, 1)
                pool.affine_select(out=ident[:, :], in_=ident[:, :], compare_op=ALU.not_equal, fill=1.0, base=0, pattern=[[-1, P]],
                                   channel_multiplier=1).then_inc(const_done, 1)
                pool.wait_ge(const_done, 2)
                pool.tensor_copy(identb[:, :], ident[:, :]).then_inc(const_done, 1)
                pool.memset(ones[:, :], 1.0).then_inc(const_done, 1)

        attention_phase(nc, "xattn0", t["x"], t["ctx"], x1, [t["attn0"]], None, ident, identb, B)
        weights = es.enter_context(nc.sbuf_tensor("weights0", [P, B, TOP], F32))
        place = es.enter_context(nc.sbuf_tensor("place0", [P, TOP, B], U32))
        with ExitStack() as moe:
            logits = moe.enter_context(nc.sbuf_tensor("logits0", [P, B, E], F32))
            slot_token = moe.enter_context(nc.sbuf_tensor("slot_token0", [P, list_tiles], U32))
            tile_expert = moe.enter_context(nc.sbuf_tensor("tile_expert0", [1, list_tiles], I32))
            matrices = expert_weights(nc, moe, "experts0", [(t["Wu"][e], t["Wd"][e]) for e in range(E)] + [(t["W1"], t["W2"])])
            route_phase(nc, "route0", x1, normed, True, t["Wg"], None, None, None, logits, ident, ones, B, matrices)
            with ExitStack() as sorting:
                sems = []

                def sem(n):
                    sems.append(nc.alloc_semaphore(name=f"top0_{n}"))
                    return sems[-1]

                sort = top_two(nc, sorting, sem, "top0", logits, weights, None, dict(
                    slots=slots, place=place, slot_token=slot_token, tile_expert=tile_expert, tiles=list_tiles, ones=ones), B)
                experts_phase(nc, "shared0", normed, None, None, matrices, x_shared, B, ident, base=x1, before=sort)
                clear_semaphores(nc, sems)
            experts_phase(nc, "experts0", normed, slot_token, tile_expert, matrices, y_rows, list_tiles, ident)

        attention_phase(nc, "xattn1", x_shared, t["ctx"], x3, [t["attn1"]], None, ident, identb, B,
                        dict(rows=y_rows, place=place, weights=weights, dst=x2))
        attention_phase(nc, "mha", x3, None, x4, [t["mha0"], t["mha1"]], dict(t["router1"], z=x3_normed), ident, identb, B)
        with ExitStack() as moe:
            logits = moe.enter_context(nc.sbuf_tensor("logits1", [P, B, E], F32))
            weights = moe.enter_context(nc.sbuf_tensor("weights1", [P, B, TOP], F32))
            tile_expert = moe.enter_context(nc.sbuf_tensor("tile_expert1", [1, B * TOP], I32))
            matrices = expert_weights(nc, moe, "experts1", [(t["fw1"][e], t["fw2"][e]) for e in range(E)])
            route_phase(nc, "route1", x4, normed, False, t["ffn_rw"], t["ffn_rb"], t["ln2_g"], t["ln2_b"], logits, ident, ones, B, matrices)
            top_two_phase(nc, "top1", logits, weights, tile_expert, B)
            experts_phase(nc, "experts1", normed, None, tile_expert, matrices, t["out"], B * TOP, ident, (x4, x3, weights))


def kernel(**inputs):
    import numpy as np
    import concourse.bacc as bacc
    from concourse.bass_utils import run_bass_kernel_spmd

    a = {k: np.asarray(v) for k, v in inputs.items()}
    B = a["x"].shape[0]

    def headwise(w):
        return w.reshape(D, P // HD, KC, HD).transpose(0, 2, 3, 1).reshape(D, D)

    def headwise_bias(b):
        return b.reshape(P // HD, KC, HD).transpose(2, 0, 1).reshape(P, KC)

    def column(v):
        return v.reshape(KC, P).T

    def unit(name, wq, wk, wv, wo, bq, bk, bv, bo):
        return {f"{name}_wq": headwise(wq), f"{name}_wk": headwise(wk), f"{name}_wv": wv, f"{name}_wo": wo,
                f"{name}_bq": headwise_bias(bq), f"{name}_bk": headwise_bias(bk), f"{name}_bv": bv, f"{name}_bo": bo}

    w = {"x": a["x"], "ctx": a["ctx_1024"]}
    w.update(unit("attn0", a["L0_xattn_Wq"].T, a["L0_xattn_Wk"].T, a["L0_xattn_Wv"].T, a["L0_xattn_Wo"].T,
                  a["L0_xattn_bq"], a["L0_xattn_bk"], a["L0_xattn_bv"], a["L0_xattn_bo"]))
    proj, bias = a["L1_xattn_in_proj_w"], a["L1_xattn_in_proj_b"]
    w.update(unit("attn1", proj[:D].T, proj[D:2 * D].T, proj[2 * D:].T, a["L1_xattn_out_w"].T,
                  bias[:D], bias[D:2 * D], bias[2 * D:], a["L1_xattn_out_b"]))
    for m in range(2):
        w.update(unit(f"mha{m}", a["L1_ffn_mha_wq"][m].reshape(D, D), a["L1_ffn_mha_wk"][m].reshape(D, D),
                      a["L1_ffn_mha_wv"][m].reshape(D, D), a["L1_ffn_mha_wo"][m].reshape(D, D), a["L1_ffn_mha_bq"][m].reshape(D),
                      a["L1_ffn_mha_bk"][m].reshape(D), a["L1_ffn_mha_bv"][m].reshape(D), a["L1_ffn_mha_bo"][m]))
    for k in ("Wg", "Wu", "Wd", "W1", "W2"):
        w[k] = a["L0_ffn_" + k]
    w["ln1_g"], w["ln1_b"] = column(a["L1_ffn_ln1_g"]), column(a["L1_ffn_ln1_b"])
    for k in ("ln2_g", "ln2_b", "mha_rw", "mha_rb", "ffn_rw", "ffn_rb", "fw1", "fw2"):
        w[k] = a["L1_ffn_" + k]

    nc = bacc.Bacc("TRN2", target_bir_lowering=False, num_devices=1)
    arrays = {f"in_{k}": np.ascontiguousarray(v) for k, v in w.items()}
    t = {k: nc.dram_tensor(f"in_{k}", arrays[f"in_{k}"].shape, mybir.dt.from_np(arrays[f"in_{k}"].dtype), kind="ExternalInput").ap() for k in w}
    for u in ("attn0", "attn1", "mha0", "mha1"):
        t[u] = {k: t[f"{u}_{k}"] for k in ("wq", "wk", "wv", "wo", "bq", "bk", "bv", "bo")}
    t["router1"] = {"gamma": t["ln1_g"], "beta": t["ln1_b"], "rw": t["mha_rw"], "rb": t["mha_rb"]}
    t["out"] = nc.dram_tensor("out", (B, P, D), F32, kind="ExternalOutput").ap()
    program(nc, t, B)
    r = run_bass_kernel_spmd(nc, [arrays], core_ids=[0])
    return r.results[0]["out"]
```
